# Optimizing a Trainium2 kernel written in Bass

```python
import numpy as np
import jax
import jax.numpy as jnp

def _softmax(x, axis=-1):
    return jax.nn.softmax(x, axis=axis)

def _gelu(x):
    return jax.nn.gelu(x, approximate=True)

def _silu(x):
    return jax.nn.silu(x)

def _sigmoid(x):
    return jax.nn.sigmoid(x)

def _layernorm(x, axis=-1, eps=1e-05):
    m = jnp.mean(x, axis=axis, keepdims=True)
    v = jnp.var(x, axis=axis, keepdims=True)
    return (x - m) / jnp.sqrt(v + eps)

def _scatter_add(tgt, idx, src, axis=0):
    return tgt.at[idx].add(src)

def _segment_sum(src, seg, n):
    return jax.ops.segment_sum(src, seg, n)
kernel_name = 'mk_seq_preln_d2_jaxref_r8_ad51bc'

def setup_inputs(seed: int=0):
    np.random.seed(seed)
    _w = jnp.asarray

    def _L0_attn_setup():
        import jax, jax.numpy as jnp
        import numpy as np
        NUM_HEADS = 16
        DIM_HEAD = 64
        SCALE = DIM_HEAD ** (-0.5)
        ROPE_BASE = 10000.0

        def _rope(t):
            n, d = (t.shape[2], t.shape[3])
            inv_freq = 1.0 / ROPE_BASE ** (jnp.arange(0, d, 2, dtype=jnp.float32) / d)
            freqs = jnp.arange(n, dtype=jnp.float32)[:, None] * inv_freq[None, :]
            cos = jnp.concatenate([jnp.cos(freqs), jnp.cos(freqs)], axis=-1)
            sin = jnp.concatenate([jnp.sin(freqs), jnp.sin(freqs)], axis=-1)
            t1, t2 = jnp.split(t, 2, axis=-1)
            rot = jnp.concatenate([-t2, t1], axis=-1)
            return t * cos + rot * sin
        key = jax.random.key(seed)
        k1, k2, k3 = jax.random.split(key, 3)
        B, N, D = (2, 2049, 128)
        x = jax.random.normal(k1, (B, N, D), dtype=jnp.float32)
        ln_gamma = jnp.ones((D,), dtype=jnp.float32)
        ln_beta = jnp.zeros((D,), dtype=jnp.float32)
        w_qkv = jax.random.normal(k2, (D, 3 * NUM_HEADS * DIM_HEAD), dtype=jnp.float32) * 0.02
        w_out = jax.random.normal(k3, (NUM_HEADS * DIM_HEAD, D), dtype=jnp.float32) * 0.02
        return {'x': x, 'ln_gamma': ln_gamma, 'ln_beta': ln_beta, 'w_qkv': w_qkv, 'w_out': w_out}
    _L0_attn_in = _L0_attn_setup()

    def _L0_ffn_setup():
        import jax, jax.numpy as jnp
        import numpy as np
        B, S, D = (4, 256, 128)
        E, F = (8, 512)
        key = jax.random.key(seed)
        ks = jax.random.split(key, 5)
        x = jax.random.normal(ks[0], (B, S, D), dtype=jnp.float32)
        switch_w = jax.random.normal(ks[1], (D, E), dtype=jnp.float32) * D ** (-0.5)
        switch_b = jnp.zeros((E,), dtype=jnp.float32)
        w1 = jax.random.normal(ks[2], (E, D, F), dtype=jnp.float32) * D ** (-0.5)
        b1 = jnp.zeros((E, F), dtype=jnp.float32)
        w2 = jax.random.normal(ks[3], (E, F, D), dtype=jnp.float32) * F ** (-0.5)
        b2 = jnp.zeros((E, D), dtype=jnp.float32)
        return {'x': x, 'switch_w': switch_w, 'switch_b': switch_b, 'w1': w1, 'b1': b1, 'w2': w2, 'b2': b2}
    _L0_ffn_in = _L0_ffn_setup()

    def _L1_attn_setup():
        import jax, jax.numpy as jnp
        import numpy as np
        NUM_HEADS = 16
        WINDOW = 32
        HIDDEN = 128
        HEAD_DIM = HIDDEN // NUM_HEADS
        key = jax.random.key(seed)
        ks = jax.random.split(key, 9)
        B, S, H = (2, 256, HIDDEN)
        s = 0.02
        return {'hidden_states': jax.random.normal(ks[0], (B, S, H), jnp.float32), 'Wq': jax.random.normal(ks[1], (H, H), jnp.float32) * s, 'bq': jnp.zeros((H,), jnp.float32), 'Wk': jax.random.normal(ks[2], (H, H), jnp.float32) * s, 'bk': jnp.zeros((H,), jnp.float32), 'Wv': jax.random.normal(ks[3], (H, H), jnp.float32) * s, 'bv': jnp.zeros((H,), jnp.float32), 'Wo': jax.random.normal(ks[4], (H, H), jnp.float32) * s, 'bo': jnp.zeros((H,), jnp.float32)}
    _L1_attn_in = _L1_attn_setup()

    def _L1_ffn_setup():
        import jax, jax.numpy as jnp
        import numpy as np
        DIM = 128

        def _reference_tuple_inner(x, W_r, W_k, W_v, mu_r, mu_k):
            B, T, C = x.shape
            x_prev = jnp.concatenate([jnp.zeros((B, 1, C), x.dtype), x[:, :-1, :]], axis=1)
            xr = mu_r * x + (1.0 - mu_r) * x_prev
            xk = mu_k * x + (1.0 - mu_k) * x_prev
            r = jax.nn.sigmoid(jnp.einsum('btc,dc->btd', xr, W_r))
            k = jnp.einsum('btc,dc->btd', xk, W_k)
            k_act = jnp.square(jax.nn.relu(k))
            out = r * jnp.einsum('btc,dc->btd', k_act, W_v)
            new_state = x[:, -1, :]
            return (out, new_state)
        key = jax.random.key(seed)
        ks = jax.random.split(key, 6)
        B, T, C = (8, 256, DIM)
        x = jax.random.normal(ks[0], (B, T, C), dtype=jnp.float32)
        s = 1.0 / np.sqrt(C)
        W_r = jax.random.uniform(ks[1], (C, C), jnp.float32, -s, s)
        W_k = jax.random.uniform(ks[2], (C, C), jnp.float32, -s, s)
        W_v = jax.random.uniform(ks[3], (C, C), jnp.float32, -s, s)
        mu_r = jax.random.uniform(ks[4], (C,), jnp.float32)
        mu_k = jax.random.uniform(ks[5], (C,), jnp.float32)
        return {'x': x, 'W_r': W_r, 'W_k': W_k, 'W_v': W_v, 'mu_r': mu_r, 'mu_k': mu_k}
    _L1_ffn_in = _L1_ffn_setup()
    _d = {'L0_attn_x': _L0_attn_in['x'], 'L0_attn_ln_gamma': _L0_attn_in['ln_gamma'], 'L0_attn_ln_beta': _L0_attn_in['ln_beta'], 'L0_attn_w_qkv': _L0_attn_in['w_qkv'], 'L0_attn_w_out': _L0_attn_in['w_out'], 'L0_ffn_switch_w': _L0_ffn_in['switch_w'], 'L0_ffn_switch_b': _L0_ffn_in['switch_b'], 'L0_ffn_w1': _L0_ffn_in['w1'], 'L0_ffn_b1': _L0_ffn_in['b1'], 'L0_ffn_w2': _L0_ffn_in['w2'], 'L0_ffn_b2': _L0_ffn_in['b2'], 'L1_attn_Wq': _L1_attn_in['Wq'], 'L1_attn_bq': _L1_attn_in['bq'], 'L1_attn_Wk': _L1_attn_in['Wk'], 'L1_attn_bk': _L1_attn_in['bk'], 'L1_attn_Wv': _L1_attn_in['Wv'], 'L1_attn_bv': _L1_attn_in['bv'], 'L1_attn_Wo': _L1_attn_in['Wo'], 'L1_attn_bo': _L1_attn_in['bo'], 'L1_ffn_W_r': _L1_ffn_in['W_r'], 'L1_ffn_W_k': _L1_ffn_in['W_k'], 'L1_ffn_W_v': _L1_ffn_in['W_v'], 'L1_ffn_mu_r': _L1_ffn_in['mu_r'], 'L1_ffn_mu_k': _L1_ffn_in['mu_k']}
    _x0 = _d['L0_attn_x']
    _d['L0_attn_x'] = jax.random.normal(jax.random.fold_in(jax.random.key(seed), 1), (2, 1024, 128), dtype=_x0.dtype)
    del _x0
    return _d

def reference(L0_attn_x, L0_attn_ln_gamma, L0_attn_ln_beta, L0_attn_w_qkv, L0_attn_w_out, L0_ffn_switch_w, L0_ffn_switch_b, L0_ffn_w1, L0_ffn_b1, L0_ffn_w2, L0_ffn_b2, L1_attn_Wq, L1_attn_bq, L1_attn_Wk, L1_attn_bk, L1_attn_Wv, L1_attn_bv, L1_attn_Wo, L1_attn_bo, L1_ffn_W_r, L1_ffn_W_k, L1_ffn_W_v, L1_ffn_mu_r, L1_ffn_mu_k):

    def _L0_attn_ref(x, ln_gamma, ln_beta, w_qkv, w_out):
        import jax, jax.numpy as jnp
        import numpy as np
        NUM_HEADS = 16
        DIM_HEAD = 64
        SCALE = DIM_HEAD ** (-0.5)
        ROPE_BASE = 10000.0

        def _rope(t):
            n, d = (t.shape[2], t.shape[3])
            inv_freq = 1.0 / ROPE_BASE ** (jnp.arange(0, d, 2, dtype=jnp.float32) / d)
            freqs = jnp.arange(n, dtype=jnp.float32)[:, None] * inv_freq[None, :]
            cos = jnp.concatenate([jnp.cos(freqs), jnp.cos(freqs)], axis=-1)
            sin = jnp.concatenate([jnp.sin(freqs), jnp.sin(freqs)], axis=-1)
            t1, t2 = jnp.split(t, 2, axis=-1)
            rot = jnp.concatenate([-t2, t1], axis=-1)
            return t * cos + rot * sin
        B, N, D = x.shape
        mu = jnp.mean(x, axis=-1, keepdims=True)
        var = jnp.mean(jnp.square(x - mu), axis=-1, keepdims=True)
        xn = (x - mu) * jax.lax.rsqrt(var + 1e-05) * ln_gamma + ln_beta
        qkv = xn @ w_qkv
        q, k, v = jnp.split(qkv, 3, axis=-1)

        def to_heads(t):
            return t.reshape(B, N, NUM_HEADS, DIM_HEAD).transpose(0, 2, 1, 3)
        q, k, v = (to_heads(q), to_heads(k), to_heads(v))
        q = jnp.concatenate([q[:, :, :1, :], _rope(q[:, :, 1:, :])], axis=2)
        k = jnp.concatenate([k[:, :, :1, :], _rope(k[:, :, 1:, :])], axis=2)
        dots = jnp.einsum('bhqd,bhkd->bhqk', q, k) * SCALE
        attn = jax.nn.softmax(dots, axis=-1)
        out = jnp.einsum('bhqk,bhkd->bhqd', attn, v)
        out = out.transpose(0, 2, 1, 3).reshape(B, N, NUM_HEADS * DIM_HEAD)
        return out @ w_out

    def _L0_ffn_ref(x, switch_w, switch_b, w1, b1, w2, b2):
        import jax, jax.numpy as jnp
        import numpy as np
        B, S, D = (4, 256, 128)
        E, F = (8, 512)
        b, s, d = x.shape
        t = x.reshape(-1, d)
        logits = t @ switch_w + switch_b
        route_prob = jax.nn.softmax(logits, axis=-1)
        route_prob_max = jnp.max(route_prob, axis=-1)
        routes = jnp.argmax(route_prob, axis=-1)
        out = jnp.zeros_like(t)
        n_experts = w1.shape[0]
        for e in range(n_experts):
            h = jax.nn.gelu(t @ w1[e] + b1[e])
            y = h @ w2[e] + b2[e]
            mask = (routes == e)[:, None]
            out = jnp.where(mask, y, out)
        out = out * route_prob_max[:, None]
        return out.reshape(b, s, d)

    def _L1_attn_ref(hidden_states, Wq, bq, Wk, bk, Wv, bv, Wo, bo):
        import jax, jax.numpy as jnp
        import numpy as np
        NUM_HEADS = 16
        WINDOW = 32
        HIDDEN = 128
        HEAD_DIM = HIDDEN // NUM_HEADS
        B, S, H = hidden_states.shape
        scale = jnp.sqrt(jnp.asarray(HEAD_DIM, hidden_states.dtype))
        q = (hidden_states @ Wq.T + bq).reshape(B, S, NUM_HEADS, HEAD_DIM)
        k = (hidden_states @ Wk.T + bk).reshape(B, S, NUM_HEADS, HEAD_DIM)
        v = (hidden_states @ Wv.T + bv).reshape(B, S, NUM_HEADS, HEAD_DIM)
        scores = jnp.einsum('bihd,bjhd->bhij', q, k) / scale
        blk = jnp.arange(S) // WINDOW
        allowed = blk[:, None] >= blk[None, :]
        scores = jnp.where(allowed, scores, jnp.zeros((), scores.dtype))
        probs = jax.nn.softmax(scores, axis=-1)
        ctx = jnp.einsum('bhij,bjhd->bihd', probs, v).reshape(B, S, H)
        return ctx @ Wo.T + bo

    def _L1_ffn_ref(x, W_r, W_k, W_v, mu_r, mu_k):
        import jax, jax.numpy as jnp
        import numpy as np
        DIM = 128

        def _reference_tuple_inner(x, W_r, W_k, W_v, mu_r, mu_k):
            B, T, C = x.shape
            x_prev = jnp.concatenate([jnp.zeros((B, 1, C), x.dtype), x[:, :-1, :]], axis=1)
            xr = mu_r * x + (1.0 - mu_r) * x_prev
            xk = mu_k * x + (1.0 - mu_k) * x_prev
            r = jax.nn.sigmoid(jnp.einsum('btc,dc->btd', xr, W_r))
            k = jnp.einsum('btc,dc->btd', xk, W_k)
            k_act = jnp.square(jax.nn.relu(k))
            out = r * jnp.einsum('btc,dc->btd', k_act, W_v)
            new_state = x[:, -1, :]
            return (out, new_state)
        return _reference_tuple_inner(x, W_r, W_k, W_v, mu_r, mu_k)[0]
    x = L0_attn_x
    x = x + _L0_attn_ref(_layernorm(x, axis=-1), L0_attn_ln_gamma, L0_attn_ln_beta, L0_attn_w_qkv, L0_attn_w_out)
    x = x + _L0_ffn_ref(_layernorm(x, axis=-1), L0_ffn_switch_w, L0_ffn_switch_b, L0_ffn_w1, L0_ffn_b1, L0_ffn_w2, L0_ffn_b2)
    x = x + _L1_attn_ref(_layernorm(x, axis=-1), L1_attn_Wq, L1_attn_bq, L1_attn_Wk, L1_attn_bk, L1_attn_Wv, L1_attn_bv, L1_attn_Wo, L1_attn_bo)
    x = x + _L1_ffn_ref(_layernorm(x, axis=-1), L1_ffn_W_r, L1_ffn_W_k, L1_ffn_W_v, L1_ffn_mu_r, L1_ffn_mu_k)
    return x

_drawn_inputs = setup_inputs


def setup_inputs(seed=0):
    import zlib

    import numpy as np

    out = dict(_drawn_inputs(seed))
    spreads = {'L0_attn_ln_gamma': (1.0, 0.6),
     'L0_attn_ln_beta': (0.0, 0.1),
     'L0_ffn_switch_b': (0.0, 0.1),
     'L0_ffn_b1': (0.0, 0.311),
     'L0_ffn_b2': (0.0, 0.1),
     'L1_attn_bq': (0.0, 0.8),
     'L1_attn_bk': (0.0, 2.0),
     'L1_attn_bv': (0.0, 0.35),
     'L1_attn_bo': (0.0, 0.1)}
    factors = {'L1_attn_Wq': 8.0,
     'L1_attn_Wk': 8.0,
     'L1_attn_Wv': 8.0,
     'L1_ffn_W_r': 3.217,
     'L1_ffn_mu_r': 6.398}
    for name, (base, spread) in spreads.items():
        noise = np.random.default_rng([zlib.crc32(name.encode()), seed]).standard_normal(out[name].shape)
        drawn = base * np.exp(spread * noise) if base else spread * noise
        out[name] = jnp.asarray(drawn.astype(out[name].dtype))
    for name, factor in factors.items():
        out[name] = (out[name] * factor).astype(out[name].dtype)
    return out
```

```python
from contextlib import ExitStack

import numpy as np

import concourse.bass as bass
from concourse import mybir

P = 128
B, N, D = 2, 1024, 128
T = B * N // P
TB = N // P
H0, DH0 = 16, 64
PAIRS = B * H0 // 2
HP = H0 // 2
SLOTS = 2 * TB
E, F = 8, 512
FC = F // P
H1, DH1, WIN = 16, 8, 32
HG = 4
EPS = 1e-5

ALU = mybir.AluOpType
ACT = mybir.ActivationFunctionType
AX = mybir.AxisListType
F32 = mybir.dt.float32
F32R = mybir.dt.float32r


def spread(ap, shape):
    return ap.rearrange("p (n o) -> p n o", o=1).broadcast_to(shape)


class Core:

    def __init__(self, nc, stack):
        self.nc, self.stack = nc, stack
        self.x = self.sb("residual", [P, T, D], F32)
        self.xT = self.sb("normed_T", [P, B * N], F32)
        self.ident = self.sb("ident", [P, P], F32)

    def sb(self, name, shape, dt):
        return self.stack.enter_context(self.nc.sbuf_tensor(name, shape, dt))

    def sem(self, name):
        return self.stack.enter_context(self.nc.semaphore(name))


def normalize(nc, core, tag, first_load=None, affine=None, twice=False, extra=None):
    with ExitStack() as st:
        sb = lambda n, s: st.enter_context(nc.sbuf_tensor(f"{tag}_{n}", s, F32))
        xc = sb("xc", [P, T, D])
        xn = sb("xn", [P, T, D])
        stat = sb("stat", [P, 8, T])
        sqrt_out = sb("sqrt", [P, 2, T])
        tp = [st.enter_context(nc.psum_tensor(f"{tag}_tp{i}", [P, 512], F32)) for i in range(4)]
        loaded = core.sem(f"{tag}_loaded")
        dve_step = core.sem(f"{tag}_dve_step")
        var_ready = core.sem(f"{tag}_var_ready")
        sqrt_ready = core.sem(f"{tag}_sqrt_ready")
        xn_ready = core.sem(f"{tag}_xn_ready")
        ident_ready = core.sem(f"{tag}_ident_ready")
        xnT_ready = core.sem(f"{tag}_xnT_ready")
        copied = core.sem(f"{tag}_copied")
        gb = sb("gamma_beta", [P, 2, D]) if affine else None

        with nc.Block() as block:
            if first_load is not None:
                @block.sync
                def _(sp):
                    sp.dma_start(core.x[:], first_load.rearrange("b (t p) d -> p (b t) d", p=P)).then_inc(loaded, 16)
                    for i, v in enumerate(affine):
                        sp.dma_start(gb[:, i, :], v.rearrange("(o d) -> o d", o=1).broadcast_to([P, D])).then_inc(loaded, 16)

                @block.gpsimd
                def _(pool):
                    nc.gpsimd.memset(core.ident[:], 0.0).then_inc(ident_ready, 1)
                    pool.wait_ge(ident_ready, 1)
                    nc.gpsimd.affine_select(out=core.ident[:], in_=core.ident[:], compare_op=ALU.not_equal, fill=1.0,
                                            base=0, pattern=[[-1, P]], channel_multiplier=1).then_inc(ident_ready, 1)

            @block.vector
            def _(dve):
                steps = [0]

                def step(ins):
                    steps[0] += 1
                    ins.then_inc(dve_step, 1)
                    dve.wait_ge(dve_step, steps[0])

                def norm(src, dst, k):
                    total, mean, var, rstd, t = (stat[:, i, :] for i in (0, 1, 2, 3, 4))
                    step(nc.vector.tensor_reduce(total, src[:], axis=AX.X, op=ALU.add))
                    step(nc.vector.tensor_scalar(mean, total, 1.0 / D, None, ALU.mult))
                    step(nc.vector.tensor_tensor(xc[:], src[:], spread(mean, [P, T, D]), ALU.subtract))
                    step(nc.vector.tensor_tensor(xn[:], xc[:], xc[:], ALU.mult))
                    step(nc.vector.tensor_reduce(total, xn[:], axis=AX.X, op=ALU.add))
                    step(nc.vector.tensor_scalar(var, total, 1.0 / D, EPS, ALU.mult, ALU.add))
                    dve.sem_inc(var_ready, 1)
                    dve.wait_ge(sqrt_ready, k + 1)
                    step(nc.vector.reciprocal(rstd, sqrt_out[:, k, :]))
                    step(nc.vector.tensor_tensor(t, rstd, rstd, ALU.mult))
                    step(nc.vector.tensor_tensor(t, t, var, ALU.mult))
                    step(nc.vector.tensor_scalar(t, t, -0.5, 1.5, ALU.mult, ALU.add))
                    step(nc.vector.tensor_tensor(rstd, rstd, t, ALU.mult))
                    last = nc.vector.tensor_tensor(dst[:], xc[:], spread(rstd, [P, T, D]), ALU.mult)
                    return last

                if first_load is not None:
                    dve.wait_ge(loaded, 48)
                if twice:
                    step(norm(core.x, xn, 0))
                    step(norm(xn, xn, 1))
                    step(nc.vector.tensor_tensor(xn[:], xn[:], gb[:, 0:1, :].broadcast_to([P, T, D]), ALU.mult))
                    nc.vector.tensor_tensor(xn[:], xn[:], gb[:, 1:2, :].broadcast_to([P, T, D]), ALU.add).then_inc(xn_ready, 1)
                else:
                    norm(core.x, xn, 0).then_inc(xn_ready, 1)

            @block.tensor
            def _(pe):
                pe.wait_ge(xn_ready, 1)
                if first_load is not None:
                    pe.wait_ge(ident_ready, 2)
                for t in range(T):
                    ins = nc.tensor.transpose(tp[t // 4][:, t % 4 * P:(t % 4 + 1) * P], xn[:, t, :], core.ident[:])
                    if t % 4 == 3:
                        ins.then_inc(xnT_ready, 1)

            @block.scalar
            def _(act):
                for k in range(2 if twice else 1):
                    act.wait_ge(var_ready, k + 1)
                    nc.scalar.activation(sqrt_out[:, k, :], stat[:, 2, :], ACT.Sqrt).then_inc(sqrt_ready, 1)
                for i in range(T // 4):
                    act.wait_ge(xnT_ready, i + 1)
                    nc.scalar.activation(core.xT[:, i * 512:(i + 1) * 512], tp[i][:], ACT.Copy).then_inc(copied, 1)


def rotary_attention(nc, core, rope, w_qkv, w_out):
    with ExitStack() as st:
        sb = lambda n, s, dt=F32: st.enter_context(nc.sbuf_tensor(f"a0_{n}", s, dt))
        ps = lambda n, s: st.enter_context(nc.psum_tensor(f"a0_{n}", s, F32))
        sem = lambda n: core.sem(f"a0_{n}")

        tables = sb("tables", [P, 4, N])
        xn_cur = sb("xn_cur", [P, N])
        w_cur = sb("w_cur", [P, 3, P])
        wo_cur = sb("wo_cur", [P, D])
        raw = [sb("q_raw", [P, N]), sb("k_raw", [P, N])]
        rot = [sb("q_rot", [P, N]), sb("k_rot", [P, N])]
        hi = [sb("q_hi", [P, N], F32R), sb("k_hi", [P, N], F32R)]
        lo = [sb("q_lo", [P, N], F32R), sb("k_lo", [P, N], F32R)]
        q_stack = [[sb(f"q_stack{i}{h}", [P, N], F32R) for h in "ab"] for i in range(2)]
        k_stack = [[[sb(f"k_stack{i}{h}{part}", [P, N], F32R) for part in ("h", "l")] for h in "ab"] for i in range(2)]
        v = [sb(f"v{i}", [P, TB, P]) for i in range(2)]
        probs = [sb(f"probs{i}", [P, N]) for i in range(4)]
        probs_T = [sb(f"probs_T{i}", [P, 2, TB, 256]) for i in range(2)]
        negmax = sb("negmax", [P, SLOTS])
        den = sb("den", [P, SLOTS])
        rden = sb("rden", [P, 4, 64])
        rden_b = sb("rden_b", [P, 256])
        attn_T = sb("attn_T", [P, 256])

        score_ps = [ps(f"score{i}", [P, N]) for i in range(2)]
        tr_ps = [ps(f"tr{i}", [P, 512]) for i in range(2)]
        out_ps = ps("out", [P, 512])
        misc_ps = ps("misc", [P, 512])

        tables_loaded, zeroed = sem("tables_loaded"), sem("zeroed")
        operands_loaded, wo_loaded = sem("operands_loaded"), sem("wo_loaded")
        swapped = [sem("q_swapped"), sem("k_swapped")]
        rotated = [sem("q_rotated"), sem("k_rotated")]
        summed = [sem("q_summed"), sem("k_summed")]
        hi_ready = [sem("q_hi_ready"), sem("k_hi_ready")]
        lo_ready = [sem("q_lo_ready"), sem("k_lo_ready")]
        stacked = [sem("q_stacked"), sem("k_stacked")]
        STACKED = [64, 128]
        scores_ready, negmax_ready, probs_ready = sem("scores_ready"), sem("negmax_ready"), sem("probs_ready")
        tr_ready = [sem("tr_lo_ready"), sem("tr_hi_ready")]
        tr_copied = [sem("tr_lo_copied"), sem("tr_hi_copied")]
        misc_ready, misc_free = sem("misc_ready"), sem("misc_free")
        pv_done, attn_ready, rden_ready = sem("pv_done"), sem("attn_ready"), sem("rden_ready")

        ITEM_SLOTS = [0, 1, 2, 3, 4, 5, 6, 7, 8, 9, 10, 11, 14, 15]
        ITEMS, FIRST_ITEMS = len(ITEM_SLOTS), 6
        ITEM = {s: FIRST_ITEMS + i for i, s in enumerate(ITEM_SLOTS)}
        LAST_ITEM = {2: FIRST_ITEMS, 3: FIRST_ITEMS + 1, 7: FIRST_ITEMS + 2}
        PAIRS2 = PAIRS // 2

        def unit(s):
            return 2 * (s // 4) + s % 4 // 2, s % 2

        def progress(it, par):
            return lambda m, c: it * (2 * m) + (par * m + c)

        LAST = lambda m, c: m * PAIRS + c
        BEFORE = lambda m, c: -m + c

        with nc.Block() as block:
            @block.sync
            def _(sp):
                def load_operands(col, row):
                    sp.dma_start(w_cur[:], w_qkv.rearrange("d (c n) -> d c n", c=3)[:, :, bass.ds(col, P)])\
                        .then_inc(operands_loaded, 16)
                    sp.dma_start(xn_cur[:], core.xT[:, bass.ds(row, N)]).then_inc(operands_loaded, 16)

                def swap_halves(i):
                    for r in range(4):
                        sp.dma_start(rot[i][32 * r:32 * r + 32, :], raw[i][32 * (r ^ 1):32 * (r ^ 1) + 32, :])\
                            .then_inc(swapped[i], 16)

                def stack_q(par):
                    for h in range(2):
                        rows = slice(64 * h, 64 * h + 64)
                        sp.dma_start(q_stack[par][h][0:64, :].bitcast(F32), hi[0][rows, :].bitcast(F32)).then_inc(stacked[0], 16)
                        sp.dma_start(q_stack[par][h][64:128, :].bitcast(F32), lo[0][rows, :].bitcast(F32)).then_inc(stacked[0], 16)

                def stack_k(par):
                    for h in range(2):
                        rows = slice(64 * h, 64 * h + 64)
                        for part, src in enumerate((hi[1], lo[1])):
                            for half in range(2):
                                sp.dma_start(k_stack[par][h][part][64 * half:64 * half + 64, :].bitcast(F32), src[rows, :].bitcast(F32))\
                                    .then_inc(stacked[1], 16)

                load_operands(0, 0)
                sp.dma_start(tables[:], rope.rearrange("t p n -> p t n")).then_inc(tables_loaded, 16)
                sp.wait_ge(misc_free, 2)
                swap_halves(0)
                sp.wait_ge(misc_free, 4)
                swap_halves(1)
                sp.wait_ge(misc_ready, FIRST_ITEMS)
                load_operands(P, 0)
                sp.wait_ge(lo_ready[0], 1)
                stack_q(0)
                sp.wait_ge(lo_ready[1], 1)
                stack_k(0)
                with sp.Fori(0, PAIRS2) as it:
                    for par in range(2):
                        at = progress(it, par)
                        wo_row = sp.snap(((it * 2 + par) % HP) * P)
                        next_col = sp.snap((it * 2 + par + 2) % HP * P)
                        next_row = sp.snap((it * 2 + par + 2) // HP % B * N)
                        for i, slot in ((0, 1), (1, 5)):
                            sp.wait_ge(misc_free, at(ITEMS, ITEM[slot] + 1))
                            sp.wait_ge(summed[i], at(1, 1))
                            swap_halves(i)
                        sp.wait_ge(lo_ready[0], at(1, 2))
                        stack_q(1 - par)
                        sp.wait_ge(misc_ready, at(ITEMS, ITEM[7] + 1))
                        sp.dma_start(wo_cur[:], w_out[bass.ds(wo_row, P), :]).then_inc(wo_loaded, 16)
                        sp.wait_ge(misc_ready, at(ITEMS, ITEM[9] + 1))
                        load_operands(next_col, next_row)
                        sp.wait_ge(lo_ready[1], at(1, 2))
                        stack_k(1 - par)
                sp.wait_ge(operands_loaded, 32 * (PAIRS + 2))
                sp.wait_ge(stacked[0], STACKED[0] * (PAIRS + 1))
                sp.wait_ge(stacked[1], STACKED[1] * (PAIRS + 1))

            @block.gpsimd
            def _(pool):
                nc.gpsimd.memset(probs[3][:], 0.0)
                nc.gpsimd.memset(probs_T[0][:], 0.0)
                nc.gpsimd.memset(probs_T[1][:], 0.0)
                nc.gpsimd.memset(v[1][:], 0.0)
                nc.gpsimd.memset(den[:], 1.0)
                nc.gpsimd.memset(rden_b[:], 0.0)
                nc.gpsimd.memset(wo_cur[:], 0.0).then_inc(zeroed, 1)

                def sums_and_rests(at):
                    for i in range(2):
                        pool.wait_ge(rotated[i], at(2, 4))
                        nc.gpsimd.tensor_tensor(raw[i][:], raw[i][:], rot[i][:], ALU.add).then_inc(summed[i], 1)
                        pool.wait_ge(hi_ready[i], at(1, 2))
                        nc.gpsimd.tensor_tensor(lo[i][:], raw[i][:], hi[i][:].bitcast(F32), ALU.subtract)\
                            .then_inc(lo_ready[i], 1)

                sums_and_rests(BEFORE)
                with pool.Fori(0, PAIRS2) as it:
                    for par in range(2):
                        sums_and_rests(progress(it, par))

            @block.tensor
            def _(pe):
                def project_T(i, half):
                    nc.tensor.matmul(misc_ps[:], w_cur[:, i, :], xn_cur[:, half * 512:half * 512 + 512],
                                     start=True, stop=True).then_inc(misc_ready, 1)

                def project_v(half):
                    for t in range(4):
                        last = nc.tensor.matmul(misc_ps[:, t * P:t * P + P], xn_cur[:, (4 * half + t) * P:(4 * half + t + 1) * P],
                                                w_cur[:, 2, :], start=True, stop=True)
                    last.then_inc(misc_ready, 1)

                def scores(s, par):
                    tile, h = unit(s)
                    for half in range(2):
                        cols = slice(half * 512, half * 512 + 512)
                        for part in range(2):
                            last = nc.tensor.matmul(score_ps[s % 2][:, cols], q_stack[par][h][:, tile * P:tile * P + P],
                                                    k_stack[par][h][part][:, cols], start=part == 0, stop=part == 1)
                    last.then_inc(scores_ready, 1)

                def transposes(s):
                    for k in range(TB):
                        last = nc.tensor.transpose(tr_ps[k // 4][:, k % 4 * P:k % 4 * P + P],
                                                   probs[s % 4][:, k * P:k * P + P], core.ident[:])
                        if k % 4 == 3:
                            last.then_inc(tr_ready[k // 4], 1)

                def slot(s, par, at, item, last=False):
                    if not last or s == 0:
                        pe.wait_ge(probs_ready, at(SLOTS, s))
                    if not last:
                        if s == SLOTS - 1:
                            for i in range(2):
                                pe.wait_ge(stacked[i], at(STACKED[i], 2 * STACKED[i]))
                            scores(0, 1 - par)
                        else:
                            scores(s + 1, par)
                    if not last or s == 0:
                        for i in range(2):
                            pe.wait_ge(tr_copied[i], at(SLOTS, s))
                        transposes(s - 1)
                    if s in item:
                        pe.wait_ge(misc_free, at(ITEMS, item[s]))
                        if s in (0, 1, 4, 5):
                            if s == 0:
                                pe.wait_ge(operands_loaded, at(32, 64))
                            project_T(s // 4, s % 2)
                        elif s in (8, 9):
                            project_v(s - 8)
                        elif s % 4 == 2:
                            pe.wait_ge(rden_ready, at(4, s // 4 + 1))
                            for q in range(2):
                                ins = nc.tensor.transpose(misc_ps[:, q * P:q * P + P],
                                                          rden[:, 2 * q:2 * q + 2, :].rearrange("p h d -> p (h d)"), core.ident[:])
                            ins.then_inc(misc_ready, 1)
                        else:
                            pe.wait_ge(attn_ready, at(4, s // 4 + 1))
                            pe.wait_ge(wo_loaded, at(16, 16 if s > 7 else 0))
                            for q in range(2):
                                ins = nc.tensor.matmul(misc_ps[:, q * P:q * P + P], attn_T[:, q * P:q * P + P], wo_cur[:],
                                                       start=True, stop=True)
                            ins.then_inc(misc_ready, 1)
                    if not last or s < 5:
                        r, grp = (s - 5) % 4, (s - 5) // 4 % 2
                        if r == 0:
                            for i in range(2):
                                pe.wait_ge(tr_copied[i], at(SLOTS, s))
                            pe.wait_ge(attn_ready, at(4, s // 4 + 1))
                            if s == 5:
                                pe.wait_ge(misc_free, at(ITEMS, 0))
                        for k in (2 * r, 2 * r + 1):
                            for h in range(2):
                                ins = nc.tensor.matmul(out_ps[64 * h:64 * h + 64, 0:256],
                                                       v[par if s >= 5 else 1 - par][:, k, 64 * h:64 * h + 64],
                                                       probs_T[grp][:, h, k, :], start=k == 0, stop=k == TB - 1)
                        if r == 3:
                            ins.then_inc(pv_done, 1)

                pe.wait_ge(operands_loaded, 32)
                for k in range(FIRST_ITEMS):
                    if k:
                        pe.wait_ge(misc_free, k)
                    if k < 4:
                        project_T(k // 2, k % 2)
                    else:
                        project_v(k - 4)
                pe.wait_ge(zeroed, 1)
                for h in range(2):
                    for k in range(6):
                        nc.tensor.matmul(out_ps[64 * h:64 * h + 64, 0:256], v[1][:, k, 64 * h:64 * h + 64],
                                         probs_T[0][:, h, k, :], start=k == 0, stop=False)
                for i in range(2):
                    pe.wait_ge(stacked[i], STACKED[i])
                scores(0, 0)
                with pe.Fori(0, PAIRS2) as it:
                    for par in range(2):
                        for s in range(SLOTS):
                            slot(s, par, progress(it, par), ITEM)
                for s in range(8):
                    slot(s, 0, LAST, LAST_ITEM, last=True)

            @block.scalar
            def _(act):
                def copy_item(dst, width=512):
                    nc.scalar.activation(dst, misc_ps[:, 0:width], ACT.Copy).then_inc(misc_free, 1)

                def copy_tr(s):
                    tile, h = unit((s - 1) % SLOTS)
                    nc.scalar.activation(probs_T[(s - 1) // 4 % 2][:, h, 0:4, tile % 2 * P:tile % 2 * P + P],
                                         tr_ps[0][:].rearrange("p (k q) -> p k q", k=4), ACT.Copy).then_inc(tr_copied[0], 1)

                def slot(s, par, at, item, last=False):
                    if not last:
                        act.wait_ge(negmax_ready, at(SLOTS, s + 1))
                        nc.scalar.activation(probs[s % 4][:], score_ps[s % 2][:], ACT.Exp, bias=negmax[:, s:s + 1],
                                             accum_out=den[:, s:s + 1]).then_inc(probs_ready, 1)
                    if not last or s == 0:
                        act.wait_ge(tr_ready[0], at(SLOTS, s + 1))
                        copy_tr(s)
                    if s in item and s % 4 != 3:
                        act.wait_ge(misc_ready, at(ITEMS, item[s] + 1))
                        if s in (0, 1, 4, 5):
                            i = s // 4
                            if s % 2 == 0:
                                act.wait_ge(lo_ready[i], at(1, 1))
                            copy_item(raw[i][:, s % 2 * 512:s % 2 * 512 + 512])
                        elif s in (8, 9):
                            copy_item(v[1 - par][:, 4 * (s - 8):4 * (s - 8) + 4, :].rearrange("p t n -> p (t n)"))
                        else:
                            copy_item(rden_b[:], 256)

                act.wait_ge(zeroed, 1)
                for k in range(FIRST_ITEMS):
                    act.wait_ge(misc_ready, k + 1)
                    copy_item(raw[k // 2][:, k % 2 * 512:k % 2 * 512 + 512] if k < 4 else
                              v[0][:, 4 * (k - 4):4 * (k - 4) + 4, :].rearrange("p t n -> p (t n)"))
                with act.Fori(0, PAIRS2) as it:
                    for par in range(2):
                        for s in range(SLOTS):
                            slot(s, par, progress(it, par), ITEM)
                for s in range(8):
                    slot(s, 0, LAST, LAST_ITEM, last=True)

            @block.vector
            def _(dve):
                def row_max(s):
                    nc.vector.tensor_reduce(negmax[:, s:s + 1], score_ps[s % 2][:], axis=AX.X, op=ALU.max, negate=True)\
                        .then_inc(negmax_ready, 1)

                def rotate(i, j):
                    t = (raw, rot)[j][i]
                    nc.vector.tensor_tensor(t[:], t[:], tables[:, 2 * i + j, :], ALU.mult).then_inc(rotated[i], 1)

                def split(i):
                    nc.vector.tensor_copy(hi[i][:], raw[i][:]).then_inc(hi_ready[i], 1)

                def slot(s, par, at, batch, item, last=False):
                    if not last:
                        dve.wait_ge(scores_ready, at(SLOTS, s + 2))
                        row_max((s + 1) % SLOTS)
                    if s % 4 == 0 and (not last or s == 0):
                        dve.wait_ge(probs_ready, at(SLOTS, s))
                        c = 4 * ((s // 4 - 1) % 4)
                        nc.vector.reciprocal(rden[:], spread(den[:, c:c + 4], [P, 4, 64])).then_inc(rden_ready, 1)
                    if s % 4 == 1:
                        dve.wait_ge(pv_done, at(4, s // 4 + 1))
                        dve.wait_ge(misc_free, at(ITEMS, item[s - 3] + 1 if s > 1 else FIRST_ITEMS - 1))
                        nc.vector.tensor_tensor(attn_T[:], out_ps[:, 0:256], rden_b[:], ALU.mult).then_inc(attn_ready, 1)
                    if not last or s == 0:
                        dve.wait_ge(tr_ready[1], at(SLOTS, s + 1))
                        tile, h = unit((s - 1) % SLOTS)
                        nc.vector.tensor_copy(probs_T[(s - 1) // 4 % 2][:, h, 4:8, tile % 2 * P:tile % 2 * P + P],
                                              tr_ps[1][:].rearrange("p (k q) -> p k q", k=4)).then_inc(tr_copied[1], 1)
                    if s % 4 == 3:
                        dve.wait_ge(misc_ready, at(ITEMS, item[s] + 1))
                        rows = core.x[:, bass.ds(batch[s > 7] * TB + 2 * ((s // 4 + 2) % 4), 2), :]
                        nc.vector.tensor_tensor(rows, misc_ps[:, 0:256].rearrange("p (t d) -> p t d", t=2), rows, ALU.add)\
                            .then_inc(misc_free, 1)
                    if not last:
                        if s in (3, 7):
                            i = s // 4
                            dve.wait_ge(swapped[i], at(64, 128))
                            rotate(i, 0)
                        if s in (4, 8):
                            rotate(s // 4 - 1, 1)
                        if s in (6, 10):
                            i = s // 8
                            dve.wait_ge(summed[i], at(1, 2))
                            dve.wait_ge(stacked[i], at(STACKED[i], STACKED[i]))
                            split(i)

                dve.wait_ge(tables_loaded, 16)
                for i in range(2):
                    dve.wait_ge(swapped[i], 64)
                    rotate(i, 0)
                    rotate(i, 1)
                    dve.wait_ge(summed[i], 1)
                    split(i)
                dve.wait_ge(scores_ready, 1)
                row_max(0)
                with dve.Fori(0, PAIRS2) as it:
                    for par in range(2):
                        batch = (((it + 2 * HP // 2 - 1) // (HP // 2)) % B if par == 0 else it // (HP // 2), it // (HP // 2))
                        for s in range(SLOTS):
                            slot(s, par, progress(it, par), batch, ITEM)
                for s in range(8):
                    slot(s, 0, LAST, (B - 1, 0), LAST_ITEM, last=True)


def experts(nc, core, sw, sb_, w1, b1, w2, b2):
    with ExitStack() as st:
        sb = lambda n, s, dt=F32: st.enter_context(nc.sbuf_tensor(f"f0_{n}", s, dt))
        ps = lambda n, s: st.enter_context(nc.psum_tensor(f"f0_{n}", s, F32))
        sem = lambda n: core.sem(f"f0_{n}")
        TG = B * N // 512

        switch = sb("switch", [P, E])
        switch_b = sb("switch_b", [P, E])
        b1_rows = sb("b1_rows", [E * FC, P])
        b1_T = sb("b1_T", [P, E * FC])
        b1_cur = [sb(f"b1_cur{i}", [P, FC]) for i in range(2)]
        b2_rows = sb("b2_rows", [E, D])
        w1_cur = [sb(f"w1_cur{i}", [P, F]) for i in range(2)]
        w2_cur = [sb(f"w2_cur{i}", [P, FC, D]) for i in range(2)]
        hidden = [sb(f"hidden{i}", [P, FC, 512]) for i in range(2)]
        logits, shifted, expd, order, cand, gates = (sb(n, [P, T, E]) for n in ("logits", "shifted", "expd", "order", "cand", "gates"))
        iota = sb("iota", [P, E])
        top, total, first = (sb(n, [P, T]) for n in ("top", "total", "first"))
        gates_e = sb("gates_e", [P, E, T])
        gates_T = sb("gates_T", [E, B * N])
        h_ps = [ps(f"h{i}", [P, 512]) for i in range(FC)]
        y_ps = [ps(f"y{i}", [P, 512]) for i in range(2)]
        route_ps = ps("route", [P, 512])
        bias_ps = ps("bias", [P, 512])

        small_loaded, weights_loaded = sem("small_loaded"), sem("weights_loaded")
        iota_ready, logits_ready, b1_ready, b1_copied = sem("iota_ready"), sem("logits_ready"), sem("b1_ready"), sem("b1_copied")
        b1_kept = sem("b1_kept")
        dve_step, shifted_ready, expd_ready, gates_ready = sem("dve_step"), sem("shifted_ready"), sem("expd_ready"), sem("gates_ready")
        gt_ready, gt_copied, bias_ready, bias_added = sem("gt_ready"), sem("gt_copied"), sem("bias_ready"), sem("bias_added")
        h_ready, h_done, y_ready, y_added = sem("h_ready"), sem("h_done"), sem("y_ready"), sem("y_added")

        with nc.Block() as block:
            @block.sync
            def _(sp):
                def load_expert(e, par):
                    sp.dma_start(w1_cur[par][:], w1.rearrange("e d f -> d e f")[:, bass.ds(e, 1), :].rearrange("d e f -> d (e f)"))\
                        .then_inc(weights_loaded, 16)
                    sp.dma_start(w2_cur[par][:], w2.rearrange("e (c p) d -> p (e c) d", p=P)[:, bass.ds(e * FC, FC), :])\
                        .then_inc(weights_loaded, 16)

                sp.dma_start(switch[:], sw).then_inc(small_loaded, 16)
                sp.dma_start(switch_b[:], sb_.rearrange("(o e) -> o e", o=1).broadcast_to([P, E])).then_inc(small_loaded, 16)
                sp.dma_start(b1_rows[:], b1.rearrange("e (c p) -> (e c) p", p=P)).then_inc(small_loaded, 16)
                sp.dma_start(b2_rows[:], b2).then_inc(small_loaded, 16)
                load_expert(0, 0)
                load_expert(1, 1)
                with sp.Fori(0, E // 2) as it:
                    for par in range(2):
                        e = sp.snap((it * 2 + par + 2) % E)
                        sp.wait_ge(y_ready, it * (2 * TG) + (par + 1) * TG)
                        load_expert(e, par)
                sp.wait_ge(weights_loaded, 32 * (E + 2))

            @block.gpsimd
            def _(pool):
                nc.gpsimd.iota(iota[:], pattern=[[1, E]], base=-E, channel_multiplier=0, allow_small_or_imprecise_dtypes=True).then_inc(iota_ready, 1)

            @block.tensor
            def _(pe):
                def hidden_of(f, tg, par):
                    nc.tensor.matmul(h_ps[f][:], w1_cur[par][:, f * P:f * P + P], core.xT[:, tg * 512:tg * 512 + 512],
                                     start=True, stop=True).then_inc(h_ready, 1)

                pe.wait_ge(small_loaded, 64)
                for t in range(T):
                    ins = nc.tensor.matmul(route_ps[:, t * E:t * E + E], core.xT[:, t * P:t * P + P], switch[:], start=True, stop=True)
                ins.then_inc(logits_ready, 1)
                nc.tensor.transpose(bias_ps[:, 0:E * FC], b1_rows[:], core.ident[0:E * FC, 0:E * FC]).then_inc(b1_ready, 1)
                pe.wait_ge(weights_loaded, 64)
                for f in range(FC):
                    hidden_of(f, 0, 0)
                pe.wait_ge(gates_ready, 1)
                pe.wait_ge(b1_copied, 1)
                for i in range(T // 4):
                    if i:
                        pe.wait_ge(gt_copied, i)
                    for t in range(4 * i, 4 * i + 4):
                        ins = nc.tensor.transpose(bias_ps[0:E, t % 4 * P:t % 4 * P + P], gates[:, t, :], core.ident[:])
                    ins.then_inc(gt_ready, 1)
                pe.wait_ge(gt_copied, T // 4)
                for i in range(T // 4):
                    if i:
                        pe.wait_ge(bias_added, i)
                    for t in range(4 * i, 4 * i + 4):
                        ins = nc.tensor.matmul(route_ps[:, t % 4 * P:t % 4 * P + P], gates_T[:, t * P:t * P + P], b2_rows[:],
                                               start=True, stop=True)
                    ins.then_inc(bias_ready, 1)

                with pe.Fori(0, E // 2) as it:
                    for par in range(2):
                        for tg in range(TG):
                            k = par * TG + tg
                            if tg == TG - 1:
                                pe.wait_ge(weights_loaded, it * 64 + 32 * (par + 2))
                            for f in range(FC):
                                pe.wait_ge(h_done, it * (2 * TG * FC) + (k * FC + f + 1))
                                hidden_of(f, (tg + 1) % TG, par if tg < TG - 1 else 1 - par)
                            if k < 2:
                                pe.wait_ge(y_added, it * (2 * TG) + max(k - 1, 0))
                            else:
                                pe.wait_ge(y_added, it * (2 * TG) + (k - 1))
                            for t in range(4):
                                for f in range(FC):
                                    ins = nc.tensor.matmul(y_ps[k % 2][:, t * P:t * P + P], hidden[k % 2][:, f, t * P:t * P + P],
                                                           w2_cur[par][:, f, :], start=f == 0, stop=f == FC - 1)
                            ins.then_inc(y_ready, 1)

            @block.scalar
            def _(act):
                def gelu(f, k, par):
                    nc.scalar.activation(hidden[k % 2][:, f, :], h_ps[f][:], ACT.Gelu_apprx_tanh,
                                         bias=b1_cur[par][:, f:f + 1]).then_inc(h_done, 1)

                def keep_b1(e, par):
                    nc.scalar.activation(b1_cur[par][:], b1_T[:, bass.ds(e * FC, FC)], ACT.Copy).then_inc(b1_kept, 1)

                act.wait_ge(b1_ready, 1)
                nc.scalar.activation(b1_T[:], bias_ps[:, 0:E * FC], ACT.Copy).then_inc(b1_copied, 1)
                act.wait_ge(shifted_ready, 1)
                nc.scalar.activation(expd[:], shifted[:], ACT.Exp).then_inc(expd_ready, 1)
                for i in range(T // 4):
                    act.wait_ge(gt_ready, i + 1)
                    nc.scalar.activation(gates_T[:, i * 512:i * 512 + 512], bias_ps[0:E, :], ACT.Copy).then_inc(gt_copied, 1)
                act.wait_ge(b1_copied, 1)
                keep_b1(0, 0)
                act.wait_ge(b1_kept, 1)
                for f in range(FC):
                    act.wait_ge(h_ready, f + 1)
                    gelu(f, 0, 0)
                with act.Fori(0, E // 2) as it:
                    for k in range(2 * TG):
                        par = (k + 1) // TG % 2
                        if k % TG == TG - 1:
                            act.wait_ge(b1_kept, it * 2 + (k // TG + 2))
                        for f in range(FC):
                            act.wait_ge(h_ready, it * (2 * TG * FC) + ((k + 1) * FC + f + 1))
                            gelu(f, k + 1, par)
                        if k % TG == 0:
                            keep_b1((it * 2 + (k // TG + 1)) % E, 1 - par)

            @block.vector
            def _(dve):
                steps = [0]

                def step(ins):
                    steps[0] += 1
                    ins.then_inc(dve_step, 1)
                    dve.wait_ge(dve_step, steps[0])

                shape = [P, T, E]
                dve.wait_ge(logits_ready, 1)
                dve.wait_ge(iota_ready, 1)
                step(nc.vector.tensor_tensor(logits[:], route_ps[:, 0:T * E].rearrange("p (t e) -> p t e", t=T),
                                             switch_b[:].rearrange("p (o e) -> p o e", o=1).broadcast_to(shape), ALU.add))
                step(nc.vector.tensor_reduce(top[:], logits[:], axis=AX.X, op=ALU.max))
                nc.vector.tensor_tensor(shifted[:], logits[:], spread(top[:], shape), ALU.subtract).then_inc(shifted_ready, 1)
                step(nc.vector.tensor_tensor(order[:], logits[:], spread(top[:], shape), ALU.is_equal))
                experts_row = iota[:].rearrange("p (o e) -> p o e", o=1).broadcast_to(shape)
                step(nc.vector.tensor_tensor(cand[:], order[:], experts_row, ALU.mult))
                step(nc.vector.tensor_reduce(first[:], cand[:], axis=AX.X, op=ALU.min))
                step(nc.vector.tensor_tensor(cand[:], experts_row, spread(first[:], shape), ALU.is_equal))
                dve.wait_ge(expd_ready, 1)
                step(nc.vector.tensor_reduce(total[:], expd[:], axis=AX.X, op=ALU.add))
                step(nc.vector.reciprocal(total[:], total[:]))
                nc.vector.tensor_tensor(gates[:], cand[:], spread(total[:], shape), ALU.mult).then_inc(gates_ready, 1)
                dve.wait_ge(gates_ready, 1)
                step(nc.vector.tensor_copy(gates_e[:].rearrange("p e t -> p t e"), gates[:]))
                for i in range(T // 4):
                    dve.wait_ge(bias_ready, i + 1)
                    rows = core.x[:, 4 * i:4 * i + 4, :]
                    nc.vector.tensor_tensor(rows, route_ps[:].rearrange("p (t d) -> p t d", t=4), rows, ALU.add).then_inc(bias_added, 1)
                dve.wait_ge(bias_added, T // 4)
                with dve.Fori(0, E // 2) as it:
                    for k in range(2 * TG):
                        dve.wait_ge(y_ready, it * (2 * TG) + (k + 1))
                        for t in range(4):
                            tile = k % TG * 4 + t
                            ins = nc.vector.scalar_tensor_tensor(
                                out=core.x[:, tile, :], in0=y_ps[k % 2][:, t * P:t * P + P],
                                scalar=gates_e[:, bass.ds(it * 2 + k // TG, 1), tile], in1=core.x[:, tile, :],
                                op0=ALU.mult, op1=ALU.add)
                        ins.then_inc(y_added, 1)


def block_attention(nc, core, consts, Wq, bq, Wk, bk, Wv, bv, Wo, bo):
    G = H1 // HG
    ITERS = B * G
    GR = TB // 2
    UNITS = GR * 2 * HG
    FIX = UNITS - 2 * HG
    VT = TB + GR - 1
    with ExitStack() as st:
        sb = lambda n, s, dt=F32: st.enter_context(nc.sbuf_tensor(f"a1_{n}", s, dt))
        sem = lambda n: core.sem(f"a1_{n}")
        q_all = sb("q_all", [P, G, B * N], F32R)
        k_all = sb("k_all", [P, G, B * N], F32R)
        v_all = sb("v_all", [P, B, VT, D])
        wo_g = sb("wo_g", [P, G, D])
        block_mask = sb("block_mask", [P, P])

        with ExitStack() as st2:
            sb2 = lambda n, s, dt=F32: st2.enter_context(nc.sbuf_tensor(f"a1p_{n}", s, dt))
            ps2 = lambda n, s: st2.enter_context(nc.psum_tensor(f"a1p_{n}_ps", s, F32))
            w = sb2("w", [P, 4, D])
            w_T = sb2("w_T", [P, 4, D])
            w_rep = sb2("w_rep", [P, 2, H1, 4, DH1])
            b_row = sb2("b_row", [1, 2, D])
            b_rep = sb2("b_rep", [1, 2, H1, 4, DH1])
            b_col = sb2("b_col", [P, 2 * G])
            ones = sb2("ones", [1, 4])
            bv_b, bo_b = sb2("bv_b", [P, D]), sb2("bo_b", [P, D])
            part = sb2("part", [P, 4])
            full = [sb2(f"full{i}", [P, 512]) for i in range(2)]
            high = [sb2(f"high{i}", [P, 512], F32R) for i in range(2)]
            pair_sum = sb2("pair_sum", [P, B, GR, D])
            w_ps, b_ps = ps2("w", [P, 512]), ps2("b", [P, 512])
            s_ps = [ps2(f"s{i}", [P, 512]) for i in range(2)]
            v_ps = [ps2(f"v{i}", [P, 512]) for i in range(2)]
            loaded, zeroed = sem("loaded"), sem("zeroed")
            wT_ready, wT_copied, rep_ready, b_ready, b_copied = (sem(n) for n in ("wT_ready", "wT_copied", "rep_ready", "b_ready", "b_copied"))
            proj_ready, full_ready, high_ready, stack_ready = (sem(n) for n in ("proj_ready", "full_ready", "high_ready", "stack_ready"))
            v_ready, v_added, pair_ready, wo_placed = (sem(n) for n in ("v_ready", "v_added", "pair_ready", "wo_placed"))
            sums_ready = sem("sums_ready")
            STEPS = 2 * G * 4

            with nc.Block() as block:
                @block.sync
                def _(sp):
                    for i, m in enumerate((Wq, Wk, Wv, Wo)):
                        sp.dma_start(w[:, i, :], m).then_inc(loaded, 16)
                    row = lambda v: v.rearrange("(o d) -> o d", o=1)
                    sp.dma_start(b_row[:, 0, :], row(bq)).then_inc(loaded, 16)
                    sp.dma_start(b_row[:, 1, :], row(bk)).then_inc(loaded, 16)
                    sp.dma_start(bv_b[:], row(bv).broadcast_to([P, D])).then_inc(loaded, 16)
                    sp.dma_start(bo_b[:], row(bo).broadcast_to([P, D])).then_inc(loaded, 16)
                    sp.dma_start(part[:], consts["part"]).then_inc(loaded, 16)
                    sp.dma_start(block_mask[:], consts["block_mask"]).then_inc(loaded, 16)
                    sp.wait_ge(wT_copied, 1)
                    sp.wait_ge(zeroed, 1)
                    for h in range(H1):
                        sp.dma_start(wo_g[32 * (h % HG):32 * (h % HG) + DH1, h // HG, :], w_T[h * DH1:h * DH1 + DH1, 3, :])\
                            .then_inc(wo_placed, 16)
                    sp.wait_ge(wo_placed, 16 * H1)

                @block.gpsimd
                def _(pool):
                    nc.gpsimd.memset(ones[:], 1.0)
                    nc.gpsimd.memset(wo_g[:], 0.0).then_inc(zeroed, 1)
                    pool.wait_ge(v_added, 4)
                    for b in range(B):
                        pairs = v_all[:, b, 0:TB, :].rearrange("p (g o) d -> p g o d", o=2)
                        ins = nc.gpsimd.tensor_tensor(pair_sum[:, b], pairs[:, :, 0, :], pairs[:, :, 1, :], ALU.add)
                    ins.then_inc(pair_ready, 1)
                    pool.wait_ge(pair_ready, 1)
                    nc.gpsimd.tensor_copy(v_all[:, :, TB + GR - 2, :], pair_sum[:, :, GR - 1, :]).then_inc(sums_ready, 1)
                    for g in reversed(range(GR - 2)):
                        pool.wait_ge(sums_ready, GR - 2 - g)
                        nc.gpsimd.tensor_tensor(v_all[:, :, TB + g, :], v_all[:, :, TB + g + 1, :], pair_sum[:, :, g + 1, :], ALU.add)\
                            .then_inc(sums_ready, 1)

                @block.tensor
                def _(pe):
                    pe.wait_ge(loaded, 160)
                    for i in range(4):
                        ins = nc.tensor.transpose(w_ps[:, i * D:i * D + D], w[:, i, :], core.ident[:])
                    ins.then_inc(wT_ready, 1)
                    pe.wait_ge(rep_ready, 2)
                    pe.wait_ge(zeroed, 1)
                    for i in range(2 * G):
                        ins = nc.tensor.matmul(b_ps[:, 2 * i:2 * i + 1], b_rep[:, i // G, i % G * HG:(i % G + 1) * HG].rearrange("o h r d -> o (h r d)"),
                                               ones[0:1, 0:1], start=True, stop=True)
                    ins.then_inc(b_ready, 1)
                    for k in range(STEPS):
                        i, g, c = k // (4 * G), k // 4 % G, k % 4
                        if k >= 2:
                            pe.wait_ge(full_ready, k - 1)
                        nc.tensor.matmul(s_ps[k % 2][:], w_rep[:, i, g * HG:(g + 1) * HG].rearrange("p h r d -> p (h r d)"),
                                         core.xT[:, c * 512:c * 512 + 512], start=True, stop=True).then_inc(proj_ready, 1)
                        if k % 8 == 7:
                            q = k // 8
                            if q >= 2:
                                pe.wait_ge(v_added, q - 1)
                            for t in range(4 * q, 4 * q + 4):
                                ins = nc.tensor.matmul(v_ps[q % 2][:, t % 4 * D:t % 4 * D + D], core.xT[:, t * P:t * P + P], w_T[:, 2, :],
                                                       start=True, stop=True)
                            ins.then_inc(v_ready, 1)

                @block.scalar
                def _(act):
                    act.wait_ge(wT_ready, 1)
                    nc.scalar.activation(w_T[:].rearrange("p i d -> p (i d)"), w_ps[:], ACT.Copy).then_inc(wT_copied, 1)
                    act.wait_ge(b_copied, 1)
                    for k in range(STEPS):
                        i, g = k // (4 * G), k // 4 % G
                        act.wait_ge(proj_ready, k + 1)
                        if k >= 2:
                            act.wait_ge(stack_ready, k - 1)
                        nc.scalar.activation(full[k % 2][:], s_ps[k % 2][:], ACT.Identity, bias=b_col[:, k // 4:k // 4 + 1],
                                             scale=float(DH1) ** -0.5 if i == 0 else 1.0).then_inc(full_ready, 1)

                @block.vector
                def _(dve):
                    dve.wait_ge(loaded, 160)
                    dve.wait_ge(wT_copied, 1)
                    for i in range(2):
                        heads = w_T[:, i, :].rearrange("p (h o d) -> p h o d", h=H1, o=1).broadcast_to([P, H1, 4, DH1])
                        nc.vector.tensor_copy(w_rep[:, i], heads)
                        bias = b_row[:, i, :].rearrange("p (h o d) -> p h o d", h=H1, o=1).broadcast_to([1, H1, 4, DH1])
                        nc.vector.tensor_copy(b_rep[:, i], bias).then_inc(rep_ready, 1)
                    dve.wait_ge(b_ready, 1)
                    cols = b_ps[:, 0:4 * G].rearrange("p (i o) -> p i o", o=2)[:, :, 0]
                    nc.vector.tensor_scalar(b_col[:, 0:G], cols[:, 0:G], float(DH1) ** -0.5, None, ALU.mult)
                    nc.vector.tensor_copy(b_col[:, G:2 * G], cols[:, G:2 * G]).then_inc(b_copied, 1)
                    nc.vector.tensor_tensor(core.x[:], core.x[:], bo_b[:].rearrange("p (o d) -> p o d", o=1).broadcast_to([P, T, D]), ALU.add)
                    for k in range(STEPS):
                        i, g, c = k // (4 * G), k // 4 % G, k % 4
                        dve.wait_ge(full_ready, k + 1)
                        nc.vector.tensor_scalar(high[k % 2][:], full[k % 2][:], part[:, 2 * i:2 * i + 1], None, ALU.mult).then_inc(high_ready, 1)
                        dve.wait_ge(high_ready, k + 1)
                        nc.vector.scalar_tensor_tensor(out=(q_all, k_all)[i][:, g, c * 512:c * 512 + 512], in0=full[k % 2][:],
                                                       scalar=part[:, 2 * i + 1:2 * i + 2], in1=high[k % 2][:].bitcast(F32),
                                                       op0=ALU.mult, op1=ALU.add).then_inc(stack_ready, 1)
                        if k % 8 == 7:
                            q = k // 8
                            dve.wait_ge(v_ready, q + 1)
                            nc.vector.tensor_tensor(v_all[:, q // 2, q % 2 * 4:q % 2 * 4 + 4, :], v_ps[q % 2][:].rearrange("p (t d) -> p t d", t=4),
                                                    bv_b[:].rearrange("p (o d) -> p o d", o=1).broadcast_to([P, 4, D]), ALU.add).then_inc(v_added, 1)

        q_cur = [sb(f"q_cur{i}", [P, N], F32R) for i in range(2)]
        k_cur = [sb(f"k_cur{i}", [P, N], F32R) for i in range(2)]
        v_cur = [sb(f"v_cur{i}", [P, VT, HG, 32]) for i in range(2)]
        zeros = sb("zeros", [P, 132], F32R)
        probs = [sb(f"probs{i}", [P, N]) for i in range(4)]
        probs_T = [sb(f"probs_T{i}", [P, TB, HG, 256]) for i in range(2)]
        negmax, den = sb("negmax", [P, UNITS]), sb("den", [P, UNITS])
        later = sb("later", [P, UNITS])
        more_keys = sb("more_keys", [P, GR - 1])
        rden = sb("rden", [P, 2 * HG, 32])
        rden_b, attn_T = sb("rden_b", [P, 256]), sb("attn_T", [P, 256])
        ps = lambda n, s: st.enter_context(nc.psum_tensor(f"a1_{n}", s, F32))
        score_ps = [ps(f"score{i}", [P, N]) for i in range(2)]
        tr_ps = [ps(f"tr{i}", [P, 512]) for i in range(2)]
        out_ps, misc_ps = ps("out", [P, 512]), ps("misc", [P, 512])
        cleared, v_copied = sem("cleared"), sem("v_copied")
        operands_loaded = [sem("even_operands_loaded"), sem("odd_operands_loaded")]
        scores_ready, masked, negmax_ready, probs_ready, later_kept = (sem(n) for n in ("scores_ready", "masked", "negmax_ready", "probs_ready", "later_kept"))
        tr_ready = [sem("tr_lo_ready"), sem("tr_hi_ready")]
        tr_copied = [sem("tr_lo_copied"), sem("tr_hi_copied")]
        pv_done, attn_ready, rden_ready, den_whole = sem("pv_done"), sem("attn_ready"), sem("rden_ready"), sem("den_whole")
        misc_ready, misc_free = sem("misc_ready"), sem("misc_free")
        ITEMS = 2 * GR
        ITEM = {2 * HG * g + q: 2 * g + q - 3 for g in range(GR) for q in (3, 4)}
        LAST_ITEM = {3: 0, 4: 1, 2 * HG + 4: 2}
        UG = 2 * HG
        ITERS2 = ITERS // 2

        def unit(s):
            s %= UNITS
            return s // UG, s // HG % 2 + 2 * (s // UG), s % HG

        def tiles(grp):
            return 2 * grp + 2 + (grp < GR - 1)

        def hi_copies(s):
            return 1 + max(0, s - UG)

        def progress(it, par):
            return lambda m, c: it * (2 * m) + (par * m + c)

        LAST = lambda m, c: m * ITERS + c

        with nc.Block() as block:
            @block.sync
            def _(sp):
                def load(col, par):
                    for cur, src in ((q_cur, q_all), (k_cur, k_all)):
                        flat = src[:].bitcast(F32).rearrange("p g n -> p (g n)")
                        sp.dma_start(cur[par][:].bitcast(F32), flat[:, bass.ds(col, N)]).then_inc(operands_loaded[par], 16)

                load(0, 0)
                with sp.Fori(0, ITERS2) as it:
                    for par in range(2):
                        n = it * 2 + par + 1
                        col = sp.snap(n % G * (B * N) + n // G % B * N)
                        sp.wait_ge(scores_ready, it * (2 * UNITS) + par * UNITS)
                        load(col, 1 - par)
                sp.wait_ge(operands_loaded[0], 32 * (ITERS2 + 1))
                sp.wait_ge(operands_loaded[1], 32 * ITERS2)

            @block.gpsimd
            def _(pool):
                nc.gpsimd.memset(probs[3][:], 0.0)
                nc.gpsimd.memset(probs_T[0][:], 0.0)
                nc.gpsimd.memset(probs_T[1][:], 0.0)
                nc.gpsimd.memset(den[:], 1.0)
                nc.gpsimd.memset(rden_b[:], 0.0)
                nc.gpsimd.memset(zeros[:].bitcast(F32), 0.0)
                for grp in range(GR - 1):
                    nc.gpsimd.memset(more_keys[:, grp:grp + 1], float(N - 2 * P * (grp + 1) - 1))
                nc.gpsimd.memset(v_cur[0][:], 0.0)
                nc.gpsimd.memset(v_cur[1][:], 0.0).then_inc(cleared, 1)
                pool.wait_ge(cleared, 1)

                def copy_v(g, b, par):
                    flat = v_all[:].rearrange("p b t d -> p (b t) d")
                    src = flat[:, bass.ds(b * VT, VT), bass.ds(g * HG * DH1, HG * DH1)].rearrange("p t (h d) -> p t h d", h=HG)
                    nc.gpsimd.tensor_copy(v_cur[par][:, :, :, 0:DH1], src).then_inc(v_copied, 1)

                copy_v(0, 0, 0)
                with pool.Fori(0, ITERS2) as it:
                    for par in range(2):
                        at = progress(it, par)
                        n = it * 2 + par + 1
                        next_g, next_b = pool.snap(n % G), pool.snap(n // G % B)
                        for s in range(FIX):
                            grp = unit(s)[0]
                            keys = 2 * P * (grp + 1)
                            pool.wait_ge(probs_ready, at(UNITS, s + 1))
                            shared = probs[s % 4][:, keys:keys + 1]
                            nc.gpsimd.tensor_tensor(later[:, s:s + 1], shared, more_keys[:, grp:grp + 1], ALU.mult).then_inc(later_kept, 1)
                            if s == UG + 2:
                                copy_v(next_g, next_b, 1 - par)

            @block.tensor
            def _(pe):
                def scores(s, par):
                    grp, tile, h = unit(s)
                    keys = 2 * P * (grp + 1)
                    rows = slice(32 * h, 32 * h + 32)
                    runs = [(0, (tile + 1) * P, True), ((tile + 1) * P, keys + (2 if keys < N else 0), False)]
                    for lo, hi, real in runs:
                        while lo < hi:
                            end = min(hi, (lo // 512 + 1) * 512)
                            src = k_cur[par][rows, lo:end] if real else zeros[rows, 0:end - lo]
                            last = nc.tensor.matmul(score_ps[s % 2][:, lo:end], q_cur[par][rows, tile * P:tile * P + P], src, start=True, stop=True)
                            lo = end
                    last.then_inc(scores_ready, 1)

                def slot(s, par, at, item, last=False):
                    if not last or s == 0:
                        pe.wait_ge(probs_ready, at(UNITS, s))
                    if not last:
                        if s == UNITS - 1:
                            pe.wait_ge(operands_loaded[1 - par], it * 32 + 32 * (par + 1))
                            scores(0, 1 - par)
                        else:
                            scores(s + 1, par)
                    if not last or s == 0:
                        grp, tile, h = unit(s - 1)
                        n = tiles(grp)
                        pe.wait_ge(tr_copied[0], at(UNITS, s))
                        if n > 4:
                            pe.wait_ge(tr_copied[1], at(FIX, hi_copies(s - 1) if s else 0))
                        for k in range(n):
                            src = probs[(s - 1) % 4][:, k * P:k * P + P] if k < 2 * grp + 2 else \
                                probs[(s - 1) % 4][:, k * P:k * P + 1].broadcast_to([P, P])
                            ins = nc.tensor.transpose(tr_ps[k // 4][:, k % 4 * P:k % 4 * P + P], src, core.ident[:])
                            if k == 3 or (k == n - 1 and n < 4):
                                ins.then_inc(tr_ready[0], 1)
                            elif k == n - 1:
                                ins.then_inc(tr_ready[1], 1)
                    if s in item:
                        pe.wait_ge(misc_free, at(ITEMS, item[s]))
                        for q in range(2):
                            cols = slice(q * P, q * P + P)
                            if s % UG == 3:
                                if q == 0:
                                    pe.wait_ge(rden_ready, at(GR, s // UG + 1))
                                ins = nc.tensor.transpose(misc_ps[:, cols], rden[:, q * HG:(q + 1) * HG, :].rearrange("p h d -> p (h d)"), core.ident[:])
                            else:
                                if q == 0:
                                    pe.wait_ge(attn_ready, at(GR, s // UG + 1))
                                ins = nc.tensor.matmul(misc_ps[:, cols], attn_T[:, cols], wo_g[:].rearrange("p g d -> p (g d)")[:, wo_cols(s)], start=True, stop=True)
                        ins.then_inc(misc_ready, 1)
                    if not last or s < UG + 1:
                        grp, r = (s - UG - 1) // UG % GR, (s - 1) % UG
                        if r == 0:
                            pe.wait_ge(tr_copied[0], at(UNITS, s))
                            if tiles(grp) > 4:
                                pe.wait_ge(tr_copied[1], at(FIX, hi_copies(s - 1)))
                            pe.wait_ge(attn_ready, at(GR, s // UG + 1))
                            if s == UG + 1:
                                pe.wait_ge(v_copied, at(1, 1))
                        if r < tiles(grp):
                            for h in range(HG):
                                tile = r if r < 2 * grp + 2 else TB + grp
                                ins = nc.tensor.matmul(out_ps[32 * h:32 * h + 32, 0:256], v_cur[par if s > UG else 1 - par][:, tile, h, :],
                                                       probs_T[grp % 2][:, r, h, :], start=r == 0, stop=r == tiles(grp) - 1)
                            if r == tiles(grp) - 1:
                                ins.then_inc(pv_done, 1)

                pe.wait_ge(cleared, 1)
                for h in range(HG):
                    ins = nc.tensor.matmul(out_ps[32 * h:32 * h + 32, 0:256], v_cur[1][:, 0, h, :], probs_T[0][:, 0, h, :], start=True, stop=True)
                ins.then_inc(pv_done, 1)
                pe.wait_ge(operands_loaded[0], 32)
                scores(0, 0)
                with pe.Fori(0, ITERS2) as it:
                    for par in range(2):
                        n = it * 2 + par
                        wo_cols = lambda s, n=n: bass.ds((n % G if s > 2 * UG else (n + G - 1) % G) * D, D)
                        for s in range(UNITS):
                            slot(s, par, progress(it, par), ITEM)
                wo_cols = lambda s: slice((G - 1) * D, G * D)
                for s in range(2 * UG):
                    slot(s, 0, LAST, LAST_ITEM, last=True)

            @block.scalar
            def _(act):
                def slot(s, at, item, last=False):
                    if not last:
                        grp, tile, h = unit(s)
                        keys = 2 * P * (grp + 1)
                        n = keys + (keys < N)
                        act.wait_ge(negmax_ready, at(UNITS, s + 1))
                        act.wait_ge(later_kept, at(FIX, min(max(s - 3, 0), FIX)))
                        nc.scalar.activation(probs[s % 4][:, 0:n], score_ps[s % 2][:, 0:n], ACT.Exp, bias=negmax[:, s:s + 1],
                                             accum_out=den[:, s:s + 1]).then_inc(probs_ready, 1)
                    if not last or s == 0:
                        grp, tile, h = unit(s - 1)
                        n = min(4, tiles(grp))
                        act.wait_ge(tr_ready[0], at(UNITS, s + 1))
                        nc.scalar.activation(probs_T[grp % 2][:, 0:n, h, tile % 2 * P:tile % 2 * P + P],
                                             tr_ps[0][:, 0:n * P].rearrange("p (k q) -> p k q", k=n), ACT.Copy).then_inc(tr_copied[0], 1)
                    if s in item and s % UG == 3:
                        act.wait_ge(misc_ready, at(ITEMS, item[s] + 1))
                        nc.scalar.activation(rden_b[:], misc_ps[:, 0:256], ACT.Copy).then_inc(misc_free, 1)

                act.wait_ge(cleared, 1)
                with act.Fori(0, ITERS2) as it:
                    for par in range(2):
                        for s in range(UNITS):
                            slot(s, progress(it, par), ITEM)
                for s in range(2 * UG):
                    slot(s, LAST, LAST_ITEM, last=True)

            @block.vector
            def _(dve):
                def row_max(s, at):
                    grp, tile, h = unit(s)
                    keys = 2 * P * (grp + 1)
                    n = keys + (keys < N)
                    own = score_ps[s % 2][:, tile * P:tile * P + P]
                    nc.vector.tensor_tensor(own, own, block_mask[:], ALU.mult).then_inc(masked, 1)
                    dve.wait_ge(masked, at(UNITS, s + 1))
                    c = s % UNITS
                    nc.vector.tensor_reduce(negmax[:, c:c + 1], score_ps[s % 2][:, 0:n], axis=AX.X, op=ALU.max, negate=True).then_inc(negmax_ready, 1)

                def slot(s, at, batch, item, last=False):
                    if not last:
                        dve.wait_ge(scores_ready, at(UNITS, s + 2))
                        row_max(s + 1, at)
                    if s % UG == 1 and (not last or s == 1):
                        dve.wait_ge(probs_ready, at(UNITS, s if not last else 0))
                        dve.wait_ge(later_kept, at(FIX, s - 1))
                        c = (s - UG - 1) % UNITS
                        if c < FIX:
                            nc.vector.tensor_tensor(den[:, c:c + UG], den[:, c:c + UG], later[:, c:c + UG], ALU.add).then_inc(den_whole, 1)
                            dve.wait_ge(den_whole, at(GR - 1, c // UG + 1))
                        nc.vector.reciprocal(rden[:], spread(den[:, c:c + UG], [P, UG, 32])).then_inc(rden_ready, 1)
                    if s % UG == 1:
                        dve.wait_ge(pv_done, at(GR, s // UG + 1))
                        dve.wait_ge(misc_free, at(ITEMS, 2 * (s // UG) - 1 if s > 1 or last else 0))
                        nc.vector.tensor_tensor(attn_T[:], out_ps[:, 0:256], rden_b[:], ALU.mult).then_inc(attn_ready, 1)
                    if not last or s == 0:
                        grp, tile, h = unit(s - 1)
                        n = tiles(grp) - 4
                        if n > 0:
                            dve.wait_ge(tr_ready[1], at(FIX, hi_copies(s - 1) + 1 if s else 1))
                            nc.vector.tensor_copy(probs_T[grp % 2][:, 4:4 + n, h, tile % 2 * P:tile % 2 * P + P],
                                                  tr_ps[1][:, 0:n * P].rearrange("p (k q) -> p k q", k=n)).then_inc(tr_copied[1], 1)
                    if s in item and s % UG == 4:
                        dve.wait_ge(misc_ready, at(ITEMS, item[s] + 1))
                        rows = core.x[:, bass.ds(batch[s > 2 * UG] * TB + 2 * ((s // UG + 2) % GR), 2), :]
                        nc.vector.tensor_tensor(rows, misc_ps[:, 0:256].rearrange("p (t d) -> p t d", t=2), rows, ALU.add).then_inc(misc_free, 1)

                dve.wait_ge(cleared, 1)
                dve.wait_ge(scores_ready, 1)
                row_max(0, lambda m, c: c)
                with dve.Fori(0, ITERS2) as it:
                    for par in range(2):
                        n = it * 2 + par
                        batch = ((n + ITERS - 1) // G % B, n // G % B)
                        for s in range(UNITS):
                            slot(s, progress(it, par), batch, ITEM)
                for s in range(2 * UG):
                    slot(s, LAST, (B - 1, 0), LAST_ITEM, last=True)


def channel_mix(nc, core, W_r, W_k, W_v, mu_r, mu_k, out):
    with ExitStack() as st:
        sb = lambda n, s: st.enter_context(nc.sbuf_tensor(f"f1_{n}", s, F32))
        ps = lambda n: st.enter_context(nc.psum_tensor(f"f1_{n}", [P, 512], F32))
        sem = lambda n: core.sem(f"f1_{n}")
        G = B * N // 512
        w_rows = sb("w_rows", [P, 3, D])
        w = sb("w", [P, 3, D])
        mu = sb("mu", [P, 2])
        rest = sb("rest", [P, 2])
        mixed = [sb("xr", [P, B, N]), sb("xk", [P, B, N])]
        k_relu = [sb(f"k_relu{i}", [P, 512]) for i in range(2)]
        k_sq = [sb(f"k_sq{i}", [P, 512]) for i in range(2)]
        gate = [sb(f"gate{i}", [P, 512]) for i in range(2)]
        prod = [sb(f"prod{i}", [P, 512]) for i in range(2)]
        k_ps, r_ps, v_ps = ([ps(f"{n}{i}") for i in range(2)] for n in "krv")
        w_ps = ps("wT")
        wT_ready, wT_copied = sem("wT_ready"), sem("wT_copied")
        loaded, rest_ready, scaled, mixed_ready = sem("loaded"), sem("rest_ready"), sem("scaled"), sem("mixed_ready")
        k_ready, r_ready, v_ready = sem("k_ready"), sem("r_ready"), sem("v_ready")
        relu_done, gate_done, sq_done, prod_done, x_done, stored = (sem(n) for n in ("relu_done", "gate_done", "sq_done", "prod_done", "x_done", "stored"))
        with nc.Block() as block:
            @block.sync
            def _(sp):
                for i, m in enumerate((W_r, W_k, W_v)):
                    sp.dma_start(w_rows[:, i, :], m).then_inc(loaded, 16)
                for i, m in enumerate((mu_r, mu_k)):
                    sp.dma_start(mu[:, i:i + 1], m.rearrange("(d o) -> d o", o=1)).then_inc(loaded, 16)
                rows = out.rearrange("b (t p) d -> p (b t) d", p=P)
                for g in range(G):
                    sp.wait_ge(x_done, g + 1)
                    sp.dma_start(rows[:, 4 * g:4 * g + 4, :], core.x[:, 4 * g:4 * g + 4, :]).then_inc(stored, 16)
                sp.wait_ge(stored, 16 * G)

            @block.tensor
            def _(pe):
                pe.wait_ge(loaded, 80)
                for i in range(3):
                    ins = nc.tensor.transpose(w_ps[:, i * D:i * D + D], w_rows[:, i, :], core.ident[:])
                ins.then_inc(wT_ready, 1)
                pe.wait_ge(wT_copied, 1)
                pe.wait_ge(mixed_ready, 2)
                flat = [m[:].rearrange("p b n -> p (b n)") for m in mixed]
                for g in range(G + 1):
                    if g < G:
                        if g >= 2:
                            pe.wait_ge(relu_done, g - 1)
                            pe.wait_ge(gate_done, g - 1)
                        nc.tensor.matmul(k_ps[g % 2][:], w[:, 1, :], flat[1][:, g * 512:g * 512 + 512], start=True, stop=True).then_inc(k_ready, 1)
                        for t in range(4):
                            ins = nc.tensor.matmul(r_ps[g % 2][:, t * P:t * P + P], flat[0][:, (4 * g + t) * P:(4 * g + t + 1) * P], w[:, 0, :],
                                                   start=True, stop=True)
                        ins.then_inc(r_ready, 1)
                    if g:
                        pe.wait_ge(sq_done, g)
                        if g >= 3:
                            pe.wait_ge(prod_done, g - 2)
                        for t in range(4):
                            ins = nc.tensor.matmul(v_ps[(g - 1) % 2][:, t * P:t * P + P], k_sq[(g - 1) % 2][:, t * P:t * P + P], w[:, 2, :],
                                                   start=True, stop=True)
                        ins.then_inc(v_ready, 1)

            @block.scalar
            def _(act):
                act.wait_ge(wT_ready, 1)
                nc.scalar.activation(w[:].rearrange("p i d -> p (i d)"), w_ps[:, 0:3 * D], ACT.Copy).then_inc(wT_copied, 1)
                for g in range(G):
                    act.wait_ge(k_ready, g + 1)
                    if g >= 2:
                        act.wait_ge(sq_done, g - 1)
                    nc.scalar.activation(k_relu[g % 2][:], k_ps[g % 2][:], ACT.Relu).then_inc(relu_done, 1)
                    act.wait_ge(r_ready, g + 1)
                    if g >= 2:
                        act.wait_ge(prod_done, g - 1)
                    nc.scalar.activation(gate[g % 2][:], r_ps[g % 2][:], ACT.Sigmoid).then_inc(gate_done, 1)

            @block.vector
            def _(dve):
                dve.wait_ge(loaded, 80)
                nc.vector.tensor_scalar(rest[:], mu[:], -1.0, 1.0, ALU.mult, ALU.add).then_inc(rest_ready, 1)
                dve.wait_ge(rest_ready, 1)
                xT = core.xT[:].rearrange("p (b n) -> p b n", b=B)
                for i in (1, 0):
                    nc.vector.tensor_scalar(mixed[i][:], xT, mu[:, i:i + 1], None, ALU.mult).then_inc(scaled, 1)
                for i in (1, 0):
                    dve.wait_ge(scaled, 2 - i)
                    nc.vector.scalar_tensor_tensor(out=mixed[i][:, :, 1:N], in0=xT[:, :, 0:N - 1], scalar=rest[:, i:i + 1],
                                                   in1=mixed[i][:, :, 1:N], op0=ALU.mult, op1=ALU.add).then_inc(mixed_ready, 1)
                for g in range(G + 1):
                    if g < G:
                        dve.wait_ge(relu_done, g + 1)
                        if g >= 2:
                            dve.wait_ge(v_ready, g - 1)
                        nc.vector.tensor_tensor(k_sq[g % 2][:], k_relu[g % 2][:], k_relu[g % 2][:], ALU.mult).then_inc(sq_done, 1)
                    if g:
                        dve.wait_ge(v_ready, g)
                        dve.wait_ge(gate_done, g)
                        p = prod[(g - 1) % 2]
                        nc.vector.tensor_tensor(p[:], v_ps[(g - 1) % 2][:], gate[(g - 1) % 2][:], ALU.mult).then_inc(prod_done, 1)
                        dve.wait_ge(prod_done, g)
                        rows = core.x[:, 4 * (g - 1):4 * g, :]
                        nc.vector.tensor_tensor(rows, rows, p[:].rearrange("p (t d) -> p t d", t=4), ALU.add).then_inc(x_done, 1)


def build(nc, a, c, out):
    with ExitStack() as stack:
        core = Core(nc, stack)
        normalize(nc, core, "n0", first_load=a["L0_attn_x"], affine=(a["L0_attn_ln_gamma"], a["L0_attn_ln_beta"]), twice=True)
        rotary_attention(nc, core, c["rope"], a["L0_attn_w_qkv"], a["L0_attn_w_out"])
        normalize(nc, core, "n1")
        experts(nc, core, *(a[f"L0_ffn_{n}"] for n in ("switch_w", "switch_b", "w1", "b1", "w2", "b2")))
        normalize(nc, core, "n2")
        block_attention(nc, core, c, *(a[f"L1_attn_{n}"] for n in ("Wq", "bq", "Wk", "bk", "Wv", "bv", "Wo", "bo")))
        normalize(nc, core, "n3")
        channel_mix(nc, core, *(a[f"L1_ffn_{n}"] for n in ("W_r", "W_k", "W_v", "mu_r", "mu_k")), out)


def rope_tables():
    inv = (1.0 / np.float32(10000.0) ** (np.arange(0, DH0, 2, dtype=np.float32) / np.float32(DH0))).astype(np.float32)
    pos = np.maximum(np.arange(N) - 1, 0).astype(np.float32)
    ang = (pos[None, :] * inv[:, None]).astype(np.float32)
    cos, sin = np.tile(np.cos(ang), (4, 1)), np.tile(np.concatenate([-np.sin(ang), np.sin(ang)]), (2, 1))
    s = np.float32(DH0 ** -0.5)
    return np.stack([cos * s, sin * s, cos, sin]).astype(np.float32)


def part_signs():
    low = np.tile(np.repeat(np.array([[0, 0, 1, 1], [0, 1, 0, 1]]), DH1, axis=1), (1, HG))
    return np.stack([1 - 2 * low[0], low[0], 1 - 2 * low[1], low[1]], axis=1).astype(np.float32)


def block_mask():
    blk = np.arange(P) // WIN
    return (blk[:, None] >= blk[None, :]).astype(np.float32)


_INS = ['L0_attn_x', 'L0_attn_ln_gamma', 'L0_attn_ln_beta', 'L0_attn_w_qkv', 'L0_attn_w_out', 'L0_ffn_switch_w', 'L0_ffn_switch_b',
        'L0_ffn_w1', 'L0_ffn_b1', 'L0_ffn_w2', 'L0_ffn_b2', 'L1_attn_Wq', 'L1_attn_bq', 'L1_attn_Wk', 'L1_attn_bk', 'L1_attn_Wv',
        'L1_attn_bv', 'L1_attn_Wo', 'L1_attn_bo', 'L1_ffn_W_r', 'L1_ffn_W_k', 'L1_ffn_W_v', 'L1_ffn_mu_r', 'L1_ffn_mu_k']


def kernel(**inputs):
    import concourse.bacc as _bacc
    from concourse.bass_utils import run_bass_kernel_spmd as _run

    nc = _bacc.Bacc("TRN2", target_bir_lowering=False, num_devices=1)
    arrays, a, c = {}, {}, {}
    for name in _INS:
        arrays[f"in_{name}"] = np.ascontiguousarray(inputs[name])
        a[name] = nc.dram_tensor(f"in_{name}", arrays[f"in_{name}"].shape, F32, kind="ExternalInput").ap()
    for name, value in (("rope", rope_tables()), ("part", part_signs()), ("block_mask", block_mask())):
        arrays[f"const_{name}"] = value
        c[name] = nc.dram_tensor(f"const_{name}", value.shape, F32, kind="ExternalInput").ap()
    out = nc.dram_tensor("out", (B, N, D), F32, kind="ExternalOutput").ap()
    build(nc, a, c, out)
    return _run(nc, [arrays], core_ids=[0]).results[0]["out"]
```

```python
from contextlib import ExitStack

import numpy as np

import concourse.bass as bass
from concourse import mybir

P = 128
B, N, D = 2, 1024, 128
T = B * N // P
TB = N // P
H0, DH0 = 16, 64
PAIRS = B * H0 // 2
HP = H0 // 2
SLOTS = 2 * TB
E, F = 8, 512
FC = F // P
H1, DH1, WIN = 16, 8, 32
HG = 4
EPS = 1e-5

ALU = mybir.AluOpType
ACT = mybir.ActivationFunctionType
AX = mybir.AxisListType
F32 = mybir.dt.float32
F32R = mybir.dt.float32r


def spread(ap, shape):
    return ap.rearrange("p (n o) -> p n o", o=1).broadcast_to(shape)


class Core:

    def __init__(self, nc, stack):
        self.nc, self.stack = nc, stack
        self.x = self.sb("residual", [P, T, D], F32)
        self.xT = self.sb("normed_T", [P, B * N], F32)
        self.ident = self.sb("ident", [P, P], F32)

    def sb(self, name, shape, dt):
        return self.stack.enter_context(self.nc.sbuf_tensor(name, shape, dt))

    def sem(self, name):
        return self.stack.enter_context(self.nc.semaphore(name))


def normalize(nc, core, tag, first_load=None, affine=None):
    LOADS = 4
    rounds = 2 if affine else 1
    with ExitStack() as st:
        sb = lambda n, s: st.enter_context(nc.sbuf_tensor(f"{tag}_{n}", s, F32))
        xn = sb("xn", [P, T, D])
        stats = sb("stats", [P, T, 6])
        moments = sb("moments", [P, T, 2])
        var, root, rstd, newton = (sb(n, [P, T]) for n in ("var", "root", "rstd", "newton"))
        gb = sb("gamma_beta", [P, 2])
        tp = [st.enter_context(nc.psum_tensor(f"{tag}_tp{i}", [P, 512], F32)) for i in range(4)]
        x_loaded = [core.sem(f"{tag}_x_loaded{i}") for i in range(LOADS)]
        affine_loaded = core.sem(f"{tag}_affine_loaded")
        dve_step = core.sem(f"{tag}_dve_step")
        var_ready = core.sem(f"{tag}_var_ready")
        root_ready = core.sem(f"{tag}_root_ready")
        xn_ready = core.sem(f"{tag}_xn_ready")
        ident_ready = core.sem(f"{tag}_ident_ready")
        xnT_ready = core.sem(f"{tag}_xnT_ready")
        copied = core.sem(f"{tag}_copied")
        TL = T // LOADS

        with nc.Block() as block:
            if first_load is not None:
                @block.sync
                def _(sp):
                    rows = first_load.rearrange("b (t p) d -> p (b t) d", p=P)
                    for i in range(LOADS):
                        sp.dma_start(core.x[:, i * TL:(i + 1) * TL, :], rows[:, i * TL:(i + 1) * TL, :]).then_inc(x_loaded[i], 16)
                    for i, v in enumerate(affine):
                        sp.dma_start(gb[:, i:i + 1], v.rearrange("(d o) -> d o", o=1)).then_inc(affine_loaded, 16)

                @block.gpsimd
                def _(pool):
                    nc.gpsimd.memset(core.ident[:], 0.0).then_inc(ident_ready, 1)
                    pool.wait_ge(ident_ready, 1)
                    nc.gpsimd.affine_select(out=core.ident[:], in_=core.ident[:], compare_op=ALU.not_equal, fill=1.0,
                                            base=0, pattern=[[-1, P]], channel_multiplier=1).then_inc(ident_ready, 1)

            @block.vector
            def _(dve):
                steps = [0]

                def step(ins):
                    steps[0] += 1
                    ins.then_inc(dve_step, 1)
                    dve.wait_ge(dve_step, steps[0])

                for k in range(rounds):
                    src = (core.x, xn)[k]
                    for t in range(T):
                        if first_load is not None and k == 0 and t % TL == 0:
                            dve.wait_ge(x_loaded[t // TL], 16)
                        ins = nc.vector.bn_stats(out=stats[:, t, :], in_=src[:, t, :])
                    step(ins)
                    for t in range(T):
                        ins = nc.vector.bn_aggr(out=moments[:, t, :], in_=stats[:, t, :])
                    step(ins)
                    nc.vector.tensor_scalar(var[:], moments[:, :, 1], EPS, None, ALU.add).then_inc(var_ready, 1)
                    dve.wait_ge(root_ready, k + 1)
                    step(nc.vector.reciprocal(rstd[:], root[:]))
                    step(nc.vector.tensor_tensor(newton[:], rstd[:], rstd[:], ALU.mult))
                    step(nc.vector.tensor_tensor(newton[:], newton[:], var[:], ALU.mult))
                    step(nc.vector.tensor_scalar(newton[:], newton[:], -0.5, 1.5, ALU.mult, ALU.add))
                    step(nc.vector.tensor_tensor(rstd[:], rstd[:], newton[:], ALU.mult))
                    for t in range(T):
                        ins = nc.vector.tensor_scalar(xn[:, t, :], src[:, t, :], moments[:, t, 0:1], rstd[:, t:t + 1], ALU.subtract, ALU.mult)
                        if k == rounds - 1 and t % 4 == 3:
                            ins.then_inc(xn_ready, 1)
                    if k < rounds - 1:
                        step(ins)

            @block.tensor
            def _(pe):
                if first_load is not None:
                    pe.wait_ge(ident_ready, 2)
                for t in range(T):
                    if t % 4 == 0:
                        pe.wait_ge(xn_ready, t // 4 + 1)
                    ins = nc.tensor.transpose(tp[t // 4][:, t % 4 * P:(t % 4 + 1) * P], xn[:, t, :], core.ident[:])
                    if t % 4 == 3:
                        ins.then_inc(xnT_ready, 1)

            @block.scalar
            def _(act):
                for k in range(rounds):
                    act.wait_ge(var_ready, k + 1)
                    nc.scalar.activation(root[:], var[:], ACT.Sqrt).then_inc(root_ready, 1)
                if affine:
                    act.wait_ge(affine_loaded, 32)
                for i in range(T // 4):
                    act.wait_ge(xnT_ready, i + 1)
                    dst = core.xT[:, i * 512:(i + 1) * 512]
                    if affine:
                        nc.scalar.activation(dst, tp[i][:], ACT.Identity, bias=gb[:, 1:2], scale=gb[:, 0:1]).then_inc(copied, 1)
                    else:
                        nc.scalar.activation(dst, tp[i][:], ACT.Copy).then_inc(copied, 1)


def rotary_attention(nc, core, rope, w_qkv, w_out):
    with ExitStack() as st:
        sb = lambda n, s, dt=F32: st.enter_context(nc.sbuf_tensor(f"a0_{n}", s, dt))
        ps = lambda n, s: st.enter_context(nc.psum_tensor(f"a0_{n}", s, F32))
        sem = lambda n: core.sem(f"a0_{n}")

        tables = sb("tables", [P, 4, N])
        xn_cur = sb("xn_cur", [P, N])
        w_cur = sb("w_cur", [P, 3, P])
        wo_cur = sb("wo_cur", [P, D])
        raw = [sb("q_raw", [P, N]), sb("k_raw", [P, N])]
        rot = [sb("q_rot", [P, N]), sb("k_rot", [P, N])]
        hi = [sb("q_hi", [P, N], F32R), sb("k_hi", [P, N], F32R)]
        lo = [sb("q_lo", [P, N], F32R), sb("k_lo", [P, N], F32R)]
        q_stack = [[sb(f"q_stack{i}{h}", [P, N], F32R) for h in "ab"] for i in range(2)]
        k_stack = [[[sb(f"k_stack{i}{h}{part}", [P, N], F32R) for part in ("h", "l")] for h in "ab"] for i in range(2)]
        v = [sb(f"v{i}", [P, TB, P]) for i in range(2)]
        probs = [sb(f"probs{i}", [P, N]) for i in range(4)]
        probs_T = [sb(f"probs_T{i}", [P, 2, TB, 256]) for i in range(2)]
        negmax = sb("negmax", [P, SLOTS])
        den = sb("den", [P, SLOTS])
        rden_col = sb("rden_col", [P, 4])
        rden = sb("rden", [P, 4, 64])
        ones = sb("ones", [P, 4, 64])
        rden_b = sb("rden_b", [P, 256])
        attn_T = sb("attn_T", [P, 256])

        score_ps = [ps(f"score{i}", [P, N]) for i in range(2)]
        tr_ps = [ps(f"tr{i}", [P, 512]) for i in range(2)]
        out_ps = ps("out", [P, 512])
        misc_ps = ps("misc", [P, 512])

        tables_loaded, zeroed = sem("tables_loaded"), sem("zeroed")
        operands_loaded, wo_loaded = sem("operands_loaded"), sem("wo_loaded")
        swapped = [sem("q_swapped"), sem("k_swapped")]
        rotated = [sem("q_rotated"), sem("k_rotated")]
        summed = [sem("q_summed"), sem("k_summed")]
        hi_ready = [sem("q_hi_ready"), sem("k_hi_ready")]
        lo_ready = [sem("q_lo_ready"), sem("k_lo_ready")]
        stacked = [sem("q_stacked"), sem("k_stacked")]
        STACKED = [64, 128]
        scores_ready, negmax_ready, probs_ready = sem("scores_ready"), sem("negmax_ready"), sem("probs_ready")
        tr_ready = [sem("tr_lo_ready"), sem("tr_hi_ready")]
        tr_copied = [sem("tr_lo_copied"), sem("tr_hi_copied")]
        misc_ready, misc_free = sem("misc_ready"), sem("misc_free")
        pv_done, attn_ready, rden_ready, rden_col_ready = (sem(n) for n in ("pv_done", "attn_ready", "rden_ready", "rden_col_ready"))

        ITEM_SLOTS = [0, 1, 2, 3, 4, 5, 6, 7, 8, 9, 10, 11, 14, 15]
        ITEMS, FIRST_ITEMS = len(ITEM_SLOTS), 6
        ITEM = {s: FIRST_ITEMS + i for i, s in enumerate(ITEM_SLOTS)}
        LAST_ITEM = {2: FIRST_ITEMS, 3: FIRST_ITEMS + 1, 7: FIRST_ITEMS + 2}
        PAIRS2 = PAIRS // 2

        def unit(s):
            return 2 * (s // 4) + s % 4 // 2, s % 2

        def progress(it, par):
            return lambda m, c: it * (2 * m) + (par * m + c)

        LAST = lambda m, c: m * PAIRS + c
        BEFORE = lambda m, c: -m + c

        with nc.Block() as block:
            @block.sync
            def _(sp):
                def load_operands(col, row):
                    sp.dma_start(w_cur[:], w_qkv.rearrange("d (c n) -> d c n", c=3)[:, :, bass.ds(col, P)])\
                        .then_inc(operands_loaded, 16)
                    sp.dma_start(xn_cur[:], core.xT[:, bass.ds(row, N)]).then_inc(operands_loaded, 16)

                def swap_halves(i):
                    for r in range(4):
                        sp.dma_start(rot[i][32 * r:32 * r + 32, :], raw[i][32 * (r ^ 1):32 * (r ^ 1) + 32, :])\
                            .then_inc(swapped[i], 16)

                def stack_q(par):
                    for h in range(2):
                        rows = slice(64 * h, 64 * h + 64)
                        sp.dma_start(q_stack[par][h][0:64, :].bitcast(F32), hi[0][rows, :].bitcast(F32)).then_inc(stacked[0], 16)
                        sp.dma_start(q_stack[par][h][64:128, :].bitcast(F32), lo[0][rows, :].bitcast(F32)).then_inc(stacked[0], 16)

                def stack_k(par):
                    for h in range(2):
                        rows = slice(64 * h, 64 * h + 64)
                        for part, src in enumerate((hi[1], lo[1])):
                            for half in range(2):
                                sp.dma_start(k_stack[par][h][part][64 * half:64 * half + 64, :].bitcast(F32), src[rows, :].bitcast(F32))\
                                    .then_inc(stacked[1], 16)

                load_operands(0, 0)
                sp.dma_start(tables[:], rope.rearrange("t p n -> p t n")).then_inc(tables_loaded, 16)
                sp.wait_ge(misc_free, 2)
                swap_halves(0)
                sp.wait_ge(misc_free, 4)
                swap_halves(1)
                sp.wait_ge(misc_ready, FIRST_ITEMS)
                load_operands(P, 0)
                sp.wait_ge(lo_ready[0], 1)
                stack_q(0)
                sp.wait_ge(lo_ready[1], 1)
                stack_k(0)
                with sp.Fori(0, PAIRS2) as it:
                    for par in range(2):
                        at = progress(it, par)
                        wo_row = sp.snap(((it * 2 + par) % HP) * P)
                        next_col = sp.snap((it * 2 + par + 2) % HP * P)
                        next_row = sp.snap((it * 2 + par + 2) // HP % B * N)
                        for i, slot in ((0, 1), (1, 5)):
                            sp.wait_ge(misc_free, at(ITEMS, ITEM[slot] + 1))
                            sp.wait_ge(summed[i], at(1, 1))
                            swap_halves(i)
                        sp.wait_ge(lo_ready[0], at(1, 2))
                        stack_q(1 - par)
                        sp.wait_ge(misc_ready, at(ITEMS, ITEM[7] + 1))
                        sp.dma_start(wo_cur[:], w_out[bass.ds(wo_row, P), :]).then_inc(wo_loaded, 16)
                        sp.wait_ge(misc_ready, at(ITEMS, ITEM[9] + 1))
                        load_operands(next_col, next_row)
                        sp.wait_ge(lo_ready[1], at(1, 2))
                        stack_k(1 - par)
                sp.wait_ge(operands_loaded, 32 * (PAIRS + 2))
                sp.wait_ge(stacked[0], STACKED[0] * (PAIRS + 1))
                sp.wait_ge(stacked[1], STACKED[1] * (PAIRS + 1))

            @block.gpsimd
            def _(pool):
                nc.gpsimd.memset(probs[3][:], 0.0)
                nc.gpsimd.memset(probs_T[0][:], 0.0)
                nc.gpsimd.memset(probs_T[1][:], 0.0)
                nc.gpsimd.memset(v[1][:], 0.0)
                nc.gpsimd.memset(den[:], 1.0)
                nc.gpsimd.memset(rden_b[:], 0.0)
                nc.gpsimd.memset(ones[:], 1.0)
                nc.gpsimd.memset(wo_cur[:], 0.0).then_inc(zeroed, 1)
                pool.wait_ge(zeroed, 1)

                def spread_rden(at, grp):
                    pool.wait_ge(rden_col_ready, at(4, grp + 1))
                    nc.gpsimd.tensor_tensor(rden[:], spread(rden_col[:], [P, 4, 64]), ones[:], ALU.mult).then_inc(rden_ready, 1)

                def sums_and_rests(at, parts=(0, 1)):
                    for i in parts:
                        pool.wait_ge(rotated[i], at(2, 4))
                        nc.gpsimd.tensor_tensor(raw[i][:], raw[i][:], rot[i][:], ALU.add).then_inc(summed[i], 1)
                        pool.wait_ge(hi_ready[i], at(1, 2))
                        nc.gpsimd.tensor_tensor(lo[i][:], raw[i][:], hi[i][:].bitcast(F32), ALU.subtract)\
                            .then_inc(lo_ready[i], 1)

                sums_and_rests(BEFORE)
                with pool.Fori(0, PAIRS2) as it:
                    for par in range(2):
                        at = progress(it, par)
                        spread_rden(at, 0)
                        spread_rden(at, 1)
                        sums_and_rests(at, (0,))
                        spread_rden(at, 2)
                        sums_and_rests(at, (1,))
                        spread_rden(at, 3)
                spread_rden(LAST, 0)

            @block.tensor
            def _(pe):
                def project_T(i, half):
                    nc.tensor.matmul(misc_ps[:], w_cur[:, i, :], xn_cur[:, half * 512:half * 512 + 512],
                                     start=True, stop=True).then_inc(misc_ready, 1)

                def project_v(half):
                    for t in range(4):
                        last = nc.tensor.matmul(misc_ps[:, t * P:t * P + P], xn_cur[:, (4 * half + t) * P:(4 * half + t + 1) * P],
                                                w_cur[:, 2, :], start=True, stop=True)
                    last.then_inc(misc_ready, 1)

                def scores(s, par):
                    tile, h = unit(s)
                    for half in range(2):
                        cols = slice(half * 512, half * 512 + 512)
                        for part in range(2):
                            last = nc.tensor.matmul(score_ps[s % 2][:, cols], q_stack[par][h][:, tile * P:tile * P + P],
                                                    k_stack[par][h][part][:, cols], start=part == 0, stop=part == 1)
                    last.then_inc(scores_ready, 1)

                def transposes(s):
                    for k in range(TB):
                        last = nc.tensor.transpose(tr_ps[k // 4][:, k % 4 * P:k % 4 * P + P],
                                                   probs[s % 4][:, k * P:k * P + P], core.ident[:])
                        if k % 4 == 3:
                            last.then_inc(tr_ready[k // 4], 1)

                def slot(s, par, at, item, last=False):
                    if not last or s == 0:
                        pe.wait_ge(probs_ready, at(SLOTS, s))
                    if not last:
                        if s == SLOTS - 1:
                            for i in range(2):
                                pe.wait_ge(stacked[i], at(STACKED[i], 2 * STACKED[i]))
                            scores(0, 1 - par)
                        else:
                            scores(s + 1, par)
                    if not last or s == 0:
                        for i in range(2):
                            pe.wait_ge(tr_copied[i], at(SLOTS, s))
                        transposes(s - 1)
                    if s in item:
                        pe.wait_ge(misc_free, at(ITEMS, item[s]))
                        if s in (0, 1, 4, 5):
                            if s == 0:
                                pe.wait_ge(operands_loaded, at(32, 64))
                            project_T(s // 4, s % 2)
                        elif s in (8, 9):
                            project_v(s - 8)
                        elif s % 4 == 2:
                            pe.wait_ge(rden_ready, at(4, s // 4 + 1))
                            for q in range(2):
                                ins = nc.tensor.transpose(misc_ps[:, q * P:q * P + P],
                                                          rden[:, 2 * q:2 * q + 2, :].rearrange("p h d -> p (h d)"), core.ident[:])
                            ins.then_inc(misc_ready, 1)
                        else:
                            pe.wait_ge(attn_ready, at(4, s // 4 + 1))
                            pe.wait_ge(wo_loaded, at(16, 16 if s > 7 else 0))
                            for q in range(2):
                                ins = nc.tensor.matmul(misc_ps[:, q * P:q * P + P], attn_T[:, q * P:q * P + P], wo_cur[:],
                                                       start=True, stop=True)
                            ins.then_inc(misc_ready, 1)
                    if not last or s < 5:
                        r, grp = (s - 5) % 4, (s - 5) // 4 % 2
                        if r == 0:
                            for i in range(2):
                                pe.wait_ge(tr_copied[i], at(SLOTS, s))
                            pe.wait_ge(attn_ready, at(4, s // 4 + 1))
                            if s == 5:
                                pe.wait_ge(misc_free, at(ITEMS, 0))
                        for k in (2 * r, 2 * r + 1):
                            for h in range(2):
                                ins = nc.tensor.matmul(out_ps[64 * h:64 * h + 64, 0:256],
                                                       v[par if s >= 5 else 1 - par][:, k, 64 * h:64 * h + 64],
                                                       probs_T[grp][:, h, k, :], start=k == 0, stop=k == TB - 1)
                        if r == 3:
                            ins.then_inc(pv_done, 1)

                pe.wait_ge(operands_loaded, 32)
                for k in range(FIRST_ITEMS):
                    if k:
                        pe.wait_ge(misc_free, k)
                    if k < 4:
                        project_T(k // 2, k % 2)
                    else:
                        project_v(k - 4)
                pe.wait_ge(zeroed, 1)
                for h in range(2):
                    for k in range(6):
                        nc.tensor.matmul(out_ps[64 * h:64 * h + 64, 0:256], v[1][:, k, 64 * h:64 * h + 64],
                                         probs_T[0][:, h, k, :], start=k == 0, stop=False)
                for i in range(2):
                    pe.wait_ge(stacked[i], STACKED[i])
                scores(0, 0)
                with pe.Fori(0, PAIRS2) as it:
                    for par in range(2):
                        for s in range(SLOTS):
                            slot(s, par, progress(it, par), ITEM)
                for s in range(8):
                    slot(s, 0, LAST, LAST_ITEM, last=True)

            @block.scalar
            def _(act):
                def copy_item(dst, width=512):
                    nc.scalar.activation(dst, misc_ps[:, 0:width], ACT.Copy).then_inc(misc_free, 1)

                def copy_tr(s, i):
                    tile, h = unit((s - 1) % SLOTS)
                    nc.scalar.activation(probs_T[(s - 1) // 4 % 2][:, h, 4 * i:4 * i + 4, tile % 2 * P:tile % 2 * P + P],
                                         tr_ps[i][:].rearrange("p (k q) -> p k q", k=4), ACT.Copy).then_inc(tr_copied[i], 1)

                def slot(s, par, at, item, last=False):
                    if not last:
                        act.wait_ge(negmax_ready, at(SLOTS, s + 1))
                        nc.scalar.activation(probs[s % 4][:], score_ps[s % 2][:], ACT.Exp, bias=negmax[:, s:s + 1],
                                             accum_out=den[:, s:s + 1]).then_inc(probs_ready, 1)
                    if not last or s == 0:
                        for i in range(2):
                            act.wait_ge(tr_ready[i], at(SLOTS, s + 1))
                            copy_tr(s, i)
                    if s in item and s % 4 != 3:
                        act.wait_ge(misc_ready, at(ITEMS, item[s] + 1))
                        if s in (0, 1, 4, 5):
                            i = s // 4
                            if s % 2 == 0:
                                act.wait_ge(lo_ready[i], at(1, 1))
                            copy_item(raw[i][:, s % 2 * 512:s % 2 * 512 + 512])
                        elif s in (8, 9):
                            copy_item(v[1 - par][:, 4 * (s - 8):4 * (s - 8) + 4, :].rearrange("p t n -> p (t n)"))
                        else:
                            copy_item(rden_b[:], 256)

                for k in range(FIRST_ITEMS):
                    act.wait_ge(misc_ready, k + 1)
                    copy_item(raw[k // 2][:, k % 2 * 512:k % 2 * 512 + 512] if k < 4 else
                              v[0][:, 4 * (k - 4):4 * (k - 4) + 4, :].rearrange("p t n -> p (t n)"))
                act.wait_ge(zeroed, 1)
                with act.Fori(0, PAIRS2) as it:
                    for par in range(2):
                        for s in range(SLOTS):
                            slot(s, par, progress(it, par), ITEM)
                for s in range(8):
                    slot(s, 0, LAST, LAST_ITEM, last=True)

            @block.vector
            def _(dve):
                def row_max(s):
                    nc.vector.tensor_reduce(negmax[:, s:s + 1], score_ps[s % 2][:], axis=AX.X, op=ALU.max, negate=True)\
                        .then_inc(negmax_ready, 1)

                def rotate(i, j):
                    t = (raw, rot)[j][i]
                    nc.vector.tensor_tensor(t[:], t[:], tables[:, 2 * i + j, :], ALU.mult).then_inc(rotated[i], 1)

                def split(i):
                    nc.vector.tensor_copy(hi[i][:], raw[i][:]).then_inc(hi_ready[i], 1)

                def slot(s, par, at, batch, item, last=False):
                    if not last:
                        dve.wait_ge(scores_ready, at(SLOTS, s + 2))
                        row_max((s + 1) % SLOTS)
                    if s % 4 == 0 and (not last or s == 0):
                        dve.wait_ge(probs_ready, at(SLOTS, s))
                        c = 4 * ((s // 4 - 1) % 4)
                        nc.vector.reciprocal(rden_col[:], den[:, c:c + 4]).then_inc(rden_col_ready, 1)
                    if s % 4 == 1:
                        dve.wait_ge(pv_done, at(4, s // 4 + 1))
                        dve.wait_ge(misc_free, at(ITEMS, item[s - 3] + 1 if s > 1 else FIRST_ITEMS - 1))
                        nc.vector.tensor_tensor(attn_T[:], out_ps[:, 0:256], rden_b[:], ALU.mult).then_inc(attn_ready, 1)
                    if s % 4 == 3:
                        dve.wait_ge(misc_ready, at(ITEMS, item[s] + 1))
                        rows = core.x[:, bass.ds(batch[s > 7] * TB + 2 * ((s // 4 + 2) % 4), 2), :]
                        nc.vector.tensor_tensor(rows, misc_ps[:, 0:256].rearrange("p (t d) -> p t d", t=2), rows, ALU.add)\
                            .then_inc(misc_free, 1)
                    if not last:
                        if s in (3, 7):
                            i = s // 4
                            dve.wait_ge(swapped[i], at(64, 128))
                            rotate(i, 0)
                        if s in (4, 8):
                            rotate(s // 4 - 1, 1)
                        if s in (6, 10):
                            i = s // 8
                            dve.wait_ge(summed[i], at(1, 2))
                            dve.wait_ge(stacked[i], at(STACKED[i], STACKED[i]))
                            split(i)

                dve.wait_ge(tables_loaded, 16)
                for i in range(2):
                    dve.wait_ge(swapped[i], 64)
                    rotate(i, 0)
                    rotate(i, 1)
                    dve.wait_ge(summed[i], 1)
                    split(i)
                dve.wait_ge(scores_ready, 1)
                row_max(0)
                with dve.Fori(0, PAIRS2) as it:
                    for par in range(2):
                        batch = (((it + 2 * HP // 2 - 1) // (HP // 2)) % B if par == 0 else it // (HP // 2), it // (HP // 2))
                        for s in range(SLOTS):
                            slot(s, par, progress(it, par), batch, ITEM)
                for s in range(8):
                    slot(s, 0, LAST, (B - 1, 0), LAST_ITEM, last=True)


def experts(nc, core, sw, sb_, w1, b1, w2, b2):
    with ExitStack() as st:
        sb = lambda n, s, dt=F32: st.enter_context(nc.sbuf_tensor(f"f0_{n}", s, dt))
        ps = lambda n, s: st.enter_context(nc.psum_tensor(f"f0_{n}", s, F32))
        sem = lambda n: core.sem(f"f0_{n}")
        TG = B * N // 512

        switch = sb("switch", [P, E])
        switch_b = sb("switch_b", [P, E])
        b1_rows = sb("b1_rows", [E * FC, P])
        b1_T = sb("b1_T", [P, E * FC])
        b1_cur = [sb(f"b1_cur{i}", [P, FC]) for i in range(2)]
        b2_rows = sb("b2_rows", [E, D])
        w1_cur = [sb(f"w1_cur{i}", [P, F]) for i in range(2)]
        w2_cur = [sb(f"w2_cur{i}", [P, FC, D]) for i in range(2)]
        hidden = [sb(f"hidden{i}", [P, FC, 512]) for i in range(2)]
        logits, shifted, expd, order, cand, gates = (sb(n, [P, T, E]) for n in ("logits", "shifted", "expd", "order", "cand", "gates"))
        iota = sb("iota", [P, E])
        top, total, first = (sb(n, [P, T]) for n in ("top", "total", "first"))
        gates_e = sb("gates_e", [P, E, T])
        gates_T = sb("gates_T", [E, B * N])
        h_ps = [ps(f"h{i}", [P, 512]) for i in range(FC)]
        y_ps = [ps(f"y{i}", [P, 512]) for i in range(2)]
        route_ps = ps("route", [P, 512])
        bias_ps = ps("bias", [P, 512])

        small_loaded, weights_loaded = sem("small_loaded"), sem("weights_loaded")
        iota_ready, logits_ready, b1_ready, b1_copied = sem("iota_ready"), sem("logits_ready"), sem("b1_ready"), sem("b1_copied")
        b1_kept = sem("b1_kept")
        dve_step, shifted_ready, expd_ready, gates_ready = sem("dve_step"), sem("shifted_ready"), sem("expd_ready"), sem("gates_ready")
        gt_ready, gt_copied, bias_ready, bias_added = sem("gt_ready"), sem("gt_copied"), sem("bias_ready"), sem("bias_added")
        h_ready, h_done, y_ready, y_added = sem("h_ready"), sem("h_done"), sem("y_ready"), sem("y_added")

        with nc.Block() as block:
            @block.sync
            def _(sp):
                def load_expert(e, par):
                    sp.dma_start(w1_cur[par][:], w1.rearrange("e d f -> d e f")[:, bass.ds(e, 1), :].rearrange("d e f -> d (e f)"))\
                        .then_inc(weights_loaded, 16)
                    sp.dma_start(w2_cur[par][:], w2.rearrange("e (c p) d -> p (e c) d", p=P)[:, bass.ds(e * FC, FC), :])\
                        .then_inc(weights_loaded, 16)

                sp.dma_start(switch[:], sw).then_inc(small_loaded, 16)
                sp.dma_start(switch_b[:], sb_.rearrange("(o e) -> o e", o=1).broadcast_to([P, E])).then_inc(small_loaded, 16)
                sp.dma_start(b1_rows[:], b1.rearrange("e (c p) -> (e c) p", p=P)).then_inc(small_loaded, 16)
                sp.dma_start(b2_rows[:], b2).then_inc(small_loaded, 16)
                load_expert(0, 0)
                load_expert(1, 1)
                with sp.Fori(0, E // 2) as it:
                    for par in range(2):
                        e = sp.snap((it * 2 + par + 2) % E)
                        sp.wait_ge(y_ready, it * (2 * TG) + (par + 1) * TG)
                        load_expert(e, par)
                sp.wait_ge(weights_loaded, 32 * (E + 2))

            @block.gpsimd
            def _(pool):
                nc.gpsimd.iota(iota[:], pattern=[[1, E]], base=-E, channel_multiplier=0, allow_small_or_imprecise_dtypes=True).then_inc(iota_ready, 1)

            @block.tensor
            def _(pe):
                def hidden_of(f, tg, par):
                    nc.tensor.matmul(h_ps[f][:], w1_cur[par][:, f * P:f * P + P], core.xT[:, tg * 512:tg * 512 + 512],
                                     start=True, stop=True).then_inc(h_ready, 1)

                pe.wait_ge(small_loaded, 64)
                for t in range(T):
                    ins = nc.tensor.matmul(route_ps[:, t * E:t * E + E], core.xT[:, t * P:t * P + P], switch[:], start=True, stop=True)
                ins.then_inc(logits_ready, 1)
                nc.tensor.transpose(bias_ps[:, 0:E * FC], b1_rows[:], core.ident[0:E * FC, 0:E * FC]).then_inc(b1_ready, 1)
                pe.wait_ge(weights_loaded, 64)
                for f in range(FC):
                    hidden_of(f, 0, 0)
                pe.wait_ge(gates_ready, 1)
                pe.wait_ge(b1_copied, 1)
                for i in range(T // 4):
                    if i:
                        pe.wait_ge(gt_copied, i)
                    for t in range(4 * i, 4 * i + 4):
                        ins = nc.tensor.transpose(bias_ps[0:E, t % 4 * P:t % 4 * P + P], gates[:, t, :], core.ident[:])
                    ins.then_inc(gt_ready, 1)
                pe.wait_ge(gt_copied, T // 4)
                for i in range(T // 4):
                    if i:
                        pe.wait_ge(bias_added, i)
                    for t in range(4 * i, 4 * i + 4):
                        ins = nc.tensor.matmul(route_ps[:, t % 4 * P:t % 4 * P + P], gates_T[:, t * P:t * P + P], b2_rows[:],
                                               start=True, stop=True)
                    ins.then_inc(bias_ready, 1)

                with pe.Fori(0, E // 2) as it:
                    for par in range(2):
                        for tg in range(TG):
                            k = par * TG + tg
                            if tg == TG - 1:
                                pe.wait_ge(weights_loaded, it * 64 + 32 * (par + 2))
                            for f in range(FC):
                                pe.wait_ge(h_done, it * (2 * TG * FC) + (k * FC + f + 1))
                                hidden_of(f, (tg + 1) % TG, par if tg < TG - 1 else 1 - par)
                            if k < 2:
                                pe.wait_ge(y_added, it * (2 * TG) + max(k - 1, 0))
                            else:
                                pe.wait_ge(y_added, it * (2 * TG) + (k - 1))
                            for t in range(4):
                                for f in range(FC):
                                    ins = nc.tensor.matmul(y_ps[k % 2][:, t * P:t * P + P], hidden[k % 2][:, f, t * P:t * P + P],
                                                           w2_cur[par][:, f, :], start=f == 0, stop=f == FC - 1)
                            ins.then_inc(y_ready, 1)

            @block.scalar
            def _(act):
                def gelu(f, k, par):
                    nc.scalar.activation(hidden[k % 2][:, f, :], h_ps[f][:], ACT.Gelu_apprx_tanh,
                                         bias=b1_cur[par][:, f:f + 1]).then_inc(h_done, 1)

                def keep_b1(e, par):
                    nc.scalar.activation(b1_cur[par][:], b1_T[:, bass.ds(e * FC, FC)], ACT.Copy).then_inc(b1_kept, 1)

                act.wait_ge(b1_ready, 1)
                nc.scalar.activation(b1_T[:], bias_ps[:, 0:E * FC], ACT.Copy).then_inc(b1_copied, 1)
                act.wait_ge(shifted_ready, 1)
                nc.scalar.activation(expd[:], shifted[:], ACT.Exp).then_inc(expd_ready, 1)
                for i in range(T // 4):
                    act.wait_ge(gt_ready, i + 1)
                    nc.scalar.activation(gates_T[:, i * 512:i * 512 + 512], bias_ps[0:E, :], ACT.Copy).then_inc(gt_copied, 1)
                act.wait_ge(b1_copied, 1)
                keep_b1(0, 0)
                act.wait_ge(b1_kept, 1)
                for f in range(FC):
                    act.wait_ge(h_ready, f + 1)
                    gelu(f, 0, 0)
                with act.Fori(0, E // 2) as it:
                    for k in range(2 * TG):
                        par = (k + 1) // TG % 2
                        if k % TG == TG - 1:
                            act.wait_ge(b1_kept, it * 2 + (k // TG + 2))
                        for f in range(FC):
                            act.wait_ge(h_ready, it * (2 * TG * FC) + ((k + 1) * FC + f + 1))
                            gelu(f, k + 1, par)
                        if k % TG == 0:
                            keep_b1((it * 2 + (k // TG + 1)) % E, 1 - par)

            @block.vector
            def _(dve):
                steps = [0]

                def step(ins):
                    steps[0] += 1
                    ins.then_inc(dve_step, 1)
                    dve.wait_ge(dve_step, steps[0])

                shape = [P, T, E]
                dve.wait_ge(logits_ready, 1)
                dve.wait_ge(iota_ready, 1)
                step(nc.vector.tensor_tensor(logits[:], route_ps[:, 0:T * E].rearrange("p (t e) -> p t e", t=T),
                                             switch_b[:].rearrange("p (o e) -> p o e", o=1).broadcast_to(shape), ALU.add))
                step(nc.vector.tensor_reduce(top[:], logits[:], axis=AX.X, op=ALU.max))
                nc.vector.tensor_tensor(shifted[:], logits[:], spread(top[:], shape), ALU.subtract).then_inc(shifted_ready, 1)
                step(nc.vector.tensor_tensor(order[:], logits[:], spread(top[:], shape), ALU.is_equal))
                experts_row = iota[:].rearrange("p (o e) -> p o e", o=1).broadcast_to(shape)
                step(nc.vector.tensor_tensor(cand[:], order[:], experts_row, ALU.mult))
                step(nc.vector.tensor_reduce(first[:], cand[:], axis=AX.X, op=ALU.min))
                step(nc.vector.tensor_tensor(cand[:], experts_row, spread(first[:], shape), ALU.is_equal))
                dve.wait_ge(expd_ready, 1)
                step(nc.vector.tensor_reduce(total[:], expd[:], axis=AX.X, op=ALU.add))
                step(nc.vector.reciprocal(total[:], total[:]))
                nc.vector.tensor_tensor(gates[:], cand[:], spread(total[:], shape), ALU.mult).then_inc(gates_ready, 1)
                dve.wait_ge(gates_ready, 1)
                step(nc.vector.tensor_copy(gates_e[:].rearrange("p e t -> p t e"), gates[:]))
                for i in range(T // 4):
                    dve.wait_ge(bias_ready, i + 1)
                    rows = core.x[:, 4 * i:4 * i + 4, :]
                    nc.vector.tensor_tensor(rows, route_ps[:].rearrange("p (t d) -> p t d", t=4), rows, ALU.add).then_inc(bias_added, 1)
                dve.wait_ge(bias_added, T // 4)
                with dve.Fori(0, E // 2) as it:
                    for k in range(2 * TG):
                        dve.wait_ge(y_ready, it * (2 * TG) + (k + 1))
                        for t in range(4):
                            tile = k % TG * 4 + t
                            ins = nc.vector.scalar_tensor_tensor(
                                out=core.x[:, tile, :], in0=y_ps[k % 2][:, t * P:t * P + P],
                                scalar=gates_e[:, bass.ds(it * 2 + k // TG, 1), tile], in1=core.x[:, tile, :],
                                op0=ALU.mult, op1=ALU.add)
                        ins.then_inc(y_added, 1)


def block_attention(nc, core, consts, Wq, bq, Wk, bk, Wv, bv, Wo, bo):
    G = H1 // HG
    ITERS = B * G
    GR = TB // 2
    UNITS = GR * 2 * HG
    FIX = UNITS - 2 * HG
    VT = TB + GR - 1
    with ExitStack() as st:
        sb = lambda n, s, dt=F32: st.enter_context(nc.sbuf_tensor(f"a1_{n}", s, dt))
        sem = lambda n: core.sem(f"a1_{n}")
        q_all = sb("q_all", [P, G, B * N], F32R)
        k_all = sb("k_all", [P, G, B * N], F32R)
        v_all = sb("v_all", [P, B, VT, D])
        wo_g = sb("wo_g", [P, G, D])
        block_mask = sb("block_mask", [P, P])

        with ExitStack() as st2:
            sb2 = lambda n, s, dt=F32: st2.enter_context(nc.sbuf_tensor(f"a1p_{n}", s, dt))
            ps2 = lambda n, s: st2.enter_context(nc.psum_tensor(f"a1p_{n}_ps", s, F32))
            w = sb2("w", [P, 4, D])
            w_T = sb2("w_T", [P, 4, D])
            w_rep = sb2("w_rep", [P, 2, H1, 4, DH1])
            b_row = sb2("b_row", [1, 2, D])
            b_rep = sb2("b_rep", [1, 2, H1, 4, DH1])
            b_col = sb2("b_col", [P, 2 * G])
            ones = sb2("ones", [1, 4])
            bv_b, bo_b = sb2("bv_b", [P, D]), sb2("bo_b", [P, D])
            part = sb2("part", [P, 4])
            full = [sb2(f"full{i}", [P, 512]) for i in range(2)]
            high = [sb2(f"high{i}", [P, 512], F32R) for i in range(2)]
            pair_sum = sb2("pair_sum", [P, B, GR, D])
            w_ps, b_ps = ps2("w", [P, 512]), ps2("b", [P, 512])
            s_ps = [ps2(f"s{i}", [P, 512]) for i in range(2)]
            v_ps = [ps2(f"v{i}", [P, 512]) for i in range(2)]
            loaded, zeroed = sem("loaded"), sem("zeroed")
            wT_ready, wT_copied, rep_ready, b_ready, b_copied = (sem(n) for n in ("wT_ready", "wT_copied", "rep_ready", "b_ready", "b_copied"))
            proj_ready, full_ready, high_ready, stack_ready = (sem(n) for n in ("proj_ready", "full_ready", "high_ready", "stack_ready"))
            v_ready, v_added, pair_ready, wo_placed = (sem(n) for n in ("v_ready", "v_added", "pair_ready", "wo_placed"))
            sums_ready = sem("sums_ready")
            STEPS = 2 * G * 4

            with nc.Block() as block:
                @block.sync
                def _(sp):
                    for i, m in enumerate((Wq, Wk, Wv, Wo)):
                        sp.dma_start(w[:, i, :], m).then_inc(loaded, 16)
                    row = lambda v: v.rearrange("(o d) -> o d", o=1)
                    sp.dma_start(b_row[:, 0, :], row(bq)).then_inc(loaded, 16)
                    sp.dma_start(b_row[:, 1, :], row(bk)).then_inc(loaded, 16)
                    sp.dma_start(bv_b[:], row(bv).broadcast_to([P, D])).then_inc(loaded, 16)
                    sp.dma_start(bo_b[:], row(bo).broadcast_to([P, D])).then_inc(loaded, 16)
                    sp.dma_start(part[:], consts["part"]).then_inc(loaded, 16)
                    sp.dma_start(block_mask[:], consts["block_mask"]).then_inc(loaded, 16)
                    sp.wait_ge(wT_copied, 1)
                    sp.wait_ge(zeroed, 1)
                    for h in range(H1):
                        sp.dma_start(wo_g[32 * (h % HG):32 * (h % HG) + DH1, h // HG, :], w_T[h * DH1:h * DH1 + DH1, 3, :])\
                            .then_inc(wo_placed, 16)
                    sp.wait_ge(wo_placed, 16 * H1)

                @block.gpsimd
                def _(pool):
                    nc.gpsimd.memset(ones[:], 1.0)
                    nc.gpsimd.memset(wo_g[:], 0.0).then_inc(zeroed, 1)
                    pool.wait_ge(v_added, 4)
                    for b in range(B):
                        pairs = v_all[:, b, 0:TB, :].rearrange("p (g o) d -> p g o d", o=2)
                        ins = nc.gpsimd.tensor_tensor(pair_sum[:, b], pairs[:, :, 0, :], pairs[:, :, 1, :], ALU.add)
                    ins.then_inc(pair_ready, 1)
                    pool.wait_ge(pair_ready, 1)
                    nc.gpsimd.tensor_copy(v_all[:, :, TB + GR - 2, :], pair_sum[:, :, GR - 1, :]).then_inc(sums_ready, 1)
                    for g in reversed(range(GR - 2)):
                        pool.wait_ge(sums_ready, GR - 2 - g)
                        nc.gpsimd.tensor_tensor(v_all[:, :, TB + g, :], v_all[:, :, TB + g + 1, :], pair_sum[:, :, g + 1, :], ALU.add)\
                            .then_inc(sums_ready, 1)

                @block.tensor
                def _(pe):
                    pe.wait_ge(loaded, 160)
                    for i in range(4):
                        ins = nc.tensor.transpose(w_ps[:, i * D:i * D + D], w[:, i, :], core.ident[:])
                    ins.then_inc(wT_ready, 1)
                    pe.wait_ge(rep_ready, 2)
                    pe.wait_ge(zeroed, 1)
                    for i in range(2 * G):
                        ins = nc.tensor.matmul(b_ps[:, 2 * i:2 * i + 1], b_rep[:, i // G, i % G * HG:(i % G + 1) * HG].rearrange("o h r d -> o (h r d)"),
                                               ones[0:1, 0:1], start=True, stop=True)
                    ins.then_inc(b_ready, 1)
                    for k in range(STEPS):
                        i, g, c = k // (4 * G), k // 4 % G, k % 4
                        if k >= 2:
                            pe.wait_ge(full_ready, k - 1)
                        nc.tensor.matmul(s_ps[k % 2][:], w_rep[:, i, g * HG:(g + 1) * HG].rearrange("p h r d -> p (h r d)"),
                                         core.xT[:, c * 512:c * 512 + 512], start=True, stop=True).then_inc(proj_ready, 1)
                        if k % 8 == 7:
                            q = k // 8
                            if q >= 2:
                                pe.wait_ge(v_added, q - 1)
                            for t in range(4 * q, 4 * q + 4):
                                ins = nc.tensor.matmul(v_ps[q % 2][:, t % 4 * D:t % 4 * D + D], core.xT[:, t * P:t * P + P], w_T[:, 2, :],
                                                       start=True, stop=True)
                            ins.then_inc(v_ready, 1)

                @block.scalar
                def _(act):
                    act.wait_ge(wT_ready, 1)
                    nc.scalar.activation(w_T[:].rearrange("p i d -> p (i d)"), w_ps[:], ACT.Copy).then_inc(wT_copied, 1)
                    act.wait_ge(b_copied, 1)
                    for k in range(STEPS):
                        i, g = k // (4 * G), k // 4 % G
                        act.wait_ge(proj_ready, k + 1)
                        if k >= 2:
                            act.wait_ge(stack_ready, k - 1)
                        nc.scalar.activation(full[k % 2][:], s_ps[k % 2][:], ACT.Identity, bias=b_col[:, k // 4:k // 4 + 1],
                                             scale=float(DH1) ** -0.5 if i == 0 else 1.0).then_inc(full_ready, 1)

                @block.vector
                def _(dve):
                    dve.wait_ge(loaded, 160)
                    dve.wait_ge(wT_copied, 1)
                    for i in range(2):
                        heads = w_T[:, i, :].rearrange("p (h o d) -> p h o d", h=H1, o=1).broadcast_to([P, H1, 4, DH1])
                        nc.vector.tensor_copy(w_rep[:, i], heads)
                        bias = b_row[:, i, :].rearrange("p (h o d) -> p h o d", h=H1, o=1).broadcast_to([1, H1, 4, DH1])
                        nc.vector.tensor_copy(b_rep[:, i], bias).then_inc(rep_ready, 1)
                    dve.wait_ge(b_ready, 1)
                    cols = b_ps[:, 0:4 * G].rearrange("p (i o) -> p i o", o=2)[:, :, 0]
                    nc.vector.tensor_scalar(b_col[:, 0:G], cols[:, 0:G], float(DH1) ** -0.5, None, ALU.mult)
                    nc.vector.tensor_copy(b_col[:, G:2 * G], cols[:, G:2 * G]).then_inc(b_copied, 1)
                    nc.vector.tensor_tensor(core.x[:], core.x[:], bo_b[:].rearrange("p (o d) -> p o d", o=1).broadcast_to([P, T, D]), ALU.add)
                    for k in range(STEPS):
                        i, g, c = k // (4 * G), k // 4 % G, k % 4
                        dve.wait_ge(full_ready, k + 1)
                        nc.vector.tensor_scalar(high[k % 2][:], full[k % 2][:], part[:, 2 * i:2 * i + 1], None, ALU.mult).then_inc(high_ready, 1)
                        dve.wait_ge(high_ready, k + 1)
                        nc.vector.scalar_tensor_tensor(out=(q_all, k_all)[i][:, g, c * 512:c * 512 + 512], in0=full[k % 2][:],
                                                       scalar=part[:, 2 * i + 1:2 * i + 2], in1=high[k % 2][:].bitcast(F32),
                                                       op0=ALU.mult, op1=ALU.add).then_inc(stack_ready, 1)
                        if k % 8 == 7:
                            q = k // 8
                            dve.wait_ge(v_ready, q + 1)
                            nc.vector.tensor_tensor(v_all[:, q // 2, q % 2 * 4:q % 2 * 4 + 4, :], v_ps[q % 2][:].rearrange("p (t d) -> p t d", t=4),
                                                    bv_b[:].rearrange("p (o d) -> p o d", o=1).broadcast_to([P, 4, D]), ALU.add).then_inc(v_added, 1)

        q_cur = [sb(f"q_cur{i}", [P, HG, 2 * P], F32R) for i in range(2)]
        k_cur = [sb(f"k_cur{i}", [P, N], F32R) for i in range(2)]
        v_cur = [sb(f"v_cur{i}", [P, VT, HG, 32]) for i in range(2)]
        zeros = sb("zeros", [P, 132], F32R)
        probs = [sb(f"probs{i}", [P, N]) for i in range(4)]
        probs_T = [sb(f"probs_T{i}", [P, TB - 1 + i, HG, 256]) for i in range(2)]
        negmax, den = sb("negmax", [P, UNITS]), sb("den", [P, UNITS])
        later = sb("later", [P, UNITS])
        more_keys = sb("more_keys", [P, GR - 1])
        rden_col = sb("rden_col", [P, 2 * HG])
        rden = sb("rden", [P, 2 * HG, 32])
        ones = sb("rden_ones", [P, 2 * HG, 32])
        rden_b, attn_T = sb("rden_b", [P, 256]), sb("attn_T", [P, 256])
        ps = lambda n, s: st.enter_context(nc.psum_tensor(f"a1_{n}", s, F32))
        score_ps = [ps(f"score{i}", [P, N]) for i in range(2)]
        tr_ps = [ps(f"tr{i}", [P, 512]) for i in range(2)]
        out_ps, misc_ps = ps("out", [P, 512]), ps("misc", [P, 512])
        q_cleared, cleared, junk_cleared, v_copied = sem("q_cleared"), sem("cleared"), sem("junk_cleared"), sem("v_copied")
        q_loaded = [sem("even_q_loaded"), sem("odd_q_loaded")]
        k_loaded = [sem("even_k_loaded"), sem("odd_k_loaded")]
        scores_ready, masked, negmax_ready, probs_ready, later_kept = (sem(n) for n in ("scores_ready", "masked", "negmax_ready", "probs_ready", "later_kept"))
        tr_ready = [sem("tr_lo_ready"), sem("tr_hi_ready")]
        tr_copied = [sem("tr_lo_copied"), sem("tr_hi_copied")]
        pv_done, attn_ready, rden_ready, rden_col_ready, den_whole = (sem(n) for n in ("pv_done", "attn_ready", "rden_ready", "rden_col_ready", "den_whole"))
        misc_ready, misc_free = sem("misc_ready"), sem("misc_free")
        ITEMS = 2 * GR
        ITEM = {2 * HG * g + q: 2 * g + q - 3 for g in range(GR) for q in (3, 4)}
        LAST_ITEM = {3: 0, 4: 1, 2 * HG + 4: 2}
        UG = 2 * HG
        Q_LOADS = 16 * HG
        ITERS2 = ITERS // 2

        def unit(s):
            s %= UNITS
            return s // UG, s // HG % 2 + 2 * (s // UG), s % HG

        def tiles(grp):
            return 2 * grp + 2 + (grp < GR - 1)

        def hi_copies(s):
            return 1 + max(0, s - UG)

        def act_copies_hi(grp, h):
            return grp == GR - 1 and h % 2 == 1

        def progress(it, par):
            return lambda m, c: it * (2 * m) + (par * m + c)

        LAST = lambda m, c: m * ITERS + c

        with nc.Block() as block:
            @block.sync
            def _(sp):
                flat_q, flat_k = (src[:].bitcast(F32).rearrange("p g n -> p (g n)") for src in (q_all, k_all))

                def load_q(col, grp):
                    for h in reversed(range(HG)):
                        rows = slice(32 * h, 32 * h + 32)
                        sp.dma_start(q_cur[grp % 2][rows, h, :].bitcast(F32), flat_q[rows, bass.ds(col, N)][:, 2 * P * grp:2 * P * (grp + 1)])\
                            .then_inc(q_loaded[grp % 2], 16)

                def load_k(col, par):
                    sp.dma_start(k_cur[par][:].bitcast(F32), flat_k[:, bass.ds(col, N)]).then_inc(k_loaded[par], 16)

                load_k(0, 0)
                sp.wait_ge(q_cleared, 1)
                load_q(0, 0)
                load_q(0, 1)
                with sp.Fori(0, ITERS2) as it:
                    for par in range(2):
                        n = it * 2 + par
                        col = sp.snap(n % G * (B * N) + n // G * N)
                        next_col = sp.snap((n + 1) % G * (B * N) + (n + 1) // G % B * N)
                        for grp in range(GR):
                            sp.wait_ge(scores_ready, it * (2 * UNITS) + (par * UNITS + UG * (grp + 1)))
                            if grp == 0:
                                load_k(next_col, 1 - par)
                            load_q(col if grp < GR - 2 else next_col, (grp + 2) % GR)
                for i in range(2):
                    sp.wait_ge(q_loaded[i], Q_LOADS * (ITERS * GR // 2 + 1))
                    sp.wait_ge(k_loaded[i], 16 * (ITERS2 + 1 - i))

            @block.gpsimd
            def _(pool):
                nc.gpsimd.memset(q_cur[0][:].bitcast(F32), 0.0)
                nc.gpsimd.memset(q_cur[1][:].bitcast(F32), 0.0).then_inc(q_cleared, 1)
                nc.gpsimd.memset(v_cur[0][:], 0.0)
                nc.gpsimd.memset(v_cur[1][:], 0.0)
                nc.gpsimd.memset(zeros[:].bitcast(F32), 0.0)
                for grp in range(GR - 1):
                    nc.gpsimd.memset(more_keys[:, grp:grp + 1], float(N - 2 * P * (grp + 1) - 1))
                nc.gpsimd.memset(probs_T[1][:, 0:3], 0.0)
                nc.gpsimd.memset(ones[:], 1.0).then_inc(cleared, 1)
                pool.wait_ge(cleared, 1)

                def copy_v(g, b, par):
                    flat = v_all[:].rearrange("p b t d -> p (b t) d")
                    src = flat[:, bass.ds(b * VT, VT), bass.ds(g * HG * DH1, HG * DH1)].rearrange("p t (h d) -> p t h d", h=HG)
                    nc.gpsimd.tensor_copy(v_cur[par][:, :, :, 0:DH1], src).then_inc(v_copied, 1)

                def spread_rden(at, grp):
                    pool.wait_ge(rden_col_ready, at(GR, grp + 1))
                    nc.gpsimd.tensor_tensor(rden[:], spread(rden_col[:], [P, UG, 32]), ones[:], ALU.mult).then_inc(rden_ready, 1)

                copy_v(0, 0, 0)
                with pool.Fori(0, ITERS2) as it:
                    for par in range(2):
                        at = progress(it, par)
                        n = it * 2 + par + 1
                        next_g, next_b = pool.snap(n % G), pool.snap(n // G % B)
                        for s in range(FIX):
                            grp = unit(s)[0]
                            keys = 2 * P * (grp + 1)
                            pool.wait_ge(probs_ready, at(UNITS, s + 1))
                            shared = probs[s % 4][:, keys:keys + 1]
                            nc.gpsimd.tensor_tensor(later[:, s:s + 1], shared, more_keys[:, grp:grp + 1], ALU.mult).then_inc(later_kept, 1)
                            if s % UG == 0:
                                spread_rden(at, grp)
                            if s == UG + 2:
                                copy_v(next_g, next_b, 1 - par)
                        spread_rden(at, GR - 1)
                spread_rden(LAST, 0)

            @block.tensor
            def _(pe):
                def scores(s, par):
                    grp, tile, h = unit(s)
                    keys = 2 * P * (grp + 1)
                    runs = [(0, (tile + 1) * P, True), ((tile + 1) * P, keys + (2 if keys < N else 0), False)]
                    for lo, hi, real in runs:
                        while lo < hi:
                            end = min(hi, (lo // 512 + 1) * 512)
                            src = k_cur[par][:, lo:end] if real else zeros[:, 0:end - lo]
                            last = nc.tensor.matmul(score_ps[s % 2][:, lo:end], q_cur[grp % 2][:, h, tile % 2 * P:tile % 2 * P + P], src, start=True, stop=True)
                            lo = end
                    last.then_inc(scores_ready, 1)

                def slot(s, par, at, item, last=False):
                    if not last or s == 0:
                        pe.wait_ge(probs_ready, at(UNITS, s))
                    if not last:
                        if s == UNITS - 1:
                            pe.wait_ge(k_loaded[1 - par], it * 16 + 16 * (par + 1))
                            pe.wait_ge(q_loaded[0], at(Q_LOADS * GR // 2, Q_LOADS * (GR // 2 + 1)))
                            scores(0, 1 - par)
                        else:
                            if (s + 1) % UG == 0:
                                grp = (s + 1) // UG
                                pe.wait_ge(q_loaded[grp % 2], at(Q_LOADS * GR // 2, Q_LOADS * (grp // 2 + 1)))
                            scores(s + 1, par)
                    if not last or s == 0:
                        grp, tile, h = unit(s - 1)
                        n = tiles(grp)
                        pe.wait_ge(tr_copied[0], at(UNITS, s))
                        if n > 4:
                            pe.wait_ge(tr_copied[1], at(FIX, hi_copies(s - 1) if s else 0))
                        for k in range(n):
                            src = probs[(s - 1) % 4][:, k * P:k * P + P] if k < 2 * grp + 2 else \
                                probs[(s - 1) % 4][:, k * P:k * P + 1].broadcast_to([P, P])
                            ins = nc.tensor.transpose(tr_ps[k // 4][:, k % 4 * P:k % 4 * P + P], src, core.ident[:])
                            if k == 3 or (k == n - 1 and n < 4):
                                ins.then_inc(tr_ready[0], 1)
                            elif k == n - 1:
                                ins.then_inc(tr_ready[1], 1)
                    if s in item:
                        pe.wait_ge(misc_free, at(ITEMS, item[s]))
                        for q in range(2):
                            cols = slice(q * P, q * P + P)
                            if s % UG == 3:
                                if q == 0:
                                    pe.wait_ge(rden_ready, at(GR, s // UG + 1))
                                ins = nc.tensor.transpose(misc_ps[:, cols], rden[:, q * HG:(q + 1) * HG, :].rearrange("p h d -> p (h d)"), core.ident[:])
                            else:
                                if q == 0:
                                    pe.wait_ge(attn_ready, at(GR, s // UG + 1))
                                ins = nc.tensor.matmul(misc_ps[:, cols], attn_T[:, cols], wo_g[:].rearrange("p g d -> p (g d)")[:, wo_cols(s)], start=True, stop=True)
                        ins.then_inc(misc_ready, 1)
                    if not last or s < UG + 1:
                        grp, r = (s - UG - 1) // UG % GR, (s - 1) % UG
                        if r == 0:
                            pe.wait_ge(tr_copied[0], at(UNITS, s))
                            if tiles(grp) > 4:
                                pe.wait_ge(tr_copied[1], at(FIX, hi_copies(s - 1)))
                            pe.wait_ge(attn_ready, at(GR, s // UG + 1))
                            if s == UG + 1:
                                pe.wait_ge(v_copied, at(1, 1))
                        n = tiles(grp)
                        done = [r] if n < UG else [0, 1] if r == 0 else [r + 1]
                        for k in [k for k in done if k < n]:
                            for h in range(HG):
                                tile = k if k < 2 * grp + 2 else TB + grp
                                ins = nc.tensor.matmul(out_ps[32 * h:32 * h + 32, 0:256], v_cur[par if s > UG else 1 - par][:, tile, h, :],
                                                       probs_T[grp % 2][:, k, h, :], start=k == 0, stop=k == n - 1)
                            if k == n - 1:
                                ins.then_inc(pv_done, 1)

                pe.wait_ge(cleared, 1)
                pe.wait_ge(junk_cleared, 1)
                for h in range(HG):
                    ins = nc.tensor.matmul(out_ps[32 * h:32 * h + 32, 0:256], v_cur[1][:, 0, h, :], probs_T[1][:, 0, h, :], start=True, stop=True)
                ins.then_inc(pv_done, 1)
                pe.wait_ge(k_loaded[0], 16)
                pe.wait_ge(q_loaded[0], Q_LOADS)
                scores(0, 0)
                with pe.Fori(0, ITERS2) as it:
                    for par in range(2):
                        n = it * 2 + par
                        wo_cols = lambda s, n=n: bass.ds((n % G if s > 2 * UG else (n + G - 1) % G) * D, D)
                        for s in range(UNITS):
                            slot(s, par, progress(it, par), ITEM)
                wo_cols = lambda s: slice((G - 1) * D, G * D)
                for s in range(2 * UG):
                    slot(s, 0, LAST, LAST_ITEM, last=True)

            @block.scalar
            def _(act):
                def slot(s, at, item, last=False):
                    if not last:
                        grp, tile, h = unit(s)
                        keys = 2 * P * (grp + 1)
                        n = keys + (keys < N)
                        act.wait_ge(negmax_ready, at(UNITS, s + 1))
                        act.wait_ge(later_kept, at(FIX, min(max(s - 3, 0), FIX)))
                        nc.scalar.activation(probs[s % 4][:, 0:n], score_ps[s % 2][:, 0:n], ACT.Exp, bias=negmax[:, s:s + 1],
                                             accum_out=den[:, s:s + 1]).then_inc(probs_ready, 1)
                    if not last or s == 0:
                        grp, tile, h = unit(s - 1)
                        n = min(4, tiles(grp))
                        act.wait_ge(tr_ready[0], at(UNITS, s + 1))
                        nc.scalar.activation(probs_T[grp % 2][:, 0:n, h, tile % 2 * P:tile % 2 * P + P],
                                             tr_ps[0][:, 0:n * P].rearrange("p (k q) -> p k q", k=n), ACT.Copy).then_inc(tr_copied[0], 1)
                        n = tiles(grp) - 4
                        if act_copies_hi(grp, h):
                            act.wait_ge(tr_ready[1], at(FIX, hi_copies(s - 1) + 1 if s else 1))
                            nc.scalar.activation(probs_T[grp % 2][:, 4:4 + n, h, tile % 2 * P:tile % 2 * P + P],
                                                 tr_ps[1][:, 0:n * P].rearrange("p (k q) -> p k q", k=n), ACT.Copy).then_inc(tr_copied[1], 1)
                    if s in item and s % UG == 3:
                        act.wait_ge(misc_ready, at(ITEMS, item[s] + 1))
                        nc.scalar.activation(rden_b[:], misc_ps[:, 0:256], ACT.Copy).then_inc(misc_free, 1)

                act.wait_ge(junk_cleared, 1)
                with act.Fori(0, ITERS2) as it:
                    for par in range(2):
                        for s in range(UNITS):
                            slot(s, progress(it, par), ITEM)
                for s in range(2 * UG):
                    slot(s, LAST, LAST_ITEM, last=True)

            @block.vector
            def _(dve):
                def row_max(s, at):
                    grp, tile, h = unit(s)
                    keys = 2 * P * (grp + 1)
                    n = keys + (keys < N)
                    own = score_ps[s % 2][:, tile * P:tile * P + P]
                    nc.vector.tensor_tensor(own, own, block_mask[:], ALU.mult).then_inc(masked, 1)
                    dve.wait_ge(masked, at(UNITS, s + 1))
                    c = s % UNITS
                    nc.vector.tensor_reduce(negmax[:, c:c + 1], score_ps[s % 2][:, 0:n], axis=AX.X, op=ALU.max, negate=True).then_inc(negmax_ready, 1)

                def slot(s, at, batch, item, last=False):
                    if not last:
                        dve.wait_ge(scores_ready, at(UNITS, s + 2))
                        row_max(s + 1, at)
                    if s % UG == 1 and (not last or s == 1):
                        dve.wait_ge(probs_ready, at(UNITS, s if not last else 0))
                        dve.wait_ge(later_kept, at(FIX, s - 1))
                        c = (s - UG - 1) % UNITS
                        if c < FIX:
                            nc.vector.tensor_tensor(den[:, c:c + UG], den[:, c:c + UG], later[:, c:c + UG], ALU.add).then_inc(den_whole, 1)
                            dve.wait_ge(den_whole, at(GR - 1, c // UG + 1))
                        nc.vector.reciprocal(rden_col[:], den[:, c:c + UG]).then_inc(rden_col_ready, 1)
                    if s % UG == 0:
                        dve.wait_ge(pv_done, at(GR, s // UG + 1))
                        dve.wait_ge(misc_free, at(ITEMS, 2 * (s // UG) - 1 if s > 0 or last else 0))
                        nc.vector.tensor_tensor(attn_T[:], out_ps[:, 0:256], rden_b[:], ALU.mult).then_inc(attn_ready, 1)
                    if not last or s == 0:
                        grp, tile, h = unit(s - 1)
                        n = tiles(grp) - 4
                        if n > 0 and not act_copies_hi(grp, h):
                            dve.wait_ge(tr_ready[1], at(FIX, hi_copies(s - 1) + 1 if s else 1))
                            nc.vector.tensor_copy(probs_T[grp % 2][:, 4:4 + n, h, tile % 2 * P:tile % 2 * P + P],
                                                  tr_ps[1][:, 0:n * P].rearrange("p (k q) -> p k q", k=n)).then_inc(tr_copied[1], 1)
                    if s in item and s % UG == 4:
                        dve.wait_ge(misc_ready, at(ITEMS, item[s] + 1))
                        rows = core.x[:, bass.ds(batch[s > 2 * UG] * TB + 2 * ((s // UG + 2) % GR), 2), :]
                        nc.vector.tensor_tensor(rows, misc_ps[:, 0:256].rearrange("p (t d) -> p t d", t=2), rows, ALU.add).then_inc(misc_free, 1)

                nc.vector.memset(probs[3][:], 0.0)
                nc.vector.memset(probs_T[1][:, 3:], 0.0)
                nc.vector.memset(den[:], 1.0)
                nc.vector.memset(rden_b[:], 0.0).then_inc(junk_cleared, 1)
                dve.wait_ge(junk_cleared, 1)
                dve.wait_ge(cleared, 1)
                dve.wait_ge(scores_ready, 1)
                row_max(0, lambda m, c: c)
                with dve.Fori(0, ITERS2) as it:
                    for par in range(2):
                        n = it * 2 + par
                        batch = ((n + ITERS - 1) // G % B, n // G % B)
                        for s in range(UNITS):
                            slot(s, progress(it, par), batch, ITEM)
                for s in range(2 * UG):
                    slot(s, LAST, (B - 1, 0), LAST_ITEM, last=True)


def channel_mix(nc, core, W_r, W_k, W_v, mu_r, mu_k, out):
    with ExitStack() as st:
        sb = lambda n, s: st.enter_context(nc.sbuf_tensor(f"f1_{n}", s, F32))
        ps = lambda n: st.enter_context(nc.psum_tensor(f"f1_{n}", [P, 512], F32))
        sem = lambda n: core.sem(f"f1_{n}")
        G = B * N // 512
        w_rows = sb("w_rows", [P, 3, D])
        w = sb("w", [P, 3, D])
        mu = sb("mu", [P, 2])
        rest = sb("rest", [P, 2])
        mixed = [sb("xr", [P, B, N]), sb("xk", [P, B, N])]
        k_relu = [sb(f"k_relu{i}", [P, 512]) for i in range(2)]
        k_sq = [sb(f"k_sq{i}", [P, 512]) for i in range(2)]
        gate = [sb(f"gate{i}", [P, 512]) for i in range(2)]
        prod = [sb(f"prod{i}", [P, 512]) for i in range(2)]
        k_ps, r_ps, v_ps = ([ps(f"{n}{i}") for i in range(2)] for n in "krv")
        w_ps = ps("wT")
        wT_ready, wT_copied = sem("wT_ready"), sem("wT_copied")
        loaded, rest_ready, scaled, mixed_ready = sem("loaded"), sem("rest_ready"), sem("scaled"), sem("mixed_ready")
        k_ready, r_ready, v_ready = sem("k_ready"), sem("r_ready"), sem("v_ready")
        relu_done, gate_done, sq_done, prod_done, x_done, stored = (sem(n) for n in ("relu_done", "gate_done", "sq_done", "prod_done", "x_done", "stored"))
        with nc.Block() as block:
            @block.sync
            def _(sp):
                for i, m in enumerate((W_r, W_k, W_v)):
                    sp.dma_start(w_rows[:, i, :], m).then_inc(loaded, 16)
                for i, m in enumerate((mu_r, mu_k)):
                    sp.dma_start(mu[:, i:i + 1], m.rearrange("(d o) -> d o", o=1)).then_inc(loaded, 16)
                rows = out.rearrange("b (t p) d -> p (b t) d", p=P)
                for g in range(G):
                    sp.wait_ge(x_done, g + 1)
                    sp.dma_start(rows[:, 4 * g:4 * g + 4, :], core.x[:, 4 * g:4 * g + 4, :]).then_inc(stored, 16)
                sp.wait_ge(stored, 16 * G)

            @block.tensor
            def _(pe):
                pe.wait_ge(loaded, 80)
                for i in range(3):
                    ins = nc.tensor.transpose(w_ps[:, i * D:i * D + D], w_rows[:, i, :], core.ident[:])
                ins.then_inc(wT_ready, 1)
                pe.wait_ge(wT_copied, 1)
                pe.wait_ge(mixed_ready, 2)
                flat = [m[:].rearrange("p b n -> p (b n)") for m in mixed]
                for g in range(G + 1):
                    if g < G:
                        if g >= 2:
                            pe.wait_ge(relu_done, g - 1)
                            pe.wait_ge(gate_done, g - 1)
                        nc.tensor.matmul(k_ps[g % 2][:], w[:, 1, :], flat[1][:, g * 512:g * 512 + 512], start=True, stop=True).then_inc(k_ready, 1)
                        for t in range(4):
                            ins = nc.tensor.matmul(r_ps[g % 2][:, t * P:t * P + P], flat[0][:, (4 * g + t) * P:(4 * g + t + 1) * P], w[:, 0, :],
                                                   start=True, stop=True)
                        ins.then_inc(r_ready, 1)
                    if g:
                        pe.wait_ge(sq_done, g)
                        if g >= 3:
                            pe.wait_ge(prod_done, g - 2)
                        for t in range(4):
                            ins = nc.tensor.matmul(v_ps[(g - 1) % 2][:, t * P:t * P + P], k_sq[(g - 1) % 2][:, t * P:t * P + P], w[:, 2, :],
                                                   start=True, stop=True)
                        ins.then_inc(v_ready, 1)

            @block.scalar
            def _(act):
                act.wait_ge(wT_ready, 1)
                nc.scalar.activation(w[:].rearrange("p i d -> p (i d)"), w_ps[:, 0:3 * D], ACT.Copy).then_inc(wT_copied, 1)
                for g in range(G):
                    act.wait_ge(k_ready, g + 1)
                    if g >= 2:
                        act.wait_ge(sq_done, g - 1)
                    nc.scalar.activation(k_relu[g % 2][:], k_ps[g % 2][:], ACT.Relu).then_inc(relu_done, 1)
                    act.wait_ge(r_ready, g + 1)
                    if g >= 2:
                        act.wait_ge(prod_done, g - 1)
                    nc.scalar.activation(gate[g % 2][:], r_ps[g % 2][:], ACT.Sigmoid).then_inc(gate_done, 1)

            @block.vector
            def _(dve):
                dve.wait_ge(loaded, 80)
                nc.vector.tensor_scalar(rest[:], mu[:], -1.0, 1.0, ALU.mult, ALU.add).then_inc(rest_ready, 1)
                dve.wait_ge(rest_ready, 1)
                xT = core.xT[:].rearrange("p (b n) -> p b n", b=B)
                for i in (1, 0):
                    nc.vector.tensor_scalar(mixed[i][:], xT, mu[:, i:i + 1], None, ALU.mult).then_inc(scaled, 1)
                for i in (1, 0):
                    dve.wait_ge(scaled, 2 - i)
                    nc.vector.scalar_tensor_tensor(out=mixed[i][:, :, 1:N], in0=xT[:, :, 0:N - 1], scalar=rest[:, i:i + 1],
                                                   in1=mixed[i][:, :, 1:N], op0=ALU.mult, op1=ALU.add).then_inc(mixed_ready, 1)
                for g in range(G + 1):
                    if g < G:
                        dve.wait_ge(relu_done, g + 1)
                        if g >= 2:
                            dve.wait_ge(v_ready, g - 1)
                        nc.vector.tensor_tensor(k_sq[g % 2][:], k_relu[g % 2][:], k_relu[g % 2][:], ALU.mult).then_inc(sq_done, 1)
                    if g:
                        dve.wait_ge(v_ready, g)
                        dve.wait_ge(gate_done, g)
                        p = prod[(g - 1) % 2]
                        nc.vector.tensor_tensor(p[:], v_ps[(g - 1) % 2][:], gate[(g - 1) % 2][:], ALU.mult).then_inc(prod_done, 1)
                        dve.wait_ge(prod_done, g)
                        rows = core.x[:, 4 * (g - 1):4 * g, :]
                        nc.vector.tensor_tensor(rows, rows, p[:].rearrange("p (t d) -> p t d", t=4), ALU.add).then_inc(x_done, 1)


def build(nc, a, c, out):
    with ExitStack() as stack:
        core = Core(nc, stack)
        normalize(nc, core, "n0", first_load=a["L0_attn_x"], affine=(a["L0_attn_ln_gamma"], a["L0_attn_ln_beta"]))
        rotary_attention(nc, core, c["rope"], a["L0_attn_w_qkv"], a["L0_attn_w_out"])
        normalize(nc, core, "n1")
        experts(nc, core, *(a[f"L0_ffn_{n}"] for n in ("switch_w", "switch_b", "w1", "b1", "w2", "b2")))
        normalize(nc, core, "n2")
        block_attention(nc, core, c, *(a[f"L1_attn_{n}"] for n in ("Wq", "bq", "Wk", "bk", "Wv", "bv", "Wo", "bo")))
        normalize(nc, core, "n3")
        channel_mix(nc, core, *(a[f"L1_ffn_{n}"] for n in ("W_r", "W_k", "W_v", "mu_r", "mu_k")), out)


def rope_tables():
    inv = (1.0 / np.float32(10000.0) ** (np.arange(0, DH0, 2, dtype=np.float32) / np.float32(DH0))).astype(np.float32)
    pos = np.maximum(np.arange(N) - 1, 0).astype(np.float32)
    ang = (pos[None, :] * inv[:, None]).astype(np.float32)
    cos, sin = np.tile(np.cos(ang), (4, 1)), np.tile(np.concatenate([-np.sin(ang), np.sin(ang)]), (2, 1))
    s = np.float32(DH0 ** -0.5)
    return np.stack([cos * s, sin * s, cos, sin]).astype(np.float32)


def part_signs():
    low = np.tile(np.repeat(np.array([[0, 0, 1, 1], [0, 1, 0, 1]]), DH1, axis=1), (1, HG))
    return np.stack([1 - 2 * low[0], low[0], 1 - 2 * low[1], low[1]], axis=1).astype(np.float32)


def block_mask():
    blk = np.arange(P) // WIN
    return (blk[:, None] >= blk[None, :]).astype(np.float32)


_INS = ['L0_attn_x', 'L0_attn_ln_gamma', 'L0_attn_ln_beta', 'L0_attn_w_qkv', 'L0_attn_w_out', 'L0_ffn_switch_w', 'L0_ffn_switch_b',
        'L0_ffn_w1', 'L0_ffn_b1', 'L0_ffn_w2', 'L0_ffn_b2', 'L1_attn_Wq', 'L1_attn_bq', 'L1_attn_Wk', 'L1_attn_bk', 'L1_attn_Wv',
        'L1_attn_bv', 'L1_attn_Wo', 'L1_attn_bo', 'L1_ffn_W_r', 'L1_ffn_W_k', 'L1_ffn_W_v', 'L1_ffn_mu_r', 'L1_ffn_mu_k']


def kernel(**inputs):
    import concourse.bacc as _bacc
    from concourse.bass_utils import run_bass_kernel_spmd as _run

    nc = _bacc.Bacc("TRN2", target_bir_lowering=False, num_devices=1)
    arrays, a, c = {}, {}, {}
    for name in _INS:
        arrays[f"in_{name}"] = np.ascontiguousarray(inputs[name])
        a[name] = nc.dram_tensor(f"in_{name}", arrays[f"in_{name}"].shape, F32, kind="ExternalInput").ap()
    for name, value in (("rope", rope_tables()), ("part", part_signs()), ("block_mask", block_mask())):
        arrays[f"const_{name}"] = value
        c[name] = nc.dram_tensor(f"const_{name}", value.shape, F32, kind="ExternalInput").ap()
    out = nc.dram_tensor("out", (B, N, D), F32, kind="ExternalOutput").ap()
    build(nc, a, c, out)
    return _run(nc, [arrays], core_ids=[0]).results[0]["out"]
```

```python
from contextlib import ExitStack

import numpy as np

import concourse.bass as bass
from concourse import mybir

P = 128
B, N, D = 2, 1024, 128
T = B * N // P
TB = N // P
H0, DH0 = 16, 64
PAIRS = B * H0 // 2
HP = H0 // 2
SLOTS = 2 * TB
E, F = 8, 512
FC = F // P
H1, DH1, WIN = 16, 8, 32
SLOT_BLOCKS = T + E
HG = 4
EPS = 1e-5

ALU = mybir.AluOpType
ACT = mybir.ActivationFunctionType
AX = mybir.AxisListType
F32 = mybir.dt.float32
F32R = mybir.dt.float32r
I32 = mybir.dt.int32


def spread(ap, shape):
    return ap.rearrange("p (n o) -> p n o", o=1).broadcast_to(shape)


class Core:

    def __init__(self, nc, stack):
        self.nc, self.stack = nc, stack
        self.x = self.sb("residual", [P, T, D], F32)
        self.xT = self.sb("normed_T", [P, B * N], F32)
        self.ident = self.sb("ident", [P, P], F32)

    def sb(self, name, shape, dt):
        return self.stack.enter_context(self.nc.sbuf_tensor(name, shape, dt))

    def sem(self, name):
        return self.stack.enter_context(self.nc.semaphore(name))


def normalize(nc, core, tag, first_load=None, affine=None, keep=None, prefetch=None):
    LOADS = 4
    rounds = 2 if affine else 1
    with ExitStack() as st:
        sb = lambda n, s: st.enter_context(nc.sbuf_tensor(f"{tag}_{n}", s, F32))
        xn = sb("xn", [P, T, D]) if keep is None else keep
        stats = sb("stats", [P, T, 6])
        moments = sb("moments", [P, T, 2])
        var, root, rstd, newton = (sb(n, [P, T]) for n in ("var", "root", "rstd", "newton"))
        gb = sb("gamma_beta", [P, 2])
        tp = [st.enter_context(nc.psum_tensor(f"{tag}_tp{i}", [P, 512], F32)) for i in range(4)]
        if first_load is not None:
            x_loaded = [core.sem(f"{tag}_x_loaded{i}") for i in range(LOADS)]
            affine_loaded, ident_ready = core.sem(f"{tag}_affine_loaded"), core.sem(f"{tag}_ident_ready")
        dve_step = core.sem(f"{tag}_dve_step")
        var_ready = core.sem(f"{tag}_var_ready")
        root_ready = core.sem(f"{tag}_root_ready")
        xn_ready = core.sem(f"{tag}_xn_ready")
        xnT_ready = core.sem(f"{tag}_xnT_ready")
        TL = T // LOADS

        with nc.Block() as block:
            if first_load is not None:
                @block.sync
                def _(sp):
                    rows = first_load.rearrange("b (t p) d -> p (b t) d", p=P)
                    for i in range(LOADS):
                        sp.dma_start(core.x[:, i * TL:(i + 1) * TL, :], rows[:, i * TL:(i + 1) * TL, :]).then_inc(x_loaded[i], 16)
                    for i, v in enumerate(affine):
                        sp.dma_start(gb[:, i:i + 1], v.rearrange("(d o) -> d o", o=1)).then_inc(affine_loaded, 16)
                    if prefetch is not None:
                        prefetch(sp)

                @block.gpsimd
                def _(pool):
                    nc.gpsimd.memset(core.ident[:], 0.0).then_inc(ident_ready, 1)
                    pool.wait_ge(ident_ready, 1)
                    nc.gpsimd.affine_select(out=core.ident[:], in_=core.ident[:], compare_op=ALU.not_equal, fill=1.0,
                                            base=0, pattern=[[-1, P]], channel_multiplier=1).then_inc(ident_ready, 1)

            if prefetch is not None and first_load is None:
                @block.sync
                def _(sp):
                    prefetch(sp)

            @block.vector
            def _(dve):
                steps = [0]

                def step(ins):
                    steps[0] += 1
                    ins.then_inc(dve_step, 1)
                    dve.wait_ge(dve_step, steps[0])

                for k in range(rounds):
                    src = (core.x, xn)[k]
                    for t in range(T):
                        if first_load is not None and k == 0 and t % TL == 0:
                            dve.wait_ge(x_loaded[t // TL], 16)
                        ins = nc.vector.bn_stats(out=stats[:, t, :], in_=src[:, t, :])
                    step(ins)
                    for t in range(T):
                        ins = nc.vector.bn_aggr(out=moments[:, t, :], in_=stats[:, t, :])
                    step(ins)
                    nc.vector.tensor_scalar(var[:], moments[:, :, 1], EPS, None, ALU.add).then_inc(var_ready, 1)
                    dve.wait_ge(root_ready, k + 1)
                    step(nc.vector.reciprocal(rstd[:], root[:]))
                    step(nc.vector.tensor_tensor(newton[:], rstd[:], rstd[:], ALU.mult))
                    step(nc.vector.tensor_tensor(newton[:], newton[:], var[:], ALU.mult))
                    step(nc.vector.tensor_scalar(newton[:], newton[:], -0.5, 1.5, ALU.mult, ALU.add))
                    step(nc.vector.tensor_tensor(rstd[:], rstd[:], newton[:], ALU.mult))
                    for t in range(T):
                        ins = nc.vector.tensor_scalar(xn[:, t, :], src[:, t, :], moments[:, t, 0:1], rstd[:, t:t + 1], ALU.subtract, ALU.mult)
                        if k == rounds - 1 and t % 4 == 3:
                            ins.then_inc(xn_ready, 1)
                    if k < rounds - 1:
                        step(ins)

            @block.tensor
            def _(pe):
                if first_load is not None:
                    pe.wait_ge(ident_ready, 2)
                for t in range(T):
                    if t % 4 == 0:
                        pe.wait_ge(xn_ready, t // 4 + 1)
                    ins = nc.tensor.transpose(tp[t // 4][:, t % 4 * P:(t % 4 + 1) * P], xn[:, t, :], core.ident[:])
                    if t % 4 == 3:
                        ins.then_inc(xnT_ready, 1)

            @block.scalar
            def _(act):
                for k in range(rounds):
                    act.wait_ge(var_ready, k + 1)
                    nc.scalar.activation(root[:], var[:], ACT.Sqrt).then_inc(root_ready, 1)
                if affine:
                    act.wait_ge(affine_loaded, 32)
                for i in range(T // 4):
                    act.wait_ge(xnT_ready, i + 1)
                    dst = core.xT[:, i * 512:(i + 1) * 512]
                    if affine:
                        nc.scalar.activation(dst, tp[i][:], ACT.Identity, bias=gb[:, 1:2], scale=gb[:, 0:1])
                    else:
                        nc.scalar.activation(dst, tp[i][:], ACT.Copy)


def rotary_attention(nc, core, x, affine, rope, w_qkv, w_out, slots_x):
    with ExitStack() as st:
        sb = lambda n, s, dt=F32: st.enter_context(nc.sbuf_tensor(f"a0_{n}", s, dt))
        ps = lambda n, s: st.enter_context(nc.psum_tensor(f"a0_{n}", s, F32))
        sem = lambda n: core.sem(f"a0_{n}")

        tables = sb("tables", [P, 4, N])
        xn_cur = sb("xn_cur", [P, N])
        w_cur = sb("w_cur", [P, 3, P])
        wo_cur = sb("wo_cur", [P, D])
        raw = [sb("q_raw", [P, N]), sb("k_raw", [P, N])]
        rot = [sb("q_rot", [P, N]), sb("k_rot", [P, N])]
        hi = [sb("q_hi", [P, N], F32R), sb("k_hi", [P, N], F32R)]
        lo = [sb("q_lo", [P, N], F32R), sb("k_lo", [P, N], F32R)]
        q_stack = [[sb(f"q_stack{i}{h}", [P, N], F32R) for h in "ab"] for i in range(2)]
        k_stack = [[[sb(f"k_stack{i}{h}{part}", [P, N], F32R) for part in ("h", "l")] for h in "ab"] for i in range(2)]
        v = [sb(f"v{i}", [P, TB, P]) for i in range(2)]
        probs = [sb(f"probs{i}", [P, N]) for i in range(4)]
        probs_T = [sb(f"probs_T{i}", [P, 2, TB, 256]) for i in range(2)]
        negmax = sb("negmax", [P, SLOTS])
        den = sb("den", [P, SLOTS])
        rden_col = sb("rden_col", [P, 4])
        rden = sb("rden", [P, 4, 64])
        ones = sb("ones", [P, 4, 64])
        rden_b = sb("rden_b", [P, 256])
        attn_T = sb("attn_T", [P, 256])
        zero_rows = sb("zero_rows", [P, 1, D])

        tables_loaded, first_w_loaded = sem("tables_loaded"), sem("first_w_loaded")

        def load_first(sp):
            sp.dma_start(w_cur[:], w_qkv.rearrange("d (c n) -> d c n", c=3)[:, :, 0:P]).then_inc(first_w_loaded, 16)
            sp.dma_start(tables[:], rope.rearrange("t p n -> p t n")).then_inc(tables_loaded, 16)

        normalize(nc, core, "n0", first_load=x, affine=affine, prefetch=load_first)

        score_ps = [ps(f"score{i}", [P, N]) for i in range(2)]
        tr_ps = [ps(f"tr{i}", [P, 512]) for i in range(2)]
        out_ps = ps("out", [P, 512])
        misc_ps = ps("misc", [P, 512])

        zeroed, slots_cleared = sem("zeroed"), sem("slots_cleared")
        operands_loaded, wo_loaded = sem("operands_loaded"), sem("wo_loaded")
        swapped = [sem("q_swapped"), sem("k_swapped")]
        rotated = [sem("q_rotated"), sem("k_rotated")]
        summed = [sem("q_summed"), sem("k_summed")]
        hi_ready = [sem("q_hi_ready"), sem("k_hi_ready")]
        lo_ready = [sem("q_lo_ready"), sem("k_lo_ready")]
        stacked = [sem("q_stacked"), sem("k_stacked")]
        STACKED = [64, 128]
        scores_ready, negmax_ready, probs_ready = sem("scores_ready"), sem("negmax_ready"), sem("probs_ready")
        tr_ready = [sem("tr_lo_ready"), sem("tr_hi_ready")]
        tr_copied = [sem("tr_lo_copied"), sem("tr_hi_copied")]
        misc_ready, misc_free = sem("misc_ready"), sem("misc_free")
        pv_done, attn_ready, rden_ready, rden_col_ready = (sem(n) for n in ("pv_done", "attn_ready", "rden_ready", "rden_col_ready"))

        ITEM_SLOTS = [0, 1, 2, 3, 4, 5, 6, 7, 8, 9, 10, 11, 14, 15]
        ITEMS, FIRST_ITEMS = len(ITEM_SLOTS), 6
        ITEM = {s: FIRST_ITEMS + i for i, s in enumerate(ITEM_SLOTS)}
        LAST_ITEM = {2: FIRST_ITEMS, 3: FIRST_ITEMS + 1, 7: FIRST_ITEMS + 2}
        PAIRS2 = PAIRS // 2

        def first_bank(k):
            return score_ps[k // 2][:, k % 2 * 512:k % 2 * 512 + 512] if k < 4 else (misc_ps, tr_ps[0])[k - 4][:]

        def unit(s):
            return 2 * (s // 4) + s % 4 // 2, s % 2

        def progress(it, par):
            return lambda m, c: it * (2 * m) + (par * m + c)

        LAST = lambda m, c: m * PAIRS + c
        BEFORE = lambda m, c: -m + c

        with nc.Block() as block:
            @block.sync
            def _(sp):
                def load_operands(col, row):
                    sp.dma_start(w_cur[:], w_qkv.rearrange("d (c n) -> d c n", c=3)[:, :, bass.ds(col, P)])\
                        .then_inc(operands_loaded, 16)
                    sp.dma_start(xn_cur[:], core.xT[:, bass.ds(row, N)]).then_inc(operands_loaded, 16)

                def swap_halves(i):
                    for r in range(4):
                        sp.dma_start(rot[i][32 * r:32 * r + 32, :], raw[i][32 * (r ^ 1):32 * (r ^ 1) + 32, :])\
                            .then_inc(swapped[i], 16)

                def stack_q(par):
                    for h in range(2):
                        rows = slice(64 * h, 64 * h + 64)
                        sp.dma_start(q_stack[par][h][0:64, :].bitcast(F32), hi[0][rows, :].bitcast(F32)).then_inc(stacked[0], 16)
                        sp.dma_start(q_stack[par][h][64:128, :].bitcast(F32), lo[0][rows, :].bitcast(F32)).then_inc(stacked[0], 16)

                def stack_k(par):
                    for h in range(2):
                        rows = slice(64 * h, 64 * h + 64)
                        for part, src in enumerate((hi[1], lo[1])):
                            for half in range(2):
                                sp.dma_start(k_stack[par][h][part][64 * half:64 * half + 64, :].bitcast(F32), src[rows, :].bitcast(F32))\
                                    .then_inc(stacked[1], 16)

                sp.wait_ge(misc_free, 2)
                swap_halves(0)
                sp.wait_ge(misc_free, 4)
                swap_halves(1)
                sp.wait_ge(misc_ready, FIRST_ITEMS)
                load_operands(P, 0)
                sp.wait_ge(lo_ready[0], 1)
                stack_q(0)
                sp.wait_ge(lo_ready[1], 1)
                stack_k(0)
                with sp.Fori(0, PAIRS2) as it:
                    for par in range(2):
                        at = progress(it, par)
                        wo_row = sp.snap(((it * 2 + par) % HP) * P)
                        next_col = sp.snap((it * 2 + par + 2) % HP * P)
                        next_row = sp.snap((it * 2 + par + 2) // HP % B * N)
                        for i, slot in ((0, 1), (1, 5)):
                            sp.wait_ge(misc_free, at(ITEMS, ITEM[slot] + 1))
                            sp.wait_ge(summed[i], at(1, 1))
                            swap_halves(i)
                        sp.wait_ge(lo_ready[0], at(1, 2))
                        stack_q(1 - par)
                        sp.wait_ge(misc_ready, at(ITEMS, ITEM[7] + 1))
                        sp.dma_start(wo_cur[:], w_out[bass.ds(wo_row, P), :]).then_inc(wo_loaded, 16)
                        sp.wait_ge(misc_ready, at(ITEMS, ITEM[9] + 1))
                        load_operands(next_col, next_row)
                        sp.wait_ge(lo_ready[1], at(1, 2))
                        stack_k(1 - par)
                sp.wait_ge(operands_loaded, 32 * (PAIRS + 1))
                sp.wait_ge(stacked[0], STACKED[0] * (PAIRS + 1))
                sp.wait_ge(stacked[1], STACKED[1] * (PAIRS + 1))

            @block.gpsimd
            def _(pool):
                nc.gpsimd.memset(probs[3][:], 0.0)
                nc.gpsimd.memset(probs_T[0][:], 0.0)
                nc.gpsimd.memset(probs_T[1][:], 0.0)
                nc.gpsimd.memset(v[1][:], 0.0)
                nc.gpsimd.memset(den[:], 1.0)
                nc.gpsimd.memset(rden_b[:], 0.0)
                nc.gpsimd.memset(ones[:], 1.0)
                nc.gpsimd.memset(zero_rows[:], 0.0)
                nc.gpsimd.memset(wo_cur[:], 0.0).then_inc(zeroed, 1)
                pool.wait_ge(zeroed, 1)
                nc.gpsimd.dma_start(slots_x.rearrange("(j p) d -> p j d", p=P), zero_rows[:].broadcast_to([P, SLOT_BLOCKS, D]))\
                    .then_inc(slots_cleared, 16)

                def spread_rden(at, grp):
                    pool.wait_ge(rden_col_ready, at(4, grp + 1))
                    nc.gpsimd.tensor_tensor(rden[:], spread(rden_col[:], [P, 4, 64]), ones[:], ALU.mult).then_inc(rden_ready, 1)

                def sums_and_rests(at, parts=(0, 1)):
                    for i in parts:
                        pool.wait_ge(rotated[i], at(2, 4))
                        nc.gpsimd.tensor_tensor(raw[i][:], raw[i][:], rot[i][:], ALU.add).then_inc(summed[i], 1)
                        pool.wait_ge(hi_ready[i], at(1, 2))
                        nc.gpsimd.tensor_tensor(lo[i][:], raw[i][:], hi[i][:].bitcast(F32), ALU.subtract)\
                            .then_inc(lo_ready[i], 1)

                sums_and_rests(BEFORE)
                with pool.Fori(0, PAIRS2) as it:
                    for par in range(2):
                        at = progress(it, par)
                        spread_rden(at, 0)
                        spread_rden(at, 1)
                        sums_and_rests(at, (0,))
                        spread_rden(at, 2)
                        sums_and_rests(at, (1,))
                        spread_rden(at, 3)
                spread_rden(LAST, 0)
                pool.wait_ge(slots_cleared, 16)

            @block.tensor
            def _(pe):
                def project_T(i, half, to=misc_ps[:], xn=xn_cur):
                    nc.tensor.matmul(to, w_cur[:, i, :], xn[:, half * 512:half * 512 + 512],
                                     start=True, stop=True).then_inc(misc_ready, 1)

                def project_v(half, to=misc_ps[:], xn=xn_cur):
                    for t in range(4):
                        last = nc.tensor.matmul(to[:, t * P:t * P + P], xn[:, (4 * half + t) * P:(4 * half + t + 1) * P],
                                                w_cur[:, 2, :], start=True, stop=True)
                    last.then_inc(misc_ready, 1)

                def scores(s, par):
                    tile, h = unit(s)
                    for half in range(2):
                        cols = slice(half * 512, half * 512 + 512)
                        for part in range(2):
                            last = nc.tensor.matmul(score_ps[s % 2][:, cols], q_stack[par][h][:, tile * P:tile * P + P],
                                                    k_stack[par][h][part][:, cols], start=part == 0, stop=part == 1)
                    last.then_inc(scores_ready, 1)

                def transposes(s):
                    for k in range(TB):
                        last = nc.tensor.transpose(tr_ps[k // 4][:, k % 4 * P:k % 4 * P + P],
                                                   probs[s % 4][:, k * P:k * P + P], core.ident[:])
                        if k % 4 == 3:
                            last.then_inc(tr_ready[k // 4], 1)

                def slot(s, par, at, item, last=False):
                    if not last or s == 0:
                        pe.wait_ge(probs_ready, at(SLOTS, s))
                    if not last:
                        if s == SLOTS - 1:
                            for i in range(2):
                                pe.wait_ge(stacked[i], at(STACKED[i], 2 * STACKED[i]))
                            scores(0, 1 - par)
                        else:
                            scores(s + 1, par)
                    if not last or s == 0:
                        for i in range(2):
                            pe.wait_ge(tr_copied[i], at(SLOTS, s))
                        transposes(s - 1)
                    if s in item:
                        pe.wait_ge(misc_free, at(ITEMS, item[s]))
                        if s in (0, 1, 4, 5):
                            if s == 0:
                                pe.wait_ge(operands_loaded, at(32, 32))
                            project_T(s // 4, s % 2)
                        elif s in (8, 9):
                            project_v(s - 8)
                        elif s % 4 == 2:
                            pe.wait_ge(rden_ready, at(4, s // 4 + 1))
                            for q in range(2):
                                ins = nc.tensor.transpose(misc_ps[:, q * P:q * P + P],
                                                          rden[:, 2 * q:2 * q + 2, :].rearrange("p h d -> p (h d)"), core.ident[:])
                            ins.then_inc(misc_ready, 1)
                        else:
                            pe.wait_ge(attn_ready, at(4, s // 4 + 1))
                            pe.wait_ge(wo_loaded, at(16, 16 if s > 7 else 0))
                            for q in range(2):
                                ins = nc.tensor.matmul(misc_ps[:, q * P:q * P + P], attn_T[:, q * P:q * P + P], wo_cur[:],
                                                       start=True, stop=True)
                            ins.then_inc(misc_ready, 1)
                    if not last or s < 5:
                        r, grp = (s - 5) % 4, (s - 5) // 4 % 2
                        if r == 0:
                            for i in range(2):
                                pe.wait_ge(tr_copied[i], at(SLOTS, s))
                            pe.wait_ge(attn_ready, at(4, s // 4 + 1))
                            if s == 5:
                                pe.wait_ge(misc_free, at(ITEMS, 0))
                        for k in (2 * r, 2 * r + 1):
                            for h in range(2):
                                ins = nc.tensor.matmul(out_ps[64 * h:64 * h + 64, 0:256],
                                                       v[par if s >= 5 else 1 - par][:, k, 64 * h:64 * h + 64],
                                                       probs_T[grp][:, h, k, :], start=k == 0, stop=k == TB - 1)
                        if r == 3:
                            ins.then_inc(pv_done, 1)

                pe.wait_ge(first_w_loaded, 16)
                for k in range(FIRST_ITEMS):
                    if k < 4:
                        project_T(k // 2, k % 2, first_bank(k), core.xT)
                    else:
                        project_v(k - 4, first_bank(k), core.xT)
                pe.wait_ge(zeroed, 1)
                for h in range(2):
                    for k in range(6):
                        nc.tensor.matmul(out_ps[64 * h:64 * h + 64, 0:256], v[1][:, k, 64 * h:64 * h + 64],
                                         probs_T[0][:, h, k, :], start=k == 0, stop=False)
                pe.wait_ge(misc_free, FIRST_ITEMS)
                for i in range(2):
                    pe.wait_ge(stacked[i], STACKED[i])
                scores(0, 0)
                with pe.Fori(0, PAIRS2) as it:
                    for par in range(2):
                        for s in range(SLOTS):
                            slot(s, par, progress(it, par), ITEM)
                for s in range(8):
                    slot(s, 0, LAST, LAST_ITEM, last=True)

            @block.scalar
            def _(act):
                def copy_item(dst, src=misc_ps[:]):
                    nc.scalar.activation(dst, src, ACT.Copy).then_inc(misc_free, 1)

                def copy_tr(s, i):
                    tile, h = unit((s - 1) % SLOTS)
                    nc.scalar.activation(probs_T[(s - 1) // 4 % 2][:, h, 4 * i:4 * i + 4, tile % 2 * P:tile % 2 * P + P],
                                         tr_ps[i][:].rearrange("p (k q) -> p k q", k=4), ACT.Copy).then_inc(tr_copied[i], 1)

                def slot(s, par, at, item, last=False):
                    if not last:
                        act.wait_ge(negmax_ready, at(SLOTS, s + 1))
                        nc.scalar.activation(probs[s % 4][:], score_ps[s % 2][:], ACT.Exp, bias=negmax[:, s:s + 1],
                                             accum_out=den[:, s:s + 1]).then_inc(probs_ready, 1)
                    if not last or s == 0:
                        for i in range(2):
                            act.wait_ge(tr_ready[i], at(SLOTS, s + 1))
                            copy_tr(s, i)
                    if s in item and s % 4 != 3:
                        act.wait_ge(misc_ready, at(ITEMS, item[s] + 1))
                        if s in (0, 1, 4, 5):
                            i = s // 4
                            if s % 2 == 0:
                                act.wait_ge(lo_ready[i], at(1, 1))
                            copy_item(raw[i][:, s % 2 * 512:s % 2 * 512 + 512])
                        elif s in (8, 9):
                            copy_item(v[1 - par][:, 4 * (s - 8):4 * (s - 8) + 4, :].rearrange("p t n -> p (t n)"))
                        else:
                            copy_item(rden_b[:], misc_ps[:, 0:256])

                for k in range(FIRST_ITEMS):
                    act.wait_ge(misc_ready, k + 1)
                    copy_item(raw[k // 2][:, k % 2 * 512:k % 2 * 512 + 512] if k < 4 else
                              v[0][:, 4 * (k - 4):4 * (k - 4) + 4, :].rearrange("p t n -> p (t n)"), first_bank(k))
                act.wait_ge(zeroed, 1)
                with act.Fori(0, PAIRS2) as it:
                    for par in range(2):
                        for s in range(SLOTS):
                            slot(s, par, progress(it, par), ITEM)
                for s in range(8):
                    slot(s, 0, LAST, LAST_ITEM, last=True)

            @block.vector
            def _(dve):
                def row_max(s):
                    nc.vector.tensor_reduce(negmax[:, s:s + 1], score_ps[s % 2][:], axis=AX.X, op=ALU.max, negate=True)\
                        .then_inc(negmax_ready, 1)

                def rotate(i, j):
                    t = (raw, rot)[j][i]
                    nc.vector.tensor_tensor(t[:], t[:], tables[:, 2 * i + j, :], ALU.mult).then_inc(rotated[i], 1)

                def split(i):
                    nc.vector.tensor_copy(hi[i][:], raw[i][:]).then_inc(hi_ready[i], 1)

                def slot(s, par, at, batch, item, last=False):
                    if s % 4 == 1:
                        dve.wait_ge(pv_done, at(4, s // 4 + 1))
                        dve.wait_ge(misc_free, at(ITEMS, item[s - 3] + 1 if s > 1 else FIRST_ITEMS - 1))
                        nc.vector.tensor_tensor(attn_T[:], out_ps[:, 0:256], rden_b[:], ALU.mult).then_inc(attn_ready, 1)
                    if not last:
                        dve.wait_ge(scores_ready, at(SLOTS, s + 2))
                        row_max((s + 1) % SLOTS)
                    if s % 4 == 0 and (not last or s == 0):
                        dve.wait_ge(probs_ready, at(SLOTS, s))
                        c = 4 * ((s // 4 - 1) % 4)
                        nc.vector.reciprocal(rden_col[:], den[:, c:c + 4]).then_inc(rden_col_ready, 1)
                    if s % 4 == 3:
                        dve.wait_ge(misc_ready, at(ITEMS, item[s] + 1))
                        rows = core.x[:, bass.ds(batch[s > 7] * TB + 2 * ((s // 4 + 2) % 4), 2), :]
                        nc.vector.tensor_tensor(rows, misc_ps[:, 0:256].rearrange("p (t d) -> p t d", t=2), rows, ALU.add)\
                            .then_inc(misc_free, 1)
                    if not last:
                        if s in (3, 7):
                            i = s // 4
                            dve.wait_ge(swapped[i], at(64, 128))
                            rotate(i, 0)
                        if s in (4, 8):
                            rotate(s // 4 - 1, 1)
                        if s in (6, 10):
                            i = s // 8
                            dve.wait_ge(summed[i], at(1, 2))
                            dve.wait_ge(stacked[i], at(STACKED[i], STACKED[i]))
                            split(i)

                dve.wait_ge(tables_loaded, 16)
                for i in range(2):
                    dve.wait_ge(swapped[i], 64)
                    rotate(i, 0)
                    rotate(i, 1)
                    dve.wait_ge(summed[i], 1)
                    split(i)
                dve.wait_ge(scores_ready, 1)
                row_max(0)
                with dve.Fori(0, PAIRS2) as it:
                    for par in range(2):
                        batch = (((it + 2 * HP // 2 - 1) // (HP // 2)) % B if par == 0 else it // (HP // 2), it // (HP // 2))
                        for s in range(SLOTS):
                            slot(s, par, progress(it, par), batch, ITEM)
                for s in range(8):
                    slot(s, 0, LAST, (B - 1, 0), LAST_ITEM, last=True)


def experts(nc, core, sw, sb_, w1, b1, w2, b2, slots_x, slots_y):
    NB = SLOT_BLOCKS
    STEPS = 4
    KMAX = B * N // P
    with ExitStack() as st:
        sb = lambda n, s, dt=F32: st.enter_context(nc.sbuf_tensor(f"f0_{n}", s, dt))
        ps = lambda n, s=(P, 512): st.enter_context(nc.psum_tensor(f"f0_{n}_ps", list(s), F32))
        sem = lambda n: core.sem(f"f0_{n}")
        xn = sb("xn", [P, T, D])
        normalize(nc, core, "n1", keep=xn)

        switch, switch_b = sb("switch", [P, E]), sb("switch_b", [P, E])
        w1_all, w2_all = sb("w1_all", [P, E, F]), sb("w2_all", [P, E * FC, D])
        b1_all, b2_all = sb("b1_all", [P, E, F]), sb("b2_all", [P, E, D])
        logits, shifted, expd, order, cand, route = (sb(n, [P, T, E]) for n in ("logits", "shifted", "expd", "order", "cand", "route"))
        iota, expert_before = sb("iota", [P, E]), sb("expert_before", [P, E, E])
        block_starts, block_iota = sb("block_starts", [P, KMAX]), sb("block_iota", [P, NB + 2])
        earlier, ones = sb("earlier", [P, P]), sb("ones", [P, P])
        top, total, first, p_max = (sb(n, [P, T]) for n in ("top", "total", "first", "p_max"))
        scan = [sb(f"scan{i}", [P, T, E]) for i in range(2)]
        full_blocks = sb("full_blocks", [P, E, KMAX])
        blocks, first_block, end_block = (sb(n, [P, E]) for n in ("blocks", "first_block", "end_block"))
        ended, block_expert = sb("ended", [P, NB + 2, E]), sb("block_expert", [P, NB + 2])
        block_expert_i = sb("block_expert_i", [P, NB + 2], I32)
        place, place_i = sb("place", [P, T]), sb("place_i", [P, T], I32)
        x_blk = [sb(f"x_blk{i}", [P, D]) for i in range(2)]
        xT_blk = [sb(f"xT_blk{i}", [P, P]) for i in range(2)]
        biased = [sb(f"biased{i}", [P, F]) for i in range(2)]
        hidden = [sb(f"hidden{i}", [P, F]) for i in range(2)]
        hidden_T = [sb(f"hidden_T{i}", [P, FC, P]) for i in range(2)]
        y_blk = [sb(f"y_blk{i}", [P, D]) for i in range(2)]
        y_rows = sb("y_rows", [P, T, D])
        route_ps, count_ps = ps("route"), ps("count")
        x_ps, tr_ps, y_ps = ps("x"), ps("tr"), ps("y")
        h_ps = [ps(f"h{i}") for i in range(2)]

        small_loaded, weights_loaded = sem("small_loaded"), sem("weights_loaded")
        consts_ready, logits_ready, dve_step = sem("consts_ready"), sem("logits_ready"), sem("dve_step")
        shifted_ready, expd_ready, route_ready, counted = (sem(n) for n in ("shifted_ready", "expd_ready", "route_ready", "counted"))
        places_ready, blocks_ready, sorted_, junk_cleared = (sem(n) for n in ("places_ready", "blocks_ready", "sorted", "junk_cleared"))
        x_landed = [sem("even_x_landed"), sem("odd_x_landed")]
        x_ready, xT_copied, h_ready, h_biased, gelu_done = (sem(n) for n in ("x_ready", "xT_copied", "h_ready", "h_biased", "gelu_done"))
        tr_ready, tr_copied, y_ready, y_kept = (sem(n) for n in ("tr_ready", "tr_copied", "y_ready", "y_kept"))
        y_stored = [sem("even_y_stored"), sem("odd_y_stored")]
        fetched = [sem(f"fetched{i}") for i in range(4)]

        with nc.Block() as block:
            @block.sync
            def _(sp):
                sp.dma_start(switch[:], sw).then_inc(small_loaded, 16)
                sp.dma_start(switch_b[:], sb_.rearrange("(o e) -> o e", o=1).broadcast_to([P, E])).then_inc(small_loaded, 16)
                sp.dma_start(w1_all[:], w1.rearrange("e d f -> d e f")).then_inc(weights_loaded, 16)
                sp.dma_start(b1_all[:].rearrange("p e f -> p (e f)"), b1.rearrange("(o e) f -> o (e f)", o=1).broadcast_to([P, E * F])).then_inc(weights_loaded, 16)
                sp.dma_start(w2_all[:], w2.rearrange("e (c p) d -> p (e c) d", p=P)).then_inc(weights_loaded, 16)
                sp.dma_start(b2_all[:].rearrange("p e d -> p (e d)"), b2.rearrange("(o e) d -> o (e d)", o=1).broadcast_to([P, E * D])).then_inc(weights_loaded, 16)

                def load(row, par):
                    sp.dma_start(x_blk[par][:], slots_x[row, :]).then_inc(x_landed[par], 16)

                def store(row, par):
                    sp.dma_start(slots_y[row, :], y_blk[par][:]).then_inc(y_stored[par], 16)

                sp.wait_ge(sorted_, 16 * T)
                for j in range(4):
                    if j >= 2:
                        sp.wait_ge(x_ready, j - 1)
                    load(slice(j * P, j * P + P), j % 2)
                with sp.Fori(0, NB // 2) as it:
                    for par in range(2):
                        j = it * 2 + par
                        next_row = sp.snap((j + 4) % NB * P)
                        done_row = sp.snap((j + NB) % (NB + 1) * P)
                        sp.wait_ge(x_ready, j + 3)
                        load(bass.ds(next_row, P), par)
                        sp.wait_ge(y_kept, j + 1)
                        store(bass.ds(done_row, P), 1 - par)
                sp.wait_ge(y_kept, NB + 1)
                store(slice((NB - 1) * P, NB * P), (NB - 1) % 2)
                for i in range(2):
                    sp.wait_ge(x_landed[i], 16 * (NB // 2 + 2))

            @block.gpsimd
            def _(pool):
                exact = dict(channel_multiplier=0, allow_small_or_imprecise_dtypes=True)
                nc.gpsimd.iota(iota[:], pattern=[[1, E]], base=-E, **exact)
                nc.gpsimd.iota(block_starts[:], pattern=[[P, KMAX]], base=0, **exact)
                nc.gpsimd.iota(block_iota[:], pattern=[[1, NB + 2]], base=-1, **exact)
                nc.gpsimd.memset(ones[:], 1.0).then_inc(consts_ready, 1)
                pool.wait_ge(consts_ready, 1)
                nc.gpsimd.affine_select(out=earlier[:], in_=ones[:], compare_op=ALU.is_gt, fill=0.0, base=0, pattern=[[1, P]], channel_multiplier=-1)
                nc.gpsimd.affine_select(out=expert_before[:], in_=ones[:, 0:E * E].rearrange("p (e o) -> p e o", e=E), compare_op=ALU.is_gt, fill=0.0,
                                        base=0, pattern=[[1, E], [-1, E]], channel_multiplier=0).then_inc(consts_ready, 1)
                nc.gpsimd.memset(hidden_T[1][:], 0.0).then_inc(junk_cleared, 1)
                pool.wait_ge(places_ready, 1)
                for t in range(T):
                    nc.gpsimd.indirect_dma_start(slots_x[:], bass.IndirectOffsetOnAxis(ap=place_i[:, t:t + 1], axis=0), xn[:, t, :], None).then_inc(sorted_, 16)
                for i in range(2):
                    pool.wait_ge(y_stored[i], 16 * (NB // 2 + (1 if i == (NB - 1) % 2 else 0)))
                for t in range(T):
                    nc.gpsimd.indirect_dma_start(y_rows[:, t, :], None, slots_y[:], bass.IndirectOffsetOnAxis(ap=place_i[:, t:t + 1], axis=0))\
                        .then_inc(fetched[t // 4], 16)

            @block.tensor
            def _(pe):
                flat1, flat2 = w1_all[:].rearrange("p e f -> p (e f)"), w2_all[:].rearrange("p c d -> p (c d)")

                def transpose_x(par):
                    nc.tensor.transpose(x_ps[:, 0:P], x_blk[par][:], core.ident[:]).then_inc(x_ready, 1)

                def hidden_of(e, par):
                    nc.tensor.matmul(h_ps[par][:], xT_blk[par][:], flat1[:, bass.ds(e * F, F)], start=True, stop=True).then_inc(h_ready, 1)

                def transpose_hidden(par):
                    for f in range(FC):
                        ins = nc.tensor.transpose(tr_ps[:, f * P:f * P + P], hidden[par][:, f * P:f * P + P], core.ident[:])
                    ins.then_inc(tr_ready, 1)

                def out_of(e, par):
                    for f in range(FC):
                        ins = nc.tensor.matmul(y_ps[:, 0:D], hidden_T[par][:, f, :], flat2[:, bass.ds(e * (FC * D) + f * D, D)], start=f == 0, stop=f == FC - 1)
                    ins.then_inc(y_ready, 1)

                def expert(i):
                    return pe.value_load(block_expert_i[0:1, bass.ds(i, 1)] if not isinstance(i, int) else block_expert_i[0:1, i:i + 1], min_val=0, max_val=E - 1)

                pe.wait_ge(small_loaded, 32)
                for t in range(T):
                    ins = nc.tensor.matmul(route_ps[:, t * E:t * E + E], core.xT[:, t * P:t * P + P], switch[:], start=True, stop=True)
                ins.then_inc(logits_ready, 1)
                pe.wait_ge(consts_ready, 2)
                pe.wait_ge(route_ready, 1)
                flat = route[:].rearrange("p t e -> p (t e)")
                nc.tensor.matmul(count_ps[:, 0:T * E], ones[:], flat, start=True, stop=True)
                nc.tensor.matmul(count_ps[:, T * E:2 * T * E], earlier[:], flat, start=True, stop=True).then_inc(counted, 1)
                pe.wait_ge(x_landed[0], 16)
                transpose_x(0)
                pe.wait_ge(x_landed[1], 16)
                pe.wait_ge(xT_copied, 1)
                transpose_x(1)
                pe.wait_ge(weights_loaded, 64)
                pe.wait_ge(blocks_ready, 1)
                hidden_of(expert(1), 0)
                pe.wait_ge(junk_cleared, 1)
                with pe.Fori(0, NB // STEPS) as it:
                    for k in range(STEPS):
                        j, par = it * STEPS + k, k % 2
                        e_next, e_before = expert(j + 2), expert(j)
                        pe.wait_ge(xT_copied, j + 2)
                        pe.wait_ge(h_biased, j + 1)
                        hidden_of(e_next, 1 - par)
                        pe.wait_ge(x_landed[par], it * (8 * STEPS) + (16 * (k // 2) + 32))
                        transpose_x(par)
                        pe.wait_ge(gelu_done, j + 1)
                        pe.wait_ge(tr_copied, j)
                        transpose_hidden(par)
                        pe.wait_ge(y_kept, j)
                        out_of(e_before, 1 - par)
                pe.wait_ge(tr_copied, NB)
                pe.wait_ge(y_kept, NB)
                out_of(expert(NB), (NB - 1) % 2)

            @block.scalar
            def _(act):
                def copy_x(par):
                    nc.scalar.activation(xT_blk[par][:], x_ps[:, 0:P], ACT.Copy).then_inc(xT_copied, 1)

                def gelu(par):
                    nc.scalar.activation(hidden[par][:], biased[par][:], ACT.Gelu_apprx_tanh).then_inc(gelu_done, 1)

                act.wait_ge(shifted_ready, 1)
                nc.scalar.activation(expd[:], shifted[:], ACT.Exp).then_inc(expd_ready, 1)
                for j in range(2):
                    act.wait_ge(x_ready, j + 1)
                    copy_x(j)
                act.wait_ge(h_biased, 1)
                gelu(0)
                with act.Fori(0, NB // STEPS) as it:
                    for k in range(STEPS):
                        j, par = it * STEPS + k, k % 2
                        act.wait_ge(x_ready, j + 3)
                        act.wait_ge(h_ready, j + 1)
                        copy_x(par)
                        act.wait_ge(h_biased, j + 2)
                        act.wait_ge(tr_ready, j)
                        gelu(1 - par)

            @block.vector
            def _(dve):
                steps = [0]

                def step(ins):
                    steps[0] += 1
                    ins.then_inc(dve_step, 1)
                    dve.wait_ge(dve_step, steps[0])

                def expert(i):
                    return dve.value_load(block_expert_i[0:1, bass.ds(i, 1)] if not isinstance(i, int) else block_expert_i[0:1, i:i + 1], min_val=0, max_val=E - 1)

                def add_b1(e, par):
                    rows = b1_all[:].rearrange("p e f -> p (e f)")[:, bass.ds(e * F, F)]
                    nc.vector.tensor_tensor(biased[par][:], h_ps[par][:], rows, ALU.add).then_inc(h_biased, 1)

                def keep_y(e, par):
                    rows = b2_all[:].rearrange("p e d -> p (e d)")[:, bass.ds(e * D, D)]
                    nc.vector.tensor_tensor(y_blk[par][:], y_ps[:, 0:D], rows, ALU.add).then_inc(y_kept, 1)

                shape = [P, T, E]
                by_tile = lambda ap: ap.rearrange("p (o e) -> p o e", o=1).broadcast_to(shape)
                dve.wait_ge(small_loaded, 32)
                dve.wait_ge(logits_ready, 1)
                dve.wait_ge(consts_ready, 2)
                step(nc.vector.tensor_tensor(logits[:], route_ps[:, 0:T * E].rearrange("p (t e) -> p t e", t=T), by_tile(switch_b[:]), ALU.add))
                step(nc.vector.tensor_reduce(top[:], logits[:], axis=AX.X, op=ALU.max))
                nc.vector.tensor_tensor(shifted[:], logits[:], spread(top[:], shape), ALU.subtract).then_inc(shifted_ready, 1)
                step(nc.vector.tensor_tensor(order[:], logits[:], spread(top[:], shape), ALU.is_equal))
                step(nc.vector.tensor_tensor(cand[:], order[:], by_tile(iota[:]), ALU.mult))
                step(nc.vector.tensor_reduce(first[:], cand[:], axis=AX.X, op=ALU.min))
                nc.vector.tensor_tensor(route[:], by_tile(iota[:]), spread(first[:], shape), ALU.is_equal).then_inc(route_ready, 1)
                dve.wait_ge(expd_ready, 1)
                step(nc.vector.tensor_reduce(total[:], expd[:], axis=AX.X, op=ALU.add))
                nc.vector.reciprocal(p_max[:], total[:])
                dve.wait_ge(counted, 1)
                in_tile = count_ps[:, 0:T * E].rearrange("p (t e) -> p t e", t=T)
                before = count_ps[:, T * E:2 * T * E].rearrange("p (t e) -> p t e", t=T)
                step(nc.vector.tensor_copy(scan[0][:], in_tile))
                far, cur = 1, 0
                while far < T:
                    nc.vector.tensor_copy(scan[1 - cur][:, 0:far, :], scan[cur][:, 0:far, :])
                    step(nc.vector.tensor_tensor(scan[1 - cur][:, far:T, :], scan[cur][:, far:T, :], scan[cur][:, 0:T - far, :], ALU.add))
                    far, cur = far * 2, 1 - cur
                step(nc.vector.tensor_tensor(full_blocks[:], spread(scan[cur][:, T - 1, :], [P, E, KMAX]),
                                             block_starts[:].rearrange("p (o k) -> p o k", o=1).broadcast_to([P, E, KMAX]), ALU.is_gt))
                step(nc.vector.tensor_reduce(blocks[:], full_blocks[:], axis=AX.X, op=ALU.add))
                step(nc.vector.tensor_tensor(full_blocks[:, :, 0:E], expert_before[:], blocks[:].rearrange("p (o e) -> p o e", o=1).broadcast_to([P, E, E]), ALU.mult))
                step(nc.vector.tensor_reduce(first_block[:], full_blocks[:, :, 0:E], axis=AX.X, op=ALU.add))
                step(nc.vector.tensor_tensor(end_block[:], first_block[:], blocks[:], ALU.add))
                step(nc.vector.tensor_tensor(scan[1 - cur][:], scan[cur][:], in_tile, ALU.subtract))
                step(nc.vector.tensor_tensor(scan[1 - cur][:], scan[1 - cur][:], before, ALU.add))
                step(nc.vector.scalar_tensor_tensor(out=scan[cur][:], in0=by_tile(first_block[:]), scalar=float(P), in1=scan[1 - cur][:], op0=ALU.mult, op1=ALU.add))
                step(nc.vector.tensor_tensor(cand[:], scan[cur][:], route[:], ALU.mult))
                step(nc.vector.tensor_reduce(place[:], cand[:], axis=AX.X, op=ALU.add))
                nc.vector.tensor_copy(place_i[:], place[:]).then_inc(places_ready, 1)
                shape = [P, NB + 2, E]
                step(nc.vector.tensor_tensor(ended[:], spread(block_iota[:], shape), end_block[:].rearrange("p (o e) -> p o e", o=1).broadcast_to(shape), ALU.is_ge))
                step(nc.vector.tensor_reduce(block_expert[:], ended[:], axis=AX.X, op=ALU.add))
                step(nc.vector.tensor_scalar(block_expert[:], block_expert[:], float(E - 1), None, ALU.min))
                nc.vector.tensor_copy(block_expert_i[:], block_expert[:]).then_inc(blocks_ready, 1)
                dve.wait_ge(blocks_ready, 1)
                dve.wait_ge(weights_loaded, 64)
                e = expert(1)
                dve.wait_ge(h_ready, 1)
                add_b1(e, 0)
                with dve.Fori(0, NB // STEPS) as it:
                    for k in range(STEPS):
                        j, par = it * STEPS + k, k % 2
                        e_next, e_before = expert(j + 2), expert(j)
                        dve.wait_ge(h_ready, j + 2)
                        dve.wait_ge(gelu_done, j)
                        add_b1(e_next, 1 - par)
                        dve.wait_ge(tr_ready, j + 1)
                        dve.wait_ge(y_ready, j)
                        nc.vector.tensor_copy(hidden_T[par][:].rearrange("p f t -> p (f t)"), tr_ps[:]).then_inc(tr_copied, 1)
                        dve.wait_ge(y_ready, j + 1)
                        dve.wait_ge(y_stored[1 - par], it * (8 * STEPS) + 16 * (k // 2))
                        keep_y(e_before, 1 - par)
                e = expert(NB)
                dve.wait_ge(y_ready, NB + 1)
                dve.wait_ge(y_stored[(NB - 1) % 2], 16 * (NB // 2))
                keep_y(e, (NB - 1) % 2)
                for t in range(T):
                    if t % 4 == 0:
                        dve.wait_ge(fetched[t // 4], 64)
                    nc.vector.scalar_tensor_tensor(out=core.x[:, t, :], in0=y_rows[:, t, :], scalar=p_max[:, t:t + 1], in1=core.x[:, t, :],
                                                   op0=ALU.mult, op1=ALU.add)


def block_attention(nc, core, consts, Wq, bq, Wk, bk, Wv, bv, Wo, bo):
    G = H1 // HG
    ITERS = B * G
    GR = TB // 2
    UNITS = GR * 2 * HG
    FIX = UNITS - HG
    DEPTH = 4
    VT = 2 * TB - 1
    with ExitStack() as st:
        sb = lambda n, s, dt=F32: st.enter_context(nc.sbuf_tensor(f"a1_{n}", s, dt))
        sem = lambda n: core.sem(f"a1_{n}")
        q_all = sb("q_all", [P, G, B * N], F32R)
        k_all = sb("k_all", [P, G, B * N], F32R)
        v_all = sb("v_all", [P, B, VT, D])
        wo_g = sb("wo_g", [P, G, D])
        block_mask = sb("block_mask", [P, P])

        with ExitStack() as st2:
            sb2 = lambda n, s, dt=F32: st2.enter_context(nc.sbuf_tensor(f"a1p_{n}", s, dt))
            ps2 = lambda n, s: st2.enter_context(nc.psum_tensor(f"a1p_{n}_ps", s, F32))
            w = sb2("w", [P, 4, D])
            w_T = sb2("w_T", [P, 4, D])
            w_rep = sb2("w_rep", [P, 2, H1, 4, DH1])
            b_row = sb2("b_row", [1, 2, D])
            b_rep = sb2("b_rep", [1, 2, H1, 4, DH1])
            b_col = sb2("b_col", [P, 2 * G])
            ones = sb2("ones", [1, 4])
            bv_b, bo_b = sb2("bv_b", [P, D]), sb2("bo_b", [P, D])
            part = sb2("part", [P, 4])
            full = [sb2(f"full{i}", [P, 512]) for i in range(DEPTH)]
            high = [sb2(f"high{i}", [P, 512], F32R) for i in range(DEPTH)]
            loaded, zeroed = sem("loaded"), sem("zeroed")

            def load_all(sp):
                for i, m in enumerate((Wq, Wk, Wv, Wo)):
                    sp.dma_start(w[:, i, :], m).then_inc(loaded, 16)
                row = lambda v: v.rearrange("(o d) -> o d", o=1)
                sp.dma_start(b_row[:, 0, :], row(bq)).then_inc(loaded, 16)
                sp.dma_start(b_row[:, 1, :], row(bk)).then_inc(loaded, 16)
                sp.dma_start(bv_b[:], row(bv).broadcast_to([P, D])).then_inc(loaded, 16)
                sp.dma_start(bo_b[:], row(bo).broadcast_to([P, D])).then_inc(loaded, 16)
                sp.dma_start(part[:], consts["part"]).then_inc(loaded, 16)
                sp.dma_start(block_mask[:], consts["block_mask"]).then_inc(loaded, 16)

            normalize(nc, core, "n2", prefetch=load_all)
            w_ps, b_ps = ps2("w", [P, 512]), ps2("b", [P, 512])
            s_ps = [ps2(f"s{i}", [P, 512]) for i in range(DEPTH)]
            v_ps = [ps2(f"v{i}", [P, 512]) for i in range(2)]
            wT_ready, wT_copied, rep_ready, b_ready, b_copied = (sem(n) for n in ("wT_ready", "wT_copied", "rep_ready", "b_ready", "b_copied"))
            proj_ready, full_ready, stack_ready = (sem(n) for n in ("proj_ready", "full_ready", "stack_ready"))
            high_ready = [sem("even_high_ready"), sem("odd_high_ready")]
            v_ready, v_added, wo_placed = (sem(n) for n in ("v_ready", "v_added", "wo_placed"))
            sums_ready = sem("sums_ready")
            STEPS = 2 * G * 4

            with nc.Block() as block:
                @block.sync
                def _(sp):
                    sp.wait_ge(wT_copied, 1)
                    sp.wait_ge(zeroed, 1)
                    for h in range(H1):
                        sp.dma_start(wo_g[32 * (h % HG):32 * (h % HG) + DH1, h // HG, :], w_T[h * DH1:h * DH1 + DH1, 3, :])\
                            .then_inc(wo_placed, 16)
                    sp.wait_ge(wo_placed, 16 * H1)

                @block.gpsimd
                def _(pool):
                    nc.gpsimd.memset(ones[:], 1.0)
                    nc.gpsimd.memset(wo_g[:], 0.0).then_inc(zeroed, 1)
                    pool.wait_ge(v_added, 4)
                    nc.gpsimd.tensor_copy(v_all[:, :, VT - 1, :], v_all[:, :, TB - 1, :]).then_inc(sums_ready, 1)
                    for tile in reversed(range(TB - 2)):
                        pool.wait_ge(sums_ready, TB - 2 - tile)
                        nc.gpsimd.tensor_tensor(v_all[:, :, TB + tile, :], v_all[:, :, TB + tile + 1, :], v_all[:, :, tile + 1, :], ALU.add)\
                            .then_inc(sums_ready, 1)

                @block.tensor
                def _(pe):
                    pe.wait_ge(loaded, 160)
                    for i in range(4):
                        ins = nc.tensor.transpose(w_ps[:, i * D:i * D + D], w[:, i, :], core.ident[:])
                    ins.then_inc(wT_ready, 1)
                    pe.wait_ge(rep_ready, 2)
                    pe.wait_ge(zeroed, 1)
                    for i in range(2 * G):
                        ins = nc.tensor.matmul(b_ps[:, 2 * i:2 * i + 1], b_rep[:, i // G, i % G * HG:(i % G + 1) * HG].rearrange("o h r d -> o (h r d)"),
                                               ones[0:1, 0:1], start=True, stop=True)
                    ins.then_inc(b_ready, 1)
                    for k in range(STEPS):
                        i, g, c = k // (4 * G), k // 4 % G, k % 4
                        if k >= DEPTH:
                            pe.wait_ge(full_ready, k - DEPTH + 1)
                        nc.tensor.matmul(s_ps[k % DEPTH][:], w_rep[:, i, g * HG:(g + 1) * HG].rearrange("p h r d -> p (h r d)"),
                                         core.xT[:, c * 512:c * 512 + 512], start=True, stop=True).then_inc(proj_ready, 1)
                        if k % 2 == 1 and k < 8:
                            q = k // 2
                            if q >= 2:
                                pe.wait_ge(v_added, q - 1)
                            for t in range(4 * q, 4 * q + 4):
                                ins = nc.tensor.matmul(v_ps[q % 2][:, t % 4 * D:t % 4 * D + D], core.xT[:, t * P:t * P + P], w_T[:, 2, :],
                                                       start=True, stop=True)
                            ins.then_inc(v_ready, 1)

                @block.scalar
                def _(act):
                    act.wait_ge(wT_ready, 1)
                    nc.scalar.activation(w_T[:].rearrange("p i d -> p (i d)"), w_ps[:], ACT.Copy).then_inc(wT_copied, 1)
                    act.wait_ge(b_copied, 1)
                    act.wait_ge(loaded, 160)
                    for k in range(STEPS):
                        i, g = k // (4 * G), k // 4 % G
                        act.wait_ge(proj_ready, k + 1)
                        if k >= DEPTH:
                            act.wait_ge(stack_ready, k - DEPTH + 1)
                        nc.scalar.activation(full[k % DEPTH][:], s_ps[k % DEPTH][:], ACT.Identity, bias=b_col[:, k // 4:k // 4 + 1],
                                             scale=float(DH1) ** -0.5 if i == 0 else 1.0).then_inc(full_ready, 1)
                        if k % 2 == 0:
                            act.wait_ge(full_ready, k + 1)
                            nc.scalar.activation(high[k % DEPTH][:], full[k % DEPTH][:], ACT.Copy, scale=part[:, 2 * i:2 * i + 1]).then_inc(high_ready[0], 1)

                @block.vector
                def _(dve):
                    dve.wait_ge(loaded, 160)
                    dve.wait_ge(wT_copied, 1)
                    for i in range(2):
                        heads = w_T[:, i, :].rearrange("p (h o d) -> p h o d", h=H1, o=1).broadcast_to([P, H1, 4, DH1])
                        nc.vector.tensor_copy(w_rep[:, i], heads)
                        bias = b_row[:, i, :].rearrange("p (h o d) -> p h o d", h=H1, o=1).broadcast_to([1, H1, 4, DH1])
                        nc.vector.tensor_copy(b_rep[:, i], bias).then_inc(rep_ready, 1)
                    dve.wait_ge(b_ready, 1)
                    cols = b_ps[:, 0:4 * G].rearrange("p (i o) -> p i o", o=2)[:, :, 0]
                    nc.vector.tensor_scalar(b_col[:, 0:G], cols[:, 0:G], float(DH1) ** -0.5, None, ALU.mult)
                    nc.vector.tensor_copy(b_col[:, G:2 * G], cols[:, G:2 * G]).then_inc(b_copied, 1)
                    nc.vector.tensor_tensor(core.x[:], core.x[:], bo_b[:].rearrange("p (o d) -> p o d", o=1).broadcast_to([P, T, D]), ALU.add)
                    for k in range(STEPS):
                        i, g, c = k // (4 * G), k // 4 % G, k % 4
                        dve.wait_ge(full_ready, k + 1)
                        if k % 2 == 1:
                            nc.vector.tensor_scalar(high[k % DEPTH][:], full[k % DEPTH][:], part[:, 2 * i:2 * i + 1], None, ALU.mult).then_inc(high_ready[1], 1)
                        dve.wait_ge(high_ready[k % 2], k // 2 + 1)
                        nc.vector.scalar_tensor_tensor(out=(q_all, k_all)[i][:, g, c * 512:c * 512 + 512], in0=full[k % DEPTH][:],
                                                       scalar=part[:, 2 * i + 1:2 * i + 2], in1=high[k % DEPTH][:].bitcast(F32),
                                                       op0=ALU.mult, op1=ALU.add).then_inc(stack_ready, 1)
                        if k % 2 == 1 and k < 8:
                            q = k // 2
                            dve.wait_ge(v_ready, q + 1)
                            nc.vector.tensor_tensor(v_all[:, q // 2, q % 2 * 4:q % 2 * 4 + 4, :], v_ps[q % 2][:].rearrange("p (t d) -> p t d", t=4),
                                                    bv_b[:].rearrange("p (o d) -> p o d", o=1).broadcast_to([P, 4, D]), ALU.add).then_inc(v_added, 1)

        q_cur = [sb(f"q_cur{i}", [P, HG, 2 * P], F32R) for i in range(2)]
        k_cur = [sb(f"k_cur{i}", [P, N], F32R) for i in range(2)]
        v_cur = [sb(f"v_cur{i}", [P, VT, HG, 32]) for i in range(2)]
        zeros = sb("zeros", [P, 2], F32R)
        probs = [sb(f"probs{i}", [P, N]) for i in range(4)]
        probs_T = [sb(f"probs_T{i}", [P, TB - 1 + i, HG, 256]) for i in range(2)]
        negmax, den = sb("negmax", [P, UNITS]), sb("den", [P, UNITS])
        later = sb("later", [P, UNITS])
        more_keys = sb("more_keys", [P, TB - 1])
        rden_col = sb("rden_col", [P, 2 * HG])
        rden = sb("rden", [P, 2 * HG, 32])
        ones = sb("rden_ones", [P, 2 * HG, 32])
        rden_b, attn_T = core.xT[:, 0:256], core.xT[:, 256:512]
        ps = lambda n, s: st.enter_context(nc.psum_tensor(f"a1_{n}", s, F32))
        score_ps = [ps(f"score{i}", [P, N]) for i in range(2)]
        tr_ps = [ps(f"tr{i}", [P, 512]) for i in range(2)]
        out_ps, misc_ps = ps("out", [P, 512]), ps("misc", [P, 512])
        q_cleared, cleared, junk_cleared, v_copied = sem("q_cleared"), sem("cleared"), sem("junk_cleared"), sem("v_copied")
        q_loaded = [sem("even_q_loaded"), sem("odd_q_loaded")]
        k_loaded = [sem("even_k_loaded"), sem("odd_k_loaded")]
        scores_ready, masked, negmax_ready, probs_ready, later_kept = (sem(n) for n in ("scores_ready", "masked", "negmax_ready", "probs_ready", "later_kept"))
        tr_ready = [sem("tr_lo_ready"), sem("tr_hi_ready")]
        tr_copied = [sem("tr_lo_copied"), sem("tr_hi_copied")]
        pv_done, attn_ready, rden_ready, rden_col_ready, den_whole = (sem(n) for n in ("pv_done", "attn_ready", "rden_ready", "rden_col_ready", "den_whole"))
        misc_ready, misc_free = sem("misc_ready"), sem("misc_free")
        ITEMS = 2 * GR
        ITEM = {2 * HG * g + q: 2 * g + q - 3 for g in range(GR) for q in (3, 4)}
        LAST_ITEM = {3: 0, 4: 1, 2 * HG + 4: 2}
        UG = 2 * HG
        Q_LOADS = 16 * HG
        HI = UNITS - 3 * HG
        ITERS2 = ITERS // 2

        def unit(s):
            s %= UNITS
            return s // UG, s // HG % 2 + 2 * (s // UG), s % HG

        def tiles(tile):
            return min(tile + 2, TB)

        def hi_copies(s):
            return 1 + max(0, s - (UNITS - HI))

        def act_copies_hi(grp, h):
            return grp >= 2 and h % 2 == 1

        def progress(it, par):
            return lambda m, c: it * (2 * m) + (par * m + c)

        LAST = lambda m, c: m * ITERS + c

        with nc.Block() as block:
            @block.sync
            def _(sp):
                flat_q, flat_k = (src[:].bitcast(F32).rearrange("p g n -> p (g n)") for src in (q_all, k_all))

                def load_q(col, grp):
                    for h in reversed(range(HG)):
                        rows = slice(32 * h, 32 * h + 32)
                        sp.dma_start(q_cur[grp % 2][rows, h, :].bitcast(F32), flat_q[rows, bass.ds(col, N)][:, 2 * P * grp:2 * P * (grp + 1)])\
                            .then_inc(q_loaded[grp % 2], 16)

                def load_k(col, par):
                    sp.dma_start(k_cur[par][:].bitcast(F32), flat_k[:, bass.ds(col, N)]).then_inc(k_loaded[par], 16)

                load_k(0, 0)
                sp.wait_ge(q_cleared, 1)
                load_q(0, 0)
                load_q(0, 1)
                with sp.Fori(0, ITERS2) as it:
                    for par in range(2):
                        n = it * 2 + par
                        col = sp.snap(n % G * (B * N) + n // G * N)
                        next_col = sp.snap((n + 1) % G * (B * N) + (n + 1) // G % B * N)
                        for grp in range(GR):
                            sp.wait_ge(scores_ready, it * (2 * UNITS) + (par * UNITS + UG * (grp + 1)))
                            if grp == 0:
                                load_k(next_col, 1 - par)
                            load_q(col if grp < GR - 2 else next_col, (grp + 2) % GR)
                for i in range(2):
                    sp.wait_ge(q_loaded[i], Q_LOADS * (ITERS * GR // 2 + 1))
                    sp.wait_ge(k_loaded[i], 16 * (ITERS2 + 1 - i))

            @block.gpsimd
            def _(pool):
                nc.gpsimd.memset(q_cur[0][:].bitcast(F32), 0.0)
                nc.gpsimd.memset(q_cur[1][:].bitcast(F32), 0.0).then_inc(q_cleared, 1)
                nc.gpsimd.memset(v_cur[0][:], 0.0)
                nc.gpsimd.memset(v_cur[1][:], 0.0)
                nc.gpsimd.memset(zeros[:].bitcast(F32), 0.0)
                for tile in range(TB - 1):
                    nc.gpsimd.memset(more_keys[:, tile:tile + 1], float(N - P * (tile + 1) - 1))
                nc.gpsimd.memset(probs_T[1][:, 0:3], 0.0)
                nc.gpsimd.memset(ones[:], 1.0).then_inc(cleared, 1)
                pool.wait_ge(cleared, 1)

                def copy_v(g, b, par):
                    flat = v_all[:].rearrange("p b t d -> p (b t) d")
                    src = flat[:, bass.ds(b * VT, VT), bass.ds(g * HG * DH1, HG * DH1)].rearrange("p t (h d) -> p t h d", h=HG)
                    nc.gpsimd.tensor_copy(v_cur[par][:, :, :, 0:DH1], src).then_inc(v_copied, 1)

                def spread_rden(at, grp):
                    pool.wait_ge(rden_col_ready, at(GR, grp + 1))
                    nc.gpsimd.tensor_tensor(rden[:], spread(rden_col[:], [P, UG, 32]), ones[:], ALU.mult).then_inc(rden_ready, 1)

                copy_v(0, 0, 0)
                with pool.Fori(0, ITERS2) as it:
                    for par in range(2):
                        at = progress(it, par)
                        n = it * 2 + par + 1
                        next_g, next_b = pool.snap(n % G), pool.snap(n // G % B)
                        for s in range(FIX):
                            grp, tile, h = unit(s)
                            keys = P * (tile + 1)
                            pool.wait_ge(probs_ready, at(UNITS, s + 1))
                            shared = probs[s % 4][:, keys:keys + 1]
                            nc.gpsimd.tensor_tensor(later[:, s:s + 1], shared, more_keys[:, tile:tile + 1], ALU.mult).then_inc(later_kept, 1)
                            if s % UG == 0:
                                spread_rden(at, grp)
                            if s == UG + 2:
                                copy_v(next_g, next_b, 1 - par)
                spread_rden(LAST, 0)

            @block.tensor
            def _(pe):
                def scores(s, par):
                    grp, tile, h = unit(s)
                    keys = P * (tile + 1)
                    runs = [(lo, min(lo + 512, keys)) for lo in range(0, keys, 512)]
                    if keys < N:
                        runs.append((keys, keys + 2))
                    for lo, hi in runs:
                        src = k_cur[par][:, lo:hi] if lo < keys else zeros[:]
                        last = nc.tensor.matmul(score_ps[s % 2][:, lo:hi], q_cur[grp % 2][:, h, tile % 2 * P:tile % 2 * P + P], src, start=True, stop=True)
                    last.then_inc(scores_ready, 1)

                def values(s, par, at):
                    grp, r = (s - UG - 1) // UG % GR, (s - 1) % UG
                    if r == 0 or r == UG - 1:
                        return
                    even, odd = 2 * grp, 2 * grp + 1
                    n = tiles(odd)
                    if r == 1:
                        pe.wait_ge(tr_copied[0], at(UNITS, s - 1))
                        if n > 4:
                            pe.wait_ge(tr_copied[1], at(HI, hi_copies(s - 2)))
                        pe.wait_ge(attn_ready, at(GR, s // UG + 1))
                        if s == UG + 2:
                            pe.wait_ge(v_copied, at(1, 1))
                    twice = max(0, n - (UG - 2))
                    first = r - 1 + min(r - 1, twice)
                    done = range(first, first + (2 if r - 1 < twice else 1))
                    for k in [k for k in done if k < n]:
                        parts = [(slice(0, 256), k)] if k <= even else [(slice(P, 256), odd if k == odd else TB + odd)]
                        if k == odd:
                            parts.append((slice(0, P), TB + even))
                        for cols, tile in parts:
                            for h in range(HG):
                                ins = nc.tensor.matmul(out_ps[32 * h:32 * h + 32, cols], v_cur[par if s > UG else 1 - par][:, tile, h, :],
                                                       probs_T[grp % 2][:, k, h, cols], start=k == 0, stop=k == n - 1 and tile == parts[-1][1])
                        if k == n - 1:
                            ins.then_inc(pv_done, 1)

                def slot(s, par, at, item, last=False):
                    if not last or s == 0:
                        pe.wait_ge(probs_ready, at(UNITS, s))
                    if not last:
                        if s == UNITS - 1:
                            pe.wait_ge(k_loaded[1 - par], it * 16 + 16 * (par + 1))
                            pe.wait_ge(q_loaded[0], at(Q_LOADS * GR // 2, Q_LOADS * (GR // 2 + 1)))
                            scores(0, 1 - par)
                        else:
                            if (s + 1) % UG == 0:
                                grp = (s + 1) // UG
                                pe.wait_ge(q_loaded[grp % 2], at(Q_LOADS * GR // 2, Q_LOADS * (grp // 2 + 1)))
                            scores(s + 1, par)
                    if not last or s < UG + 1:
                        values(s, par, at)
                    if not last or s == 0:
                        grp, tile, h = unit(s - 1)
                        n = tiles(tile)
                        pe.wait_ge(tr_copied[0], at(UNITS, s))
                        if n > 4:
                            pe.wait_ge(tr_copied[1], at(HI, hi_copies(s - 1) if s else 0))
                        for k in range(n):
                            src = probs[(s - 1) % 4][:, k * P:k * P + P] if k <= tile else \
                                probs[(s - 1) % 4][:, k * P:k * P + 1].broadcast_to([P, P])
                            ins = nc.tensor.transpose(tr_ps[k // 4][:, k % 4 * P:k % 4 * P + P], src, core.ident[:])
                            if k == 3 or (k == n - 1 and n < 4):
                                ins.then_inc(tr_ready[0], 1)
                            elif k == n - 1:
                                ins.then_inc(tr_ready[1], 1)
                    if s in item:
                        pe.wait_ge(misc_free, at(ITEMS, item[s]))
                        for q in range(2):
                            cols = slice(q * P, q * P + P)
                            if s % UG == 3:
                                if q == 0:
                                    pe.wait_ge(rden_ready, at(GR, s // UG + 1))
                                ins = nc.tensor.transpose(misc_ps[:, cols], rden[:, q * HG:(q + 1) * HG, :].rearrange("p h d -> p (h d)"), core.ident[:])
                            else:
                                if q == 0:
                                    pe.wait_ge(attn_ready, at(GR, s // UG + 1))
                                ins = nc.tensor.matmul(misc_ps[:, cols], attn_T[:, cols], wo_g[:].rearrange("p g d -> p (g d)")[:, wo_cols(s)], start=True, stop=True)
                        ins.then_inc(misc_ready, 1)

                pe.wait_ge(cleared, 1)
                pe.wait_ge(junk_cleared, 1)
                for h in range(HG):
                    ins = nc.tensor.matmul(out_ps[32 * h:32 * h + 32, 0:256], v_cur[1][:, 0, h, :], probs_T[1][:, 0, h, :], start=True, stop=True)
                ins.then_inc(pv_done, 1)
                pe.wait_ge(k_loaded[0], 16)
                pe.wait_ge(q_loaded[0], Q_LOADS)
                scores(0, 0)
                with pe.Fori(0, ITERS2) as it:
                    for par in range(2):
                        n = it * 2 + par
                        wo_cols = lambda s, n=n: bass.ds((n % G if s > 2 * UG else (n + G - 1) % G) * D, D)
                        for s in range(UNITS):
                            slot(s, par, progress(it, par), ITEM)
                wo_cols = lambda s: slice((G - 1) * D, G * D)
                for s in range(2 * UG):
                    slot(s, 0, LAST, LAST_ITEM, last=True)

            @block.scalar
            def _(act):
                def slot(s, at, item, last=False):
                    if not last:
                        grp, tile, h = unit(s)
                        keys = P * (tile + 1)
                        n = keys + (keys < N)
                        act.wait_ge(negmax_ready, at(UNITS, s + 1))
                        act.wait_ge(later_kept, at(FIX, min(max(s - 3, 0), FIX)))
                        nc.scalar.activation(probs[s % 4][:, 0:n], score_ps[s % 2][:, 0:n], ACT.Exp, bias=negmax[:, s:s + 1],
                                             accum_out=den[:, s:s + 1]).then_inc(probs_ready, 1)
                    if not last or s == 0:
                        grp, tile, h = unit(s - 1)
                        n = min(4, tiles(tile))
                        act.wait_ge(tr_ready[0], at(UNITS, s + 1))
                        nc.scalar.activation(probs_T[grp % 2][:, 0:n, h, tile % 2 * P:tile % 2 * P + P],
                                             tr_ps[0][:, 0:n * P].rearrange("p (k q) -> p k q", k=n), ACT.Copy).then_inc(tr_copied[0], 1)
                        n = tiles(tile) - 4
                        if act_copies_hi(grp, h):
                            act.wait_ge(tr_ready[1], at(HI, hi_copies(s - 1) + 1 if s else 1))
                            nc.scalar.activation(probs_T[grp % 2][:, 4:4 + n, h, tile % 2 * P:tile % 2 * P + P],
                                                 tr_ps[1][:, 0:n * P].rearrange("p (k q) -> p k q", k=n), ACT.Copy).then_inc(tr_copied[1], 1)
                    if s in item and s % UG == 3:
                        act.wait_ge(misc_ready, at(ITEMS, item[s] + 1))
                        nc.scalar.activation(rden_b[:], misc_ps[:, 0:256], ACT.Copy).then_inc(misc_free, 1)

                act.wait_ge(junk_cleared, 1)
                with act.Fori(0, ITERS2) as it:
                    for par in range(2):
                        for s in range(UNITS):
                            slot(s, progress(it, par), ITEM)
                for s in range(2 * UG):
                    slot(s, LAST, LAST_ITEM, last=True)

            @block.vector
            def _(dve):
                def row_max(s, at):
                    grp, tile, h = unit(s)
                    keys = P * (tile + 1)
                    n = keys + (keys < N)
                    own = score_ps[s % 2][:, tile * P:tile * P + P]
                    nc.vector.tensor_tensor(own, own, block_mask[:], ALU.mult).then_inc(masked, 1)
                    dve.wait_ge(masked, at(UNITS, s + 1))
                    c = s % UNITS
                    nc.vector.tensor_reduce(negmax[:, c:c + 1], score_ps[s % 2][:, 0:n], axis=AX.X, op=ALU.max, negate=True).then_inc(negmax_ready, 1)

                def slot(s, at, batch, item, last=False):
                    if not last:
                        dve.wait_ge(scores_ready, at(UNITS, s + 2))
                        row_max(s + 1, at)
                    if s % UG == 1 and (not last or s == 1):
                        dve.wait_ge(probs_ready, at(UNITS, s if not last else 0))
                        dve.wait_ge(later_kept, at(FIX, min(s - 1, FIX)))
                        c = (s - UG - 1) % UNITS
                        end = min(c + UG, FIX)
                        nc.vector.tensor_tensor(den[:, c:end], den[:, c:end], later[:, c:end], ALU.add).then_inc(den_whole, 1)
                        dve.wait_ge(den_whole, at(GR, s // UG + 1))
                        nc.vector.reciprocal(rden_col[:], den[:, c:c + UG]).then_inc(rden_col_ready, 1)
                    if s % UG == 0:
                        dve.wait_ge(pv_done, at(GR, s // UG + 1))
                        dve.wait_ge(misc_free, at(ITEMS, 2 * (s // UG) - 1 if s > 0 or last else 0))
                        nc.vector.tensor_tensor(attn_T[:], out_ps[:, 0:256], rden_b[:], ALU.mult).then_inc(attn_ready, 1)
                    if not last or s == 0:
                        grp, tile, h = unit(s - 1)
                        n = tiles(tile) - 4
                        if n > 0 and not act_copies_hi(grp, h):
                            dve.wait_ge(tr_ready[1], at(HI, hi_copies(s - 1) + 1 if s else 1))
                            nc.vector.tensor_copy(probs_T[grp % 2][:, 4:4 + n, h, tile % 2 * P:tile % 2 * P + P],
                                                  tr_ps[1][:, 0:n * P].rearrange("p (k q) -> p k q", k=n)).then_inc(tr_copied[1], 1)
                    if s in item and s % UG == 4:
                        dve.wait_ge(misc_ready, at(ITEMS, item[s] + 1))
                        rows = core.x[:, bass.ds(batch[s > 2 * UG] * TB + 2 * ((s // UG + 2) % GR), 2), :]
                        nc.vector.tensor_tensor(rows, misc_ps[:, 0:256].rearrange("p (t d) -> p t d", t=2), rows, ALU.add).then_inc(misc_free, 1)

                nc.vector.memset(probs[3][:], 0.0)
                nc.vector.memset(probs_T[1][:, 3:], 0.0)
                nc.vector.memset(den[:], 1.0)
                nc.vector.memset(later[:], 0.0)
                nc.vector.memset(rden_b[:], 0.0).then_inc(junk_cleared, 1)
                dve.wait_ge(junk_cleared, 1)
                dve.wait_ge(cleared, 1)
                dve.wait_ge(scores_ready, 1)
                row_max(0, lambda m, c: c)
                with dve.Fori(0, ITERS2) as it:
                    for par in range(2):
                        n = it * 2 + par
                        batch = ((n + ITERS - 1) // G % B, n // G % B)
                        for s in range(UNITS):
                            slot(s, progress(it, par), batch, ITEM)
                for s in range(2 * UG):
                    slot(s, LAST, (B - 1, 0), LAST_ITEM, last=True)


def channel_mix(nc, core, W_r, W_k, W_v, mu_r, mu_k, out):
    with ExitStack() as st:
        sb = lambda n, s: st.enter_context(nc.sbuf_tensor(f"f1_{n}", s, F32))
        ps = lambda n: st.enter_context(nc.psum_tensor(f"f1_{n}", [P, 512], F32))
        sem = lambda n: core.sem(f"f1_{n}")
        G = B * N // 512
        w_rows = sb("w_rows", [P, 3, D])
        w = sb("w", [P, 3, D])
        mu = sb("mu", [P, 2])
        rest = sb("rest", [P, 2])
        mixed = [sb("xr", [P, B, N]), sb("xk", [P, B, N])]
        k_relu = [sb(f"k_relu{i}", [P, 512]) for i in range(2)]
        k_sq = [sb(f"k_sq{i}", [P, 512]) for i in range(2)]
        gate = [sb(f"gate{i}", [P, 512]) for i in range(2)]
        prod = [sb(f"prod{i}", [P, 512]) for i in range(2)]
        loaded = sem("loaded")

        def load_all(sp):
            for i, m in enumerate((W_r, W_k, W_v)):
                sp.dma_start(w_rows[:, i, :], m).then_inc(loaded, 16)
            for i, m in enumerate((mu_r, mu_k)):
                sp.dma_start(mu[:, i:i + 1], m.rearrange("(d o) -> d o", o=1)).then_inc(loaded, 16)

        normalize(nc, core, "n3", prefetch=load_all)
        k_ps, r_ps, v_ps = ([ps(f"{n}{i}") for i in range(2)] for n in "krv")
        w_ps = ps("wT")
        wT_ready, wT_copied = sem("wT_ready"), sem("wT_copied")
        rest_ready, k_scaled, r_scaled, mixed_ready = (sem(n) for n in ("rest_ready", "k_scaled", "r_scaled", "mixed_ready"))
        k_ready, r_ready, v_ready = sem("k_ready"), sem("r_ready"), sem("v_ready")
        relu_done, gate_done, sq_done, prod_done, x_done, stored = (sem(n) for n in ("relu_done", "gate_done", "sq_done", "prod_done", "x_done", "stored"))
        with nc.Block() as block:
            @block.sync
            def _(sp):
                rows = out.rearrange("b (t p) d -> p (b t) d", p=P)
                for g in range(G):
                    sp.wait_ge(x_done, g + 1)
                    sp.dma_start(rows[:, 4 * g:4 * g + 4, :], core.x[:, 4 * g:4 * g + 4, :]).then_inc(stored, 16)
                sp.wait_ge(stored, 16 * G)

            @block.tensor
            def _(pe):
                pe.wait_ge(loaded, 80)
                for i in range(3):
                    ins = nc.tensor.transpose(w_ps[:, i * D:i * D + D], w_rows[:, i, :], core.ident[:])
                ins.then_inc(wT_ready, 1)
                pe.wait_ge(wT_copied, 1)
                pe.wait_ge(mixed_ready, 1)
                flat = [m[:].rearrange("p b n -> p (b n)") for m in mixed]
                for g in range(G + 1):
                    if g < G:
                        if g >= 2:
                            pe.wait_ge(relu_done, g - 1)
                            pe.wait_ge(gate_done, g - 1)
                        nc.tensor.matmul(k_ps[g % 2][:], w[:, 1, :], flat[1][:, g * 512:g * 512 + 512], start=True, stop=True).then_inc(k_ready, 1)
                        if g == 0:
                            pe.wait_ge(mixed_ready, 2)
                        for t in range(4):
                            ins = nc.tensor.matmul(r_ps[g % 2][:, t * P:t * P + P], flat[0][:, (4 * g + t) * P:(4 * g + t + 1) * P], w[:, 0, :],
                                                   start=True, stop=True)
                        ins.then_inc(r_ready, 1)
                    if g:
                        pe.wait_ge(sq_done, g)
                        if g >= 3:
                            pe.wait_ge(prod_done, g - 2)
                        for t in range(4):
                            ins = nc.tensor.matmul(v_ps[(g - 1) % 2][:, t * P:t * P + P], k_sq[(g - 1) % 2][:, t * P:t * P + P], w[:, 2, :],
                                                   start=True, stop=True)
                        ins.then_inc(v_ready, 1)

            @block.scalar
            def _(act):
                act.wait_ge(loaded, 80)
                xT = core.xT[:].rearrange("p (b n) -> p b n", b=B)
                nc.scalar.activation(mixed[0][:], xT, ACT.Copy, scale=mu[:, 0:1]).then_inc(r_scaled, 1)
                act.wait_ge(wT_ready, 1)
                nc.scalar.activation(w[:].rearrange("p i d -> p (i d)"), w_ps[:, 0:3 * D], ACT.Copy).then_inc(wT_copied, 1)
                for g in range(G):
                    act.wait_ge(k_ready, g + 1)
                    if g >= 2:
                        act.wait_ge(sq_done, g - 1)
                    nc.scalar.activation(k_relu[g % 2][:], k_ps[g % 2][:], ACT.Relu).then_inc(relu_done, 1)
                    act.wait_ge(r_ready, g + 1)
                    if g >= 2:
                        act.wait_ge(prod_done, g - 1)
                    nc.scalar.activation(gate[g % 2][:], r_ps[g % 2][:], ACT.Sigmoid).then_inc(gate_done, 1)

            @block.vector
            def _(dve):
                dve.wait_ge(loaded, 80)
                nc.vector.tensor_scalar(rest[:], mu[:], -1.0, 1.0, ALU.mult, ALU.add).then_inc(rest_ready, 1)
                dve.wait_ge(rest_ready, 1)
                xT = core.xT[:].rearrange("p (b n) -> p b n", b=B)
                nc.vector.tensor_scalar(mixed[1][:], xT, mu[:, 1:2], None, ALU.mult).then_inc(k_scaled, 1)
                for i in (1, 0):
                    dve.wait_ge((r_scaled, k_scaled)[i], 1)
                    nc.vector.scalar_tensor_tensor(out=mixed[i][:, :, 1:N], in0=xT[:, :, 0:N - 1], scalar=rest[:, i:i + 1],
                                                   in1=mixed[i][:, :, 1:N], op0=ALU.mult, op1=ALU.add).then_inc(mixed_ready, 1)
                for g in range(G + 1):
                    if g < G:
                        dve.wait_ge(relu_done, g + 1)
                        if g >= 2:
                            dve.wait_ge(v_ready, g - 1)
                        nc.vector.tensor_tensor(k_sq[g % 2][:], k_relu[g % 2][:], k_relu[g % 2][:], ALU.mult).then_inc(sq_done, 1)
                    if g:
                        dve.wait_ge(v_ready, g)
                        dve.wait_ge(gate_done, g)
                        p = prod[(g - 1) % 2]
                        nc.vector.tensor_tensor(p[:], v_ps[(g - 1) % 2][:], gate[(g - 1) % 2][:], ALU.mult).then_inc(prod_done, 1)
                        dve.wait_ge(prod_done, g)
                        rows = core.x[:, 4 * (g - 1):4 * g, :]
                        nc.vector.tensor_tensor(rows, rows, p[:].rearrange("p (t d) -> p t d", t=4), ALU.add).then_inc(x_done, 1)


def build(nc, a, c, slots, out):
    with ExitStack() as stack:
        core = Core(nc, stack)
        rotary_attention(nc, core, a["L0_attn_x"], (a["L0_attn_ln_gamma"], a["L0_attn_ln_beta"]), c["rope"], a["L0_attn_w_qkv"], a["L0_attn_w_out"], slots[0])
        experts(nc, core, *(a[f"L0_ffn_{n}"] for n in ("switch_w", "switch_b", "w1", "b1", "w2", "b2")), *slots)
        block_attention(nc, core, c, *(a[f"L1_attn_{n}"] for n in ("Wq", "bq", "Wk", "bk", "Wv", "bv", "Wo", "bo")))
        channel_mix(nc, core, *(a[f"L1_ffn_{n}"] for n in ("W_r", "W_k", "W_v", "mu_r", "mu_k")), out)


def rope_tables():
    inv = (1.0 / np.float32(10000.0) ** (np.arange(0, DH0, 2, dtype=np.float32) / np.float32(DH0))).astype(np.float32)
    pos = np.maximum(np.arange(N) - 1, 0).astype(np.float32)
    ang = (pos[None, :] * inv[:, None]).astype(np.float32)
    cos, sin = np.tile(np.cos(ang), (4, 1)), np.tile(np.concatenate([-np.sin(ang), np.sin(ang)]), (2, 1))
    s = np.float32(DH0 ** -0.5)
    return np.stack([cos * s, sin * s, cos, sin]).astype(np.float32)


def part_signs():
    low = np.tile(np.repeat(np.array([[0, 0, 1, 1], [0, 1, 0, 1]]), DH1, axis=1), (1, HG))
    return np.stack([1 - 2 * low[0], low[0], 1 - 2 * low[1], low[1]], axis=1).astype(np.float32)


def block_mask():
    blk = np.arange(P) // WIN
    return (blk[:, None] >= blk[None, :]).astype(np.float32)


_INS = ['L0_attn_x', 'L0_attn_ln_gamma', 'L0_attn_ln_beta', 'L0_attn_w_qkv', 'L0_attn_w_out', 'L0_ffn_switch_w', 'L0_ffn_switch_b',
        'L0_ffn_w1', 'L0_ffn_b1', 'L0_ffn_w2', 'L0_ffn_b2', 'L1_attn_Wq', 'L1_attn_bq', 'L1_attn_Wk', 'L1_attn_bk', 'L1_attn_Wv',
        'L1_attn_bv', 'L1_attn_Wo', 'L1_attn_bo', 'L1_ffn_W_r', 'L1_ffn_W_k', 'L1_ffn_W_v', 'L1_ffn_mu_r', 'L1_ffn_mu_k']


def kernel(**inputs):
    import concourse.bacc as _bacc
    from concourse.bass_utils import run_bass_kernel_spmd as _run

    nc = _bacc.Bacc("TRN2", target_bir_lowering=False, num_devices=1)
    arrays, a, c = {}, {}, {}
    for name in _INS:
        arrays[f"in_{name}"] = np.ascontiguousarray(inputs[name])
        a[name] = nc.dram_tensor(f"in_{name}", arrays[f"in_{name}"].shape, F32, kind="ExternalInput").ap()
    for name, value in (("rope", rope_tables()), ("part", part_signs()), ("block_mask", block_mask())):
        arrays[f"const_{name}"] = value
        c[name] = nc.dram_tensor(f"const_{name}", value.shape, F32, kind="ExternalInput").ap()
    out = nc.dram_tensor("out", (B, N, D), F32, kind="ExternalOutput").ap()
    slots = [nc.dram_tensor(f"slots_{n}", (blocks * P, D), F32, kind="Internal").ap() for n, blocks in (("x", SLOT_BLOCKS), ("y", SLOT_BLOCKS + 1))]
    build(nc, a, c, slots, out)
    return _run(nc, [arrays], core_ids=[0]).results[0]["out"]
```
